# Optimizing a Trainium2 kernel written in Bass

```python
import numpy as np
import jax
import jax.numpy as jnp

def _softmax(x, axis=-1):
    return jax.nn.softmax(x, axis=axis)

def _gelu(x):
    return jax.nn.gelu(x, approximate=True)

def _silu(x):
    return jax.nn.silu(x)

def _sigmoid(x):
    return jax.nn.sigmoid(x)

def _layernorm(x, axis=-1, eps=1e-05):
    m = jnp.mean(x, axis=axis, keepdims=True)
    v = jnp.var(x, axis=axis, keepdims=True)
    return (x - m) / jnp.sqrt(v + eps)

def _scatter_add(tgt, idx, src, axis=0):
    return tgt.at[idx].add(src)

def _segment_sum(src, seg, n):
    return jax.ops.segment_sum(src, seg, n)
kernel_name = 'mk_seq_preln_d1_jaxref_r8_2fee46'

def setup_inputs(seed: int=0):
    np.random.seed(seed)
    _w = jnp.asarray

    def _L0_attn_setup():
        import jax, jax.numpy as jnp
        import numpy as np
        ROPE_THETA = 10000.0
        N_HEAD = 16

        def _rope(x, theta):
            T, D = (x.shape[-2], x.shape[-1])
            pos = jnp.arange(T, dtype=jnp.float32)
            inv_freq = 1.0 / theta ** (jnp.arange(0, D, 2, dtype=jnp.float32) / D)
            freqs = pos[:, None] * inv_freq[None, :]
            cos = jnp.cos(freqs).astype(x.dtype)[None, None]
            sin = jnp.sin(freqs).astype(x.dtype)[None, None]
            x_even = x[..., ::2]
            x_odd = x[..., 1::2]
            rot = jnp.stack((x_even * cos - x_odd * sin, x_even * sin + x_odd * cos), axis=-1)
            return rot.reshape(x.shape)
        key = jax.random.key(seed)
        ks = jax.random.split(key, 5)
        B, T, E = (4, 256, 128)
        s = 0.02
        return {'x': jax.random.normal(ks[0], (B, T, E), jnp.float32), 'Wqkv': jax.random.normal(ks[1], (E, 3 * E), jnp.float32) * s, 'bqkv': jax.random.normal(ks[2], (3 * E,), jnp.float32) * s, 'Wproj': jax.random.normal(ks[3], (E, E), jnp.float32) * s, 'bproj': jax.random.normal(ks[4], (E,), jnp.float32) * s}
    _L0_attn_in = _L0_attn_setup()

    def _L0_ffn_setup():
        import jax, jax.numpy as jnp
        import numpy as np
        B, S, D = (4, 256, 128)
        EXP = 4
        H = EXP * D
        E = 8
        TOP_K = 2
        key = jax.random.key(seed)
        ks = jax.random.split(key, 8)
        scale1 = 1.0 / np.sqrt(D)
        scale2 = 1.0 / np.sqrt(H)
        x = jax.random.normal(ks[0], (B, S, D), dtype=jnp.float32)
        W1 = jax.random.uniform(ks[1], (E, D, H), jnp.float32, -scale1, scale1)
        b1 = jax.random.uniform(ks[2], (E, H), jnp.float32, -scale1, scale1)
        W2 = jax.random.uniform(ks[3], (E, H, D), jnp.float32, -scale2, scale2)
        b2 = jax.random.uniform(ks[4], (E, D), jnp.float32, -scale2, scale2)
        Wr = jax.random.uniform(ks[5], (D, E), jnp.float32, -scale1, scale1)
        br = jax.random.uniform(ks[6], (E,), jnp.float32, -scale1, scale1)
        return {'input_emb': x, 'W1': W1, 'b1': b1, 'W2': W2, 'b2': b2, 'Wr': Wr, 'br': br}
    _L0_ffn_in = _L0_ffn_setup()
    _d = {'L0_attn_x': _L0_attn_in['x'], 'L0_attn_Wqkv': _L0_attn_in['Wqkv'], 'L0_attn_bqkv': _L0_attn_in['bqkv'], 'L0_attn_Wproj': _L0_attn_in['Wproj'], 'L0_attn_bproj': _L0_attn_in['bproj'], 'L0_ffn_W1': _L0_ffn_in['W1'], 'L0_ffn_b1': _L0_ffn_in['b1'], 'L0_ffn_W2': _L0_ffn_in['W2'], 'L0_ffn_b2': _L0_ffn_in['b2'], 'L0_ffn_Wr': _L0_ffn_in['Wr'], 'L0_ffn_br': _L0_ffn_in['br']}
    _x0 = _d['L0_attn_x']
    _d['L0_attn_x'] = jax.random.normal(jax.random.fold_in(jax.random.key(seed), 1), (16, 256, 128), dtype=_x0.dtype)
    del _x0
    return _d

def reference(L0_attn_x, L0_attn_Wqkv, L0_attn_bqkv, L0_attn_Wproj, L0_attn_bproj, L0_ffn_W1, L0_ffn_b1, L0_ffn_W2, L0_ffn_b2, L0_ffn_Wr, L0_ffn_br):

    def _L0_attn_ref(x, Wqkv, bqkv, Wproj, bproj):
        import jax, jax.numpy as jnp
        import numpy as np
        ROPE_THETA = 10000.0
        N_HEAD = 16

        def _rope(x, theta):
            T, D = (x.shape[-2], x.shape[-1])
            pos = jnp.arange(T, dtype=jnp.float32)
            inv_freq = 1.0 / theta ** (jnp.arange(0, D, 2, dtype=jnp.float32) / D)
            freqs = pos[:, None] * inv_freq[None, :]
            cos = jnp.cos(freqs).astype(x.dtype)[None, None]
            sin = jnp.sin(freqs).astype(x.dtype)[None, None]
            x_even = x[..., ::2]
            x_odd = x[..., 1::2]
            rot = jnp.stack((x_even * cos - x_odd * sin, x_even * sin + x_odd * cos), axis=-1)
            return rot.reshape(x.shape)
        B, T, E = x.shape
        H = N_HEAD
        D = E // H
        qkv = x @ Wqkv + bqkv
        q, k, v = jnp.split(qkv, 3, axis=-1)
        q = q.reshape(B, T, H, D).transpose(0, 2, 1, 3)
        k = k.reshape(B, T, H, D).transpose(0, 2, 1, 3)
        v = v.reshape(B, T, H, D).transpose(0, 2, 1, 3)
        q = _rope(q, ROPE_THETA)
        k = _rope(k, ROPE_THETA)
        scores = jnp.einsum('bhqd,bhkd->bhqk', q, k) * D ** (-0.5)
        causal = jnp.tril(jnp.ones((T, T), dtype=bool))
        scores = jnp.where(causal[None, None], scores, -jnp.inf)
        weights = jax.nn.softmax(scores, axis=-1)
        out = jnp.einsum('bhqk,bhkd->bhqd', weights, v)
        out = out.transpose(0, 2, 1, 3).reshape(B, T, E)
        return out @ Wproj + bproj

    def _L0_ffn_ref(input_emb, W1, b1, W2, b2, Wr, br):
        import jax, jax.numpy as jnp
        import numpy as np
        B, S, D = (4, 256, 128)
        EXP = 4
        H = EXP * D
        E = 8
        TOP_K = 2
        logits = jnp.einsum('bsd,de->bse', input_emb, Wr) + br
        route_w = jax.nn.softmax(logits, axis=-1)
        _, topk_idx = jax.lax.top_k(route_w, TOP_K)
        mask = jax.nn.one_hot(topk_idx, E, dtype=route_w.dtype).sum(-2)
        routed = route_w * mask
        routed = routed / routed.sum(axis=-1, keepdims=True)
        h = jax.nn.relu(jnp.einsum('bsd,edh->ebsh', input_emb, W1) + b1[:, None, None, :])
        expert_out = jnp.einsum('ebsh,ehd->ebsd', h, W2) + b2[:, None, None, :]
        return jnp.einsum('bse,ebsd->bsd', routed, expert_out)
    x = L0_attn_x
    x = x + _L0_attn_ref(_layernorm(x, axis=-1), L0_attn_Wqkv, L0_attn_bqkv, L0_attn_Wproj, L0_attn_bproj)
    x = x + _L0_ffn_ref(_layernorm(x, axis=-1), L0_ffn_W1, L0_ffn_b1, L0_ffn_W2, L0_ffn_b2, L0_ffn_Wr, L0_ffn_br)
    return x

_drawn_inputs = setup_inputs


def setup_inputs(seed=0):
    import zlib

    import numpy as np

    out = dict(_drawn_inputs(seed))
    spreads = {}
    factors = {'L0_attn_Wqkv': 4.333,
     'L0_attn_bqkv': 5.534,
     'L0_attn_Wproj': 4.296,
     'L0_ffn_b1': 3.788,
     'L0_ffn_b2': 3.181}
    for name, (base, spread) in spreads.items():
        noise = np.random.default_rng([zlib.crc32(name.encode()), seed]).standard_normal(out[name].shape)
        drawn = base * np.exp(spread * noise) if base else spread * noise
        out[name] = jnp.asarray(drawn.astype(out[name].dtype))
    for name, factor in factors.items():
        out[name] = (out[name] * factor).astype(out[name].dtype)
    return out
```

```python
import numpy as np
import concourse.bass as bass
from concourse import mybir
from contextlib import ExitStack

fp32 = mybir.dt.float32
bf16 = mybir.dt.bfloat16
i32 = mybir.dt.int32
ALU = mybir.AluOpType
ACT = mybir.ActivationFunctionType
X = mybir.AxisListType.X

NB, T, E = 16, 256, 128
H, D = 16, 8
NE, HID, TOPK = 8, 512, 2
P = 128
TT = T // P
NT = NB * TT
NTOK = NB * T
EPS = 1e-5
SCALE = D ** -0.5
HIDDEN_MASK = -3.0e38

PARTS = 3
TERMS = PARTS * PARTS
QK_ROWS = TERMS * D
HH = H // 2
GROUP = 4
NG = H // GROUP
UNITS = 3 * NG
VC = 32

STRIDE = NTOK + P
TILES = NTOK * TOPK // P + NE
SPARE = NE
ROW = E + 1
KT = HID // P
BIAS_COLS = 43
B1_AT, B2_AT = 0, NE * HID
BP_AT = B2_AT + NE * E
BV_AT = BP_AT + E
BR_AT = BV_AT + E
NBIAS = P * BIAS_COLS


class Batch:

    def __init__(self, pair, par):
        self.pair, self.par, self.n = pair, par, 2 * pair + par
        self.known = isinstance(pair, int)

    def off(self, d):
        return Batch(self.pair + (self.par + d) // 2, (self.par + d) % 2)

    def real(self):
        return 0 <= self.n < NB if self.known else True

    def after(self, n):
        return self.n >= n if self.known else True


FIRST_STEP, LOOP_FROM, LOOP_PAIRS, LAST_STEP = -3, 3, 5, NB + 2


def run_steps(eng, step):
    for t in range(FIRST_STEP, LOOP_FROM):
        step(Batch(t // 2, t % 2))
    with eng.Fori(LOOP_FROM // 2, LOOP_FROM // 2 + LOOP_PAIRS) as pair:
        step(Batch(pair, 1))
        step(Batch(pair + 1, 0))
    for t in range(LOOP_FROM + 2 * LOOP_PAIRS, LAST_STEP):
        step(Batch(t // 2, t % 2))


def layer(nc, x, wqkv, qk_bias, wproj, w1, w2, wr, biases, rope, out):
    ctx = ExitStack()
    with ctx:
        def sb(name, shape, dt=fp32):
            return ctx.enter_context(nc.sbuf_tensor(name, shape, dt))

        def sem(name):
            return ctx.enter_context(nc.semaphore(name))

        parts_dram = nc.dram_tensor("parts_dram", [2, 2, PARTS, P, T], bf16)
        bias_dram = nc.dram_tensor("bias_dram", [PARTS, NBIAS], bf16)
        lists = nc.dram_tensor("lists", [NE * STRIDE + SPARE * P, ROW], fp32)
        results = nc.dram_tensor("results", [TOPK * NTOK + (NE + SPARE) * P, E], fp32)

        x_sb = sb("x_sb", [P, NT, E])
        wqkv_sb = sb("wqkv_sb", [P, 3, E])
        wswap = sb("wswap", [P, 2, E])
        wproj_sb = sb("wproj_sb", [P, E])
        wr_sb = sb("wr_sb", [P, NE])
        w1_sb = sb("w1_sb", [P, NE, HID])
        w2_sb = sb("w2_sb", [P, NE, KT, E])
        qkb = sb("qkb", [P, 4])
        rope_sb = sb("rope_sb", [P, 2, T])
        bias_in = sb("bias_in", [P, BIAS_COLS])
        bias_rest = sb("bias_rest", [P, 2, BIAS_COLS])
        bias_split = sb("bias_split", [P, PARTS, BIAS_COLS], bf16)
        bias_rows = sb("bias_rows", [PARTS, NBIAS], bf16)
        ident = sb("ident", [P, P])
        identb = sb("identb", [P, P], bf16)
        maskb = sb("maskb", [P, P], bf16)
        beforeb = sb("beforeb", [P, P], bf16)
        onesb = sb("onesb", [P, P], bf16)
        half_neg = sb("half_neg", [P, TT])
        rank_down = sb("rank_down", [P, TT, NE])
        stats1 = sb("stats1", [P, TT, 6])
        mv1 = sb("mv1", [P, TT, 2])
        ve1 = sb("ve1", [P, TT])
        rstd1 = sb("rstd1", [P, TT])
        xn1 = sb("xn1", [P, TT, E])
        xn1T = [sb(f"xn1T{i}", [P, T]) for i in range(2)]
        rope_a = sb("rope_a", [P, 2, T])
        rope_b = sb("rope_b", [P, 2, T])
        qk = sb("qk", [P, 2, T])
        qk_rest = sb("qk_rest", [P, 2, T])
        split = [sb(f"split{i}", [P, 2, PARTS, T], bf16) for i in range(2)]
        qa = [sb(f"qa{i}", [P, H, T], bf16) for i in range(2)]
        ka = [sb(f"ka{i}", [P, H, T], bf16) for i in range(2)]
        va = [sb(f"va{i}", [P, TT, H, VC]) for i in range(2)]
        mx = [sb(f"mx{i}", [P, H, TT]) for i in range(2)]
        mx_rest = sb("mx_rest", [P, HH, TT])
        mx_split = sb("mx_split", [P, PARTS, HH, TT], bf16)
        mxT = [sb(f"mxT{i}", [PARTS * HH * TT, P], bf16) for i in range(2)]
        NP = 6
        pr = sb("pr", [P, NP, 512])
        ot = sb("ot", [P, NG, T])
        rec = sb("rec", [P, TT, H])
        on = sb("on", [P, TT, E])
        onT = sb("onT", [P, T])
        stats2 = sb("stats2", [P, TT, 6])
        mv2 = sb("mv2", [P, TT, 2])
        ve2 = sb("ve2", [P, TT])
        rstd2 = sb("rstd2", [P, TT])
        xn2T = sb("xn2T", [P, T])
        rows = [sb(f"rows{i}", [P, TOPK, TT, ROW]) for i in range(2)]
        lg = [sb(f"lg{i}", [P, TT, NE]) for i in range(2)]
        top = sb("top", [P, TOPK, NT])
        r_dif = sb("r_dif", [P, TT, NE])
        r_key = sb("r_key", [P, TT, NE])
        r_kmax = sb("r_kmax", [P, TT])
        r_rest = sb("r_rest", [P, TT, NE])
        chosen = sb("chosen", [P, TOPK, TT, NE])
        both = sb("both", [P, TT, NE], bf16)
        used = sb("used", [P, NE])
        slot_of = sb("slot_of", [P, TT, NE])
        slot_sel = sb("slot_sel", [P, TOPK, TT, NE])
        slot_f = sb("slot_f", [P, TOPK, TT])
        slot_i = [sb(f"slot_i{i}", [P, TOPK, TT], i32) for i in range(2)]
        gate = sb("gate", [P, TOPK, NT])
        gate_t = sb("gate_t", [P, 3, NT])
        pad = sb("pad", [P, NE + SPARE, ROW])
        list0 = sb("list0", [P, NE])
        count = sb("count", [1, NE])
        count_i = sb("count_i", [1, 2, NE], i32)
        tiles_f = sb("tiles_f", [1, NE])
        tiles_end = sb("tiles_end", [1, NE])
        zero_e = sb("zero_e", [1, NE])
        jump = sb("jump", [1, NE])
        tile_no = sb("tile_no", [1, TILES])
        ended = sb("ended", [1, TILES, NE])
        ended_j = sb("ended_j", [1, TILES, NE])
        tab_f = sb("tab_f", [1, 3, TILES])
        tab = sb("tab", [1, 2, TILES], i32)
        pad_at = sb("pad_at", [1, NE], i32)
        NX = 4
        xt = [sb(f"xt{i}", [P, ROW]) for i in range(NX)]
        xtT = [sb(f"xtT{i}", [P, P]) for i in range(2)]
        hid = [sb(f"hid{i}", [P, HID]) for i in range(2)]
        hidT = [sb(f"hidT{i}", [P, HID]) for i in range(2)]
        yt = [sb(f"yt{i}", [P, E]) for i in range(NX)]
        NF = 4
        fin = [sb(f"fin{i}", [P, TOPK, NF, E]) for i in range(4)]

        bank = [ctx.enter_context(nc.psum_tensor(f"bank{i}", [P, 512], fp32)) for i in range(8)]
        SQ, ST, OT, PJ, OC, MISC = bank[0:2], bank[2:4], bank[4], bank[5], bank[6], bank[7]
        mxT_ps = MISC[0:PARTS * HH * TT, 256:320].bitcast(bf16)
        XT_PS, HID_PS, HIDT_PS, Y_PS = bank[0:2], bank[2:4], bank[4:6], bank[6:8]

        s_x = [sem(f"x_chunk{i}") for i in range(3)]
        s_w = sem("weights_loaded")
        s_we = sem("expert_weights_loaded")
        s_bin = sem("bias_in_loaded")
        s_bout = sem("bias_parts_stored")
        s_brow = sem("bias_rows_loaded")
        s_const = sem("constants_made")
        s_bsplit = sem("bias_split_step")
        s_swap = sem("wswap_made")
        s_st1, s_mv1, s_ve1, s_rstd1, s_xn1 = (sem(n) for n in ("stats1_done", "mv1_done", "ve1_done", "rstd1_done", "xn1_done"))
        s_xT_ps, s_xT = sem("xn1T_in_psum"), sem("xn1T_done")
        s_q_ps, s_k_ps, s_v_ps = sem("q_in_psum"), sem("k_in_psum"), sem("v_in_psum")
        s_qrot, s_krot, s_va = sem("q_rotated"), sem("k_rotated"), sem("v_done")
        s_qk, s_hi, s_rest, s_mid, s_lo = (sem(n) for n in ("qk_done", "hi_done", "rest_done", "mid_done", "lo_done"))
        s_pst = [sem(f"parts_stored{i}") for i in range(2)]
        s_ld = [[sem(f"qk_loaded{h}{i}") for i in range(2)] for h in range(2)]
        s_sq, s_mx = sem("sq_in_psum"), sem("max_done")
        s_ms = sem("max_split_step")
        s_mT_ps, s_mT = sem("mxT_in_psum"), sem("mxT_done")
        s_ml = [sem(f"max_rows_loaded{h}") for h in range(2)]
        s_stp, s_exp, s_msk = sem("st_in_psum"), sem("exp_done"), sem("mask_done")
        s_pv, s_ot = sem("pv_done"), sem("ot_done")
        s_oc, s_rec, s_on = sem("o_turned"), sem("reciprocals_done"), sem("on_done")
        s_onT_ps, s_onT, s_y_ps, s_x1 = sem("onT_in_psum"), sem("onT_done"), sem("proj_in_psum"), sem("x1_done")
        s_st2, s_mv2, s_ve2, s_rstd2 = (sem(n) for n in ("stats2_done", "mv2_done", "ve2_done", "rstd2_done"))
        s_row0, s_row1, s_rowno = sem("rows_first_done"), sem("rows_second_done"), sem("row_numbers_done")
        s_x2T_ps, s_x2T, s_lg_ps, s_lg = sem("xn2T_in_psum"), sem("xn2T_done"), sem("logits_in_psum"), sem("logits_done")
        s_rt = sem("route_step")
        s_both, s_rk_ps, s_slot = sem("both_done"), sem("ranks_in_psum"), sem("slots_done")
        s_sc = [sem(f"rows_scattered{i}") for i in range(2)]
        s_used, s_tab, s_tabs = sem("used_step"), sem("table_step"), sem("tables_done")
        s_pad, s_spare = sem("padding_stored"), sem("spare_stored")
        s_g, s_gexp, s_gate = sem("gate_step"), sem("gate_exp_done"), sem("gates_done")
        s_xt = [sem(f"tile_loaded{i}") for i in range(NX)]
        s_tx, s_xtT, s_hp, s_hid = sem("tile_turned"), sem("tileT_done"), sem("hidden_in_psum"), sem("hidden_done")
        s_thp, s_hidT, s_yp, s_yt = sem("hiddenT_in_psum"), sem("hiddenT_done"), sem("y_in_psum"), sem("y_done")
        s_ys = [sem(f"y_scattered{i}") for i in range(NX)]
        s_fl = [sem(f"results_loaded{i}") for i in range(4)]
        s_fs, s_fin, s_out = sem("first_added"), sem("final_done"), sem("out_stored")

        block = ctx.enter_context(nc.Block())

        N_CONST = 14
        N_W = 16 * 5
        x_tiles = x.rearrange("(n p) e -> p n e", p=P)
        out_tiles = out.rearrange("(n p) e -> p n e", p=P)
        LD_DMAS = 2 * PARTS
        NC_FIN = NT // NF

        def j_in(j, ahead, last):
            return j + ahead < last if isinstance(j, int) else True

        def apart(eng, *values):
            held = [v if isinstance(v, int) else eng.compute_val(v) for v in values]
            eng.wait_ge(s_const, N_CONST)
            return held

        @block.sync
        def _(sp):
            sp.dma_start(x_sb[:, 0:TT, :], x_tiles[:, 0:TT, :]).then_inc(s_x[0], 16)
            sp.dma_start(wqkv_sb[:], wqkv.rearrange("p (a e) -> p a e", a=3)).then_inc(s_w, 16)
            sp.dma_start(qkb[:], qk_bias).then_inc(s_w, 16)
            sp.dma_start(rope_sb[:], rope).then_inc(s_w, 16)
            sp.dma_start(x_sb[:, TT:4 * TT, :], x_tiles[:, TT:4 * TT, :]).then_inc(s_x[1], 16)
            sp.dma_start(wproj_sb[:], wproj).then_inc(s_w, 16)
            sp.dma_start(wr_sb[:], wr).then_inc(s_w, 16)
            sp.dma_start(x_sb[:, 4 * TT:NT, :], x_tiles[:, 4 * TT:NT, :]).then_inc(s_x[2], 16)
            sp.wait_ge(s_bsplit, 5)
            sp.dma_start(bias_dram.ap().rearrange("a (p c) -> p a c", p=P), bias_split[:]).then_inc(s_bout, 16)
            sp.wait_ge(s_bout, 16)
            sp.dma_start(bias_rows[:], bias_dram.ap()).then_inc(s_brow, 16)
            sp.dma_start(w1_sb[:], w1.rearrange("e p n -> p e n")).then_inc(s_we, 16)
            sp.dma_start(w2_sb[:], w2.rearrange("e (k p) n -> p e k n", p=P)).then_inc(s_we, 16)

            def load_half(b, half):
                par = b.par
                at = half * HH * T
                for a in range(PARTS):
                    rows_ = slice(a * PARTS * D, (a + 1) * PARTS * D)
                    src = bass.AP(parts_dram, ((par * 2 + 0) * PARTS + a) * P * T + at,
                                  [[0, PARTS], [H * T, D], [1, HH * T]])
                    sp.dma_start(qa[par][rows_, half * HH:(half + 1) * HH, :], src).then_inc(s_ld[half][par], 16)
                    src = bass.AP(parts_dram, (par * 2 + 1) * PARTS * P * T + at,
                                  [[H * T, PARTS * D], [1, HH * T]])
                    sp.dma_start(ka[par][rows_, half * HH:(half + 1) * HH, :], src).then_inc(s_ld[half][par], 16)

            def max_rows(b, half):
                sp.wait_ge(s_mT, 2 * b.n + half + 1)
                for a in range(PARTS):
                    dst = qa[b.par][QK_ROWS + a:QK_ROWS + a + 1, half * HH:(half + 1) * HH, :]
                    sp.dma_start(dst.rearrange("p h (t q) -> p (h t) q", t=TT),
                                 mxT[half][a * HH * TT:(a + 1) * HH * TT, :]).then_inc(s_ml[half], 16)

            def step(t):
                b2, b1 = t.off(2), t.off(1)
                if t.real():
                    max_rows(t, 1)
                if b1.real():
                    max_rows(b1, 0)
                if b2.real():
                    done, read = apart(sp, b2.n + 1, 16 * LD_DMAS * b2.pair)
                    sp.wait_ge(s_lo, done)
                    sp.wait_ge(s_mid, done)
                    if b2.after(2):
                        sp.wait_ge(s_ld[0][b2.par], read)
                        sp.wait_ge(s_ld[1][b2.par], read)
                    sp.dma_start(parts_dram.ap()[b2.par].rearrange("q s p t -> p (q s) t"),
                                 split[b2.par][:].rearrange("p q s t -> p (q s) t")).then_inc(s_pst[b2.par], 16)
                    sp.wait_ge(s_pst[b2.par], 16 * (b2.pair + 1))
                    for half in range(2):
                        if b2.after(2):
                            sp.wait_ge(s_stp, UNITS * t.n + UNITS // 2 * (half + 1))
                        load_half(b2, half)

            run_steps(sp, step)

            sp.wait_ge(s_tabs, 1)
            for e in range(NE):
                at = sp.value_load(pad_at[0:1, e:e + 1], min_val=0, max_val=NE * STRIDE)
                sp.dma_start(lists.ap()[bass.ds(at, P), :], pad[:, e, :]).then_inc(s_pad, 16)
            for i in range(2):
                sp.wait_ge(s_sc[i], 16 * TOPK * TT * (NB // 2))
            sp.wait_ge(s_pad, 16 * NE)
            sp.wait_ge(s_spare, 16)

            for j in range(NX):
                at = sp.value_load(tab[0:1, 1, j:j + 1], min_val=0, max_val=NE * STRIDE + SPARE * P - P)
                sp.dma_start(xt[j][:], lists.ap()[bass.ds(at, P), :]).then_inc(s_xt[j], 16)
            with sp.Fori(1, TILES // NX) as g:
                for i in range(NX):
                    sent, = apart(sp, 16 * g)
                    sp.wait_ge(s_ys[i], sent)
                    at = sp.value_load(tab[0:1, 1, bass.ds(NX * g + i, 1)], min_val=0,
                                       max_val=NE * STRIDE + SPARE * P - P)
                    sp.dma_start(xt[i][:], lists.ap()[bass.ds(at, P), :]).then_inc(s_xt[i], 16)

            for i in range(NX):
                sp.wait_ge(s_ys[i], 16 * (TILES // NX))
            res = results.ap()[0:TOPK * NTOK, :].rearrange("(c n p) e -> p c n e", c=TOPK, p=P)

            def load_results(c):
                for k in range(TOPK):
                    sp.dma_start(fin[c % 4][:, k], res[:, k, c * NF:(c + 1) * NF, :]).then_inc(s_fl[c % 4], 16)

            for c in range(4):
                load_results(c)
            for c in range(NC_FIN):
                sp.wait_ge(s_fin, (c + 1) * NF)
                sp.dma_start(out_tiles[:, c * NF:(c + 1) * NF, :], x_sb[:, c * NF:(c + 1) * NF, :]).then_inc(s_out, 16)
                if c + 4 < NC_FIN:
                    load_results(c + 4)
            sp.wait_ge(s_out, 16 * NC_FIN)

        @block.gpsimd
        def _(pool):
            nc.gpsimd.memset(ident[:], 0.0).then_inc(s_const, 1)
            nc.gpsimd.memset(maskb[:], 0.0).then_inc(s_const, 1)
            nc.gpsimd.memset(beforeb[:], 1.0).then_inc(s_const, 1)
            nc.gpsimd.memset(half_neg[:], -0.5).then_inc(s_const, 1)
            pool.wait_ge(s_const, 4)
            nc.gpsimd.affine_select(out=ident[:], in_=ident[:], compare_op=ALU.not_equal, fill=1.0, base=0,
                                    pattern=[[-1, P]], channel_multiplier=1).then_inc(s_const, 1)
            nc.gpsimd.affine_select(out=maskb[:], in_=maskb[:], compare_op=ALU.is_ge, fill=HIDDEN_MASK, base=0,
                                    pattern=[[-1, P]], channel_multiplier=1).then_inc(s_const, 1)
            nc.gpsimd.affine_select(out=beforeb[:], in_=beforeb[:], compare_op=ALU.is_gt, fill=0.0, base=0,
                                    pattern=[[1, P]], channel_multiplier=-1).then_inc(s_const, 1)
            pool.iota(tile_no[:], pattern=[[1, TILES]], base=0, channel_multiplier=0,
                      allow_small_or_imprecise_dtypes=True).then_inc(s_const, 1)
            pool.iota(list0[:], pattern=[[STRIDE, NE]], base=0, channel_multiplier=0,
                      allow_small_or_imprecise_dtypes=True).then_inc(s_const, 1)
            pool.iota(rank_down[:], pattern=[[0, TT], [-1, NE]], base=NE, channel_multiplier=0,
                      allow_small_or_imprecise_dtypes=True).then_inc(s_const, 1)
            for par in range(2):
                pool.iota(rows[par][:, :, :, E].bitcast(i32), pattern=[[NTOK, TOPK], [P, TT]],
                          base=par * T - 2 * T, channel_multiplier=1).then_inc(s_const, 1)
            pool.iota(pad[:, :, E].bitcast(i32), pattern=[[P, NE + SPARE]], base=TOPK * NTOK,
                      channel_multiplier=1).then_inc(s_const, 1)
            nc.gpsimd.memset(pad[:, :, 0:E], 0.0).then_inc(s_const, 1)
            pool.wait_ge(s_const, N_CONST)
            pool.dma_start(lists.ap()[NE * STRIDE:NE * STRIDE + SPARE * P, :].rearrange("(k p) e -> p k e", p=P),
                           pad[:, NE:NE + SPARE, :]).then_inc(s_spare, 16)

            def scatter(b, c, tile):
                pool.indirect_dma_start(
                    lists.ap(), bass.IndirectOffsetOnAxis(ap=slot_i[b.par][:, c, tile:tile + 1], axis=0),
                    rows[b.par][:, c, tile, :], None).then_inc(s_sc[b.par], 16)

            def step(t):
                b3, b2, bm1, bm2 = t.off(3), t.off(2), t.off(-1), t.off(-2)
                for u in range(UNITS):
                    if t.real():
                        n = UNITS * t.n + u
                        done, = apart(pool, n + 1)
                        pool.wait_ge(s_exp, done)
                        if u % 3 == 2:
                            v = pr[:, slot(t, u), :].rearrange("p (h q) -> p h q", h=GROUP)
                        else:
                            v = pr[:, slot(t, u), :].rearrange("p (h q) -> p h q", h=2)[:, :, 0:P]
                        nc.gpsimd.affine_select(out=v, in_=v, compare_op=ALU.is_ge, fill=0.0, base=0,
                                                pattern=[[0, v.shape[1]], [1, P]],
                                                channel_multiplier=-1).then_inc(s_msk, 1)
                    if u == 7 and b2.real():
                        pool.wait_ge(s_mid, b2.n + 1)
                        nc.gpsimd.tensor_tensor(split[b2.par][:, :, 2], qk_rest[:], split[b2.par][:, :, 1],
                                                ALU.subtract).then_inc(s_lo, 1)
                    if u == 8 and b3.real():
                        pool.wait_ge(s_ve1, b3.n + 1)
                        nc.gpsimd.tensor_tensor(rstd1[:], ve1[:], half_neg[:], ALU.pow).then_inc(s_rstd1, 1)
                    if u == 9 and bm1.real():
                        pool.wait_ge(s_ve2, bm1.n + 1)
                        nc.gpsimd.tensor_tensor(rstd2[:], ve2[:], half_neg[:], ALU.pow).then_inc(s_rstd2, 1)
                    if u == 8 and bm1.real():
                        sent, = apart(pool, 16 * TOPK * TT * bm1.pair)
                        if bm1.after(2):
                            pool.wait_ge(s_sc[bm1.par], sent)
                        v = rows[bm1.par][:, :, :, E].bitcast(i32)
                        nc.gpsimd.tensor_scalar(v, v, float(2 * T), None, ALU.add).then_inc(s_rowno, 1)
                    if u in (5, 6, 7, 8) and bm2.real():
                        k = u - 5
                        if k == 0:
                            done, done2 = apart(pool, bm2.n + 1, 2 * (bm2.n + 1))
                            pool.wait_ge(s_slot, done)
                            pool.wait_ge(s_row0, done2)
                            pool.wait_ge(s_row1, done)
                            pool.wait_ge(s_rowno, done)
                        if k < 3:
                            scatter(bm2, k // 2, k % 2)
                        if k == 2:
                            scatter(bm2, 1, 1)

            def slot(t, u):
                return (UNITS * t.par + u) % NP

            run_steps(pool, step)

            def scatter_y(j, i, g):
                done, loaded = apart(pool, j + 1, 16 * (g + 1))
                pool.wait_ge(s_yt, done)
                pool.wait_ge(s_xt[i], loaded)
                pool.indirect_dma_start(
                    results.ap(), bass.IndirectOffsetOnAxis(ap=xt[i][:, E:E + 1].bitcast(i32), axis=0),
                    yt[i][:], None).then_inc(s_ys[i], 16)

            with pool.Fori(0, TILES // NX) as g:
                for i in range(NX):
                    scatter_y(NX * g + i, i, g)

        @block.scalar
        def _(act):
            act.dma_start(bias_in[:], biases).then_inc(s_bin, 16)

            def step(t):
                b2, b1, bm1 = t.off(2), t.off(1), t.off(-1)
                for u in range(UNITS):
                    if t.real():
                        n = UNITS * t.n + u
                        act.wait_ge(s_stp, n + 1)
                        if t.after(1) or u >= NP:
                            act.wait_ge(s_pv, NG * t.n + u // 3 - 1)
                        nc.scalar.activation(pr[:, (UNITS * t.par + u) % NP, :], ST[u % 2][:], ACT.Exp,
                                             scale=SCALE).then_inc(s_exp, 1)
                    if u == 0 and b2.real():
                        act.wait_ge(s_xT_ps, b2.n + 1)
                        nc.scalar.copy(xn1T[b2.par][:], PJ[:, 0:T]).then_inc(s_xT, 1)
                    if u == 6 and b2.real():
                        act.wait_ge(s_qk, b2.n + 1)
                        if b2.after(2):
                            act.wait_ge(s_pst[b2.par], 16 * b2.pair)
                        nc.scalar.copy(split[b2.par][:, :, 0], qk[:]).then_inc(s_hi, 1)
                        act.wait_ge(s_rest, b2.n + 1)
                        nc.scalar.copy(split[b2.par][:, :, 1], qk_rest[:]).then_inc(s_mid, 1)
                    if u == 2 and t.real():
                        turn_max(t, 1)
                    if u == 8 and b1.real():
                        turn_max(b1, 0)
                    if u == 2 and bm1.real():
                        out_pair(bm1, 1)
                    if u == 8 and t.real():
                        out_pair(t, 0)
                    if u == 6 and bm1.real():
                        act.wait_ge(s_onT_ps, bm1.n + 1)
                        nc.scalar.copy(onT[:], OC[:, 0:T]).then_inc(s_onT, 1)
                    if u == 10 and bm1.real():
                        act.wait_ge(s_x2T_ps, bm1.n + 1)
                        nc.scalar.copy(xn2T[:], OC[:, 0:T]).then_inc(s_x2T, 1)
                        act.wait_ge(s_row0, 2 * (bm1.n + 1))
                        if bm1.after(2):
                            act.wait_ge(s_sc[bm1.par], 16 * TOPK * TT * bm1.pair)
                        nc.scalar.copy(rows[bm1.par][:, 1, :, 0:E], rows[bm1.par][:, 0, :, 0:E]).then_inc(s_row1, 1)

            def turn_max(b, half):
                act.wait_ge(s_mT_ps, 2 * b.n + half + 1)
                if b.after(1):
                    act.wait_ge(s_ml[half], 16 * PARTS * b.n)
                nc.scalar.copy(mxT[half][:], mxT_ps).then_inc(s_mT, 1)

            def out_pair(b, k):
                act.wait_ge(s_pv, NG * b.n + 2 * k + 2)
                if b.after(1):
                    act.wait_ge(s_oc, 2 * b.n)
                nc.scalar.copy(ot[:, 2 * k:2 * k + 2, :].rearrange("p g q -> p (g q)"), OT[:]).then_inc(s_ot, 1)

            run_steps(act, step)

            act.wait_ge(s_g, 1)
            nc.scalar.activation(gate_t[:, 1, :], gate_t[:, 0, :], ACT.Exp).then_inc(s_gexp, 1)

            def copy_xT(j, i, first=False):
                act.wait_ge(s_tx, j + 1)
                nc.scalar.copy(xtT[i % 2][:], XT_PS[i % 2][:, 0:P]).then_inc(s_xtT, 1)

            def relu(j, i):
                act.wait_ge(s_hp, j + 1)
                nc.scalar.activation(hid[i % 2][:], HID_PS[i % 2][:], ACT.Relu).then_inc(s_hid, 1)

            def copy_y(j, i, g=None):
                act.wait_ge(s_yp, j + 1)
                if g is not None:
                    act.wait_ge(s_ys[i], 16 * g)
                nc.scalar.copy(yt[i][:], Y_PS[i % 2][:, 0:E]).then_inc(s_yt, 1)

            copy_xT(0, 0)
            copy_xT(1, 1)
            relu(0, 0)

            def tile(j, i, g=None, last=TILES):
                if j_in(j, 2, last):
                    copy_xT(j + 2, i)
                if j_in(j, 1, last):
                    relu(j + 1, i + 1)
                copy_y(j, i, g)

            for j in range(NX):
                tile(j, j)
            with act.Fori(1, TILES // NX - 1) as g:
                for i in range(NX):
                    tile(NX * g + i, i, g)
            for j in range(TILES - NX, TILES):
                tile(j, j % NX, j // NX)

        @block.vector
        def _(dve):
            nc.vector.memset(onesb[:], 1.0).then_inc(s_swap, 1)
            dve.wait_ge(s_const, N_CONST)
            nc.vector.tensor_copy(identb[:], ident[:]).then_inc(s_swap, 1)
            nc.vector.tensor_copy(used[:], list0[:]).then_inc(s_swap, 1)
            nc.vector.memset(zero_e[:], 0.0).then_inc(s_swap, 1)
            for i in range(2):
                nc.vector.memset(ka[i][64:P, :, :], 1.0).then_inc(s_swap, 1)
                nc.vector.memset(qa[i][64:P, :, :], 0.0).then_inc(s_swap, 1)
            for i in range(2):
                nc.vector.memset(va[i][:, :, :, D:VC], 0.0).then_inc(s_swap, 1)
            dve.wait_ge(s_swap, 10)
            for i in range(2):
                nc.vector.memset(va[i][:, :, :, D:D + 1], 1.0).then_inc(s_swap, 1)
            dve.wait_ge(s_w, N_W)
            for a in range(2):
                for z in range(2):
                    nc.vector.tensor_copy(wswap[:, a, :].rearrange("p (i z h) -> p i z h", z=2, h=H)[:, :, z, :],
                                          wqkv_sb[:, a, :].rearrange("p (i z h) -> p i z h", z=2, h=H)[:, :, 1 - z, :]
                                          ).then_inc(s_swap, 1)
            dve.wait_ge(s_bin, 16)
            nc.vector.tensor_copy(bias_split[:, 0], bias_in[:]).then_inc(s_bsplit, 1)
            dve.wait_ge(s_bsplit, 1)
            nc.vector.tensor_tensor(bias_rest[:, 0], bias_in[:], bias_split[:, 0], ALU.subtract).then_inc(s_bsplit, 1)
            dve.wait_ge(s_bsplit, 2)
            nc.vector.tensor_copy(bias_split[:, 1], bias_rest[:, 0]).then_inc(s_bsplit, 1)
            dve.wait_ge(s_bsplit, 3)
            nc.vector.tensor_tensor(bias_rest[:, 1], bias_rest[:, 0], bias_split[:, 1], ALU.subtract).then_inc(s_bsplit, 1)
            dve.wait_ge(s_bsplit, 4)
            nc.vector.tensor_copy(bias_split[:, 2], bias_rest[:, 1]).then_inc(s_bsplit, 1)

            def norm_stats(b, xin, stats, mv, ve, s_stat, s_mv, s_ve):
                for i in range(TT):
                    nc.vector.bn_stats(stats[:, i, :], xin(i)).then_inc(s_stat, 1)
                for i in range(TT):
                    done, = apart(dve, TT * b.n + i + 1)
                    dve.wait_ge(s_stat, done)
                    nc.vector.bn_aggr(mv[:, i, :], stats[:, i, :]).then_inc(s_mv, 1)
                dve.wait_ge(s_mv, TT * (b.n + 1))
                nc.vector.tensor_scalar(ve[:], mv[:, :, 1], EPS, None, ALU.add).then_inc(s_ve, 1)

            def rotate(b, which, s_ps, s_done):
                dve.wait_ge(s_ps, b.n + 1)
                nc.vector.scalar_tensor_tensor(rope_a[:, which], PJ[:, 0:T], qkb[:, which:which + 1],
                                               rope_sb[:, 0], ALU.add, ALU.mult).then_inc(s_done, 1)
                nc.vector.scalar_tensor_tensor(rope_b[:, which], PJ[:, T:2 * T], qkb[:, 2 + which:3 + which],
                                               rope_sb[:, 1], ALU.add, ALU.mult).then_inc(s_done, 1)

            def split_max(b, half, k):
                m = mx[b.par][:, half * HH:(half + 1) * HH, :]
                at = 4 * (2 * b.n + half)
                if k == 0:
                    dve.wait_ge(s_mx, UNITS * b.n + UNITS // 2 * (half + 1))
                    if half or b.after(1):
                        dve.wait_ge(s_mT_ps, 2 * b.n + half)
                    nc.vector.tensor_scalar(mx_split[:, 0], m, -1.0, None, ALU.mult).then_inc(s_ms, 1)
                elif k == 1:
                    dve.wait_ge(s_ms, at + 1)
                    nc.vector.scalar_tensor_tensor(mx_rest[:], m, -1.0, mx_split[:, 0], ALU.mult,
                                                   ALU.subtract).then_inc(s_ms, 1)
                elif k == 2:
                    dve.wait_ge(s_ms, at + 2)
                    nc.vector.tensor_copy(mx_split[:, 1], mx_rest[:]).then_inc(s_ms, 1)
                else:
                    dve.wait_ge(s_ms, at + 3)
                    nc.vector.tensor_tensor(mx_split[:, 2], mx_rest[:], mx_split[:, 1],
                                            ALU.subtract).then_inc(s_ms, 1)

            ROUTE = 13

            def route(b, k):
                at = ROUTE * b.n
                if k > 0:
                    dve.wait_ge(s_rt, at + k)
                lgb = lg[b.par]
                tiles = bass.ds(TT * b.n, TT) if not b.known else slice(TT * b.n, TT * b.n + TT)

                def wide(v):
                    return v.unsqueeze(2).to_broadcast([P, TT, NE])

                if k == 0:
                    dve.wait_ge(s_lg, b.n + 1)
                    ins = nc.vector.tensor_reduce(top[:, 0, tiles], lgb[:], X, ALU.max)
                elif k == 1:
                    ins = nc.vector.tensor_tensor(r_dif[:], lgb[:], wide(top[:, 0, tiles]), ALU.is_ge)
                elif k == 2:
                    ins = nc.vector.tensor_tensor(r_key[:], r_dif[:], rank_down[:], ALU.mult)
                elif k == 3:
                    ins = nc.vector.tensor_reduce(r_kmax[:], r_key[:], X, ALU.max)
                elif k == 4:
                    ins = nc.vector.tensor_tensor(chosen[:, 0], r_key[:], wide(r_kmax[:]), ALU.is_equal)
                elif k == 5:
                    ins = nc.vector.scalar_tensor_tensor(r_rest[:], chosen[:, 0], HIDDEN_MASK, lgb[:],
                                                         ALU.mult, ALU.add)
                elif k == 6:
                    ins = nc.vector.tensor_reduce(top[:, 1, tiles], r_rest[:], X, ALU.max)
                elif k == 7:
                    ins = nc.vector.tensor_tensor(r_dif[:], r_rest[:], wide(top[:, 1, tiles]), ALU.is_ge)
                elif k == 8:
                    ins = nc.vector.tensor_tensor(r_key[:], r_dif[:], rank_down[:], ALU.mult)
                elif k == 9:
                    ins = nc.vector.tensor_reduce(r_kmax[:], r_key[:], X, ALU.max)
                elif k == 10:
                    ins = nc.vector.tensor_tensor(chosen[:, 1], r_key[:], wide(r_kmax[:]), ALU.is_equal)
                elif k == 11:
                    ins = nc.vector.tensor_tensor(both[:], chosen[:, 0], chosen[:, 1], ALU.add)
                elif k == 12:
                    dve.wait_ge(s_rk_ps, b.n + 1)
                    ins = nc.vector.tensor_tensor(slot_of[:], MISC[:, 0:TT * NE].rearrange("p (t e) -> p t e", e=NE),
                                                  used[:].unsqueeze(1).to_broadcast([P, TT, NE]), ALU.add)
                ins.then_inc(s_rt, 1)

            def route_end(b, k):
                at = 3 * b.n
                if k == 0:
                    dve.wait_ge(s_rt, ROUTE * (b.n + 1))
                    nc.vector.tensor_tensor(used[:], used[:], MISC[:, TT * NE:(TT + 1) * NE],
                                            ALU.add).then_inc(s_used, 1)
                    nc.vector.tensor_tensor(slot_sel[:], chosen[:], slot_of[:].unsqueeze(1).to_broadcast([P, TOPK, TT, NE]),
                                            ALU.mult).then_inc(s_used, 1)
                elif k == 1:
                    dve.wait_ge(s_used, at + 2)
                    nc.vector.tensor_reduce(slot_f[:], slot_sel[:], X, ALU.add).then_inc(s_used, 1)
                else:
                    dve.wait_ge(s_used, at + 3)
                    nc.vector.tensor_copy(slot_i[b.par][:], slot_f[:]).then_inc(s_slot, 1)

            def tiles_of(b, i):
                return TT * b.n + i

            def xrow(b, i):
                if b.known:
                    return x_sb[:, TT * b.n + i, :]
                return x_sb[:, bass.ds(TT * b.n + i, 1), :].rearrange("p a e -> p (a e)")

            def step(t):
                b3, b2, b1, bm1, bm2 = t.off(3), t.off(2), t.off(1), t.off(-1), t.off(-2)
                for u in range(UNITS):
                    if b1.real():
                        n = UNITS * b1.n + u
                        dve.wait_ge(s_sq, n + 1)
                        g = u // 3
                        if u % 3 == 2:
                            src = SQ[u % 2][:].rearrange("p (h k) -> p h k", h=GROUP)
                            dst = mx[b1.par][:, GROUP * g:GROUP * g + GROUP, 0]
                        else:
                            h0 = GROUP * g + 2 * (u % 3)
                            src = SQ[u % 2][:].rearrange("p (h k) -> p h k", h=2)
                            dst = mx[b1.par][:, h0:h0 + 2, 1]
                        if u % (UNITS // 2) == 0 and b1.after(1):
                            pass
                        nc.vector.tensor_reduce(dst, src, X, ALU.max).then_inc(s_mx, 1)
                    if u in (0, 1) and t.real():
                        split_max(t, 1, 2 * u)
                        split_max(t, 1, 2 * u + 1)
                    if u in (6, 7) and b1.real():
                        split_max(b1, 0, 2 * (u - 6))
                        split_max(b1, 0, 2 * (u - 6) + 1)
                    if u == 1 and b2.real():
                        rotate(b2, 0, s_q_ps, s_qrot)
                    if u == 3 and b2.real():
                        rotate(b2, 1, s_k_ps, s_krot)
                    if u == 4 and b2.real():
                        dve.wait_ge(s_krot, 2 * (b2.n + 1))
                        if b2.after(1):
                            dve.wait_ge(s_rest, b2.n)
                            dve.wait_ge(s_hi, b2.n)
                        nc.vector.tensor_tensor(qk[:], rope_a[:], rope_b[:], ALU.add).then_inc(s_qk, 1)
                    if u == 5 and b1.real():
                        dve.wait_ge(s_v_ps, b1.n + 1)
                        if b1.after(2):
                            dve.wait_ge(s_pv, NG * (b1.n - 1))
                        nc.vector.tensor_copy(va[b1.par][:, :, :, 0:D],
                                              PJ[:, 0:T].rearrange("p (t h d) -> p t h d", t=TT, d=D)).then_inc(s_va, 1)
                    if u == 6 and b2.real():
                        dve.wait_ge(s_hi, b2.n + 1)
                        if b2.after(1):
                            dve.wait_ge(s_lo, b2.n)
                            dve.wait_ge(s_mid, b2.n)
                        nc.vector.tensor_tensor(qk_rest[:], qk[:], split[b2.par][:, :, 0], ALU.subtract).then_inc(s_rest, 1)
                    if u in (3, 5) and bm1.real():
                        qt = (u - 3) // 2
                        dve.wait_ge(s_oc, 2 * bm1.n + qt + 1)
                        o4 = OC[:].rearrange("p (h c) -> p h c", c=VC)
                        nc.vector.reciprocal(rec[:, qt, :], o4[:, :, D]).then_inc(s_rec, 1)
                        dve.wait_ge(s_rec, 2 * bm1.n + qt + 1)
                        nc.vector.tensor_tensor(on[:, qt, :].rearrange("p (h d) -> p h d", d=D), o4[:, :, 0:D],
                                                rec[:, qt, :].unsqueeze(2).to_broadcast([P, H, D]),
                                                ALU.mult).then_inc(s_on, 1)
                    if u == 8 and bm1.real():
                        dve.wait_ge(s_y_ps, bm1.n + 1)
                        xr = (x_sb[:, TT * bm1.n:TT * (bm1.n + 1), :] if bm1.known
                              else x_sb[:, bass.ds(TT * bm1.n, TT), :])
                        nc.vector.tensor_tensor(xr, OC[:, 0:T].rearrange("p (t e) -> p t e", t=TT), xr,
                                                ALU.add).then_inc(s_x1, 1)
                        done, = apart(dve, bm1.n + 1)
                        dve.wait_ge(s_x1, done)
                        norm_stats(bm1, lambda i: xrow(bm1, i), stats2, mv2, ve2, s_st2, s_mv2, s_ve2)
                    if u == 7 and b3.real():
                        if b3.known and b3.n in (0, 1, 4):
                            dve.wait_ge(s_x[{0: 0, 1: 1, 4: 2}[b3.n]], 16)
                        norm_stats(b3, lambda i: xrow(b3, i), stats1, mv1, ve1, s_st1, s_mv1, s_ve1)
                    if u == 9 and b3.real():
                        dve.wait_ge(s_rstd1, b3.n + 1)
                        if b3.after(1):
                            dve.wait_ge(s_xT_ps, b3.n)
                        for i in range(TT):
                            nc.vector.tensor_scalar(xn1[:, i, :], xrow(b3, i), mv1[:, i, 0:1], rstd1[:, i:i + 1],
                                                    ALU.subtract, ALU.mult).then_inc(s_xn1, 1)
                    if u == 9 and bm1.real():
                        dve.wait_ge(s_rstd2, bm1.n + 1)
                        if bm1.after(2):
                            dve.wait_ge(s_sc[bm1.par], 16 * TOPK * TT * bm1.pair)
                        for i in range(TT):
                            nc.vector.tensor_scalar(rows[bm1.par][:, 0, i, 0:E], xrow(bm1, i), mv2[:, i, 0:1],
                                                    rstd2[:, i:i + 1], ALU.subtract, ALU.mult).then_inc(s_row0, 1)
                    if u == 0 and bm2.real():
                        dve.wait_ge(s_lg_ps, bm2.n + 1)
                        nc.vector.tensor_copy(lg[bm2.par][:], OC[:, 0:TT * NE].rearrange("p (t e) -> p t e", e=NE)).then_inc(s_lg, 1)
                    if bm2.real():
                        if u < 4:
                            for k in range(3 * u, 3 * u + 3):
                                if k == 11:
                                    if bm2.after(1):
                                        dve.wait_ge(s_rk_ps, bm2.n)
                                route(bm2, k)
                        if u == 5:
                            route(bm2, 12)
                            if bm2.after(2):
                                dve.wait_ge(s_sc[bm2.par], 16 * TOPK * TT * bm2.pair)
                            for k in range(3):
                                route_end(bm2, k)

            run_steps(dve, step)

            chain = [0]

            def then(ins):
                chain[0] += 1
                ins.then_inc(s_tab, 1)
                dve.wait_ge(s_tab, chain[0])

            dve.wait_ge(s_used, 3 * NB)
            then(nc.vector.tensor_copy(pad_at[:], used[0:1, :]))
            then(nc.vector.tensor_tensor(count[:], used[0:1, :], list0[0:1, :], ALU.subtract))
            then(nc.vector.tensor_scalar(count_i[:, 0], count[:], float(P - 1), None, ALU.add))
            then(nc.vector.tensor_scalar(count_i[:, 1], count_i[:, 0], P.bit_length() - 1, None,
                                         ALU.arith_shift_right))
            then(nc.vector.tensor_copy(tiles_f[:], count_i[:, 1]))
            then(nc.vector.tensor_tensor_scan(tiles_end[:], tiles_f[:], zero_e[:], 0.0, ALU.add, ALU.add))
            then(nc.vector.tensor_scalar(jump[:], tiles_f[:], float(-P), float(STRIDE), ALU.mult, ALU.add))
            then(nc.vector.tensor_tensor(ended[:], tile_no[:].unsqueeze(2).to_broadcast([1, TILES, NE]),
                                         tiles_end[:].unsqueeze(1).to_broadcast([1, TILES, NE]), ALU.is_ge))
            then(nc.vector.tensor_reduce(tab_f[:, 0], ended[:], X, ALU.add))
            then(nc.vector.tensor_tensor(ended_j[:], ended[:], jump[:].unsqueeze(1).to_broadcast([1, TILES, NE]), ALU.mult))
            then(nc.vector.tensor_reduce(tab_f[:, 1], ended_j[:], X, ALU.add))
            then(nc.vector.scalar_tensor_tensor(tab_f[:, 2], tile_no[:], float(P), tab_f[:, 1], ALU.mult, ALU.add))
            then(nc.vector.tensor_scalar(tab[:, 0], tab_f[:, 0], float(NE - 1), None, ALU.min))
            nc.vector.tensor_copy(tab[:, 1], tab_f[:, 2]).then_inc(s_tabs, 1)
            nc.vector.tensor_tensor(gate_t[:, 0], top[:, 1], top[:, 0], ALU.subtract).then_inc(s_g, 1)
            dve.wait_ge(s_gexp, 1)
            nc.vector.tensor_scalar(gate_t[:, 2], gate_t[:, 1], 1.0, None, ALU.add).then_inc(s_g, 1)
            dve.wait_ge(s_g, 2)
            nc.vector.reciprocal(gate[:, 0], gate_t[:, 2]).then_inc(s_g, 1)
            dve.wait_ge(s_g, 3)
            nc.vector.tensor_tensor(gate[:, 1], gate_t[:, 1], gate[:, 0], ALU.mult).then_inc(s_gate, 1)

            def copy_hT(j, i):
                dve.wait_ge(s_thp, j + 1)
                nc.vector.tensor_copy(hidT[i % 2][:], HIDT_PS[i % 2][:]).then_inc(s_hidT, 1)

            with dve.Fori(0, TILES // 2) as g:
                for i in range(2):
                    copy_hT(2 * g + i, i)

            dve.wait_ge(s_gate, 1)
            for c in range(NC_FIN):
                dve.wait_ge(s_fl[c % 4], 16 * TOPK * (c // 4 + 1))
                for i in range(NF):
                    n = c * NF + i
                    nc.vector.scalar_tensor_tensor(fin[c % 4][:, 0, i], fin[c % 4][:, 0, i], gate[:, 0, n:n + 1],
                                                   x_sb[:, n, :], ALU.mult, ALU.add).then_inc(s_fs, 1)
                for i in range(NF):
                    n = c * NF + i
                    dve.wait_ge(s_fs, n + 1)
                    nc.vector.scalar_tensor_tensor(x_sb[:, n, :], fin[c % 4][:, 1, i], gate[:, 1, n:n + 1],
                                                   fin[c % 4][:, 0, i], ALU.mult, ALU.add).then_inc(s_fin, 1)

        @block.tensor
        def _(pe):
            pe.wait_ge(s_const, N_CONST)
            pe.wait_ge(s_w, N_W)
            pe.wait_ge(s_swap, 16)

            def add_bias(dst, at, n, stop=True):
                return nc.tensor.matmul(dst, onesb[0:PARTS, 0:dst.shape[0]], bias_rows[:, at:at + n],
                                        start=False, stop=stop, skip_group_check=True)

            def max_unit(b, u):
                n = UNITS * b.n + u
                g, dst = u // 3, SQ[u % 2]
                if b.after(1) or u >= 2:
                    pe.wait_ge(s_mx, n - 1)
                if u % 6 == 0:
                    pe.wait_ge(s_ld[u // 6][b.par], 16 * LD_DMAS * (b.pair + 1))
                q, k = qa[b.par], ka[b.par]
                if u % 3 == 2:
                    for j in range(GROUP):
                        h = GROUP * g + j
                        nc.tensor.matmul(dst[:, j * P:(j + 1) * P], q[0:QK_ROWS, h, 0:P], k[0:QK_ROWS, h, 0:P],
                                         start=(j == 0), stop=False, skip_group_check=True)
                    nc.tensor.matmul(dst[:].rearrange("p (h k) -> p h k", h=GROUP), identb[:],
                                     maskb[:].unsqueeze(1).to_broadcast([P, GROUP, P]), start=False, stop=True,
                                     skip_group_check=True).then_inc(s_sq, 1)
                else:
                    for j in range(2):
                        h = GROUP * g + 2 * (u % 3) + j
                        nc.tensor.matmul(dst[:, j * T:(j + 1) * T], q[0:QK_ROWS, h, P:T], k[0:QK_ROWS, h, :],
                                         start=(j == 0), stop=False, skip_group_check=True)
                    nc.tensor.matmul(dst[:].rearrange("p (h k) -> p h k", h=2)[:, :, P:T], identb[:],
                                     maskb[:].unsqueeze(1).to_broadcast([P, 2, P]), start=False, stop=True,
                                     skip_group_check=True).then_inc(s_sq, 1)

            def exp_unit(b, u):
                n = UNITS * b.n + u
                g, dst = u // 3, ST[u % 2]
                if b.after(1) or u >= 2:
                    pe.wait_ge(s_exp, n - 1)
                if u % 6 == 0:
                    pe.wait_ge(s_ml[u // 6], 16 * PARTS * (b.n + 1))
                q, k = qa[b.par], ka[b.par]
                if u % 3 == 2:
                    for j in range(GROUP):
                        h = GROUP * g + j
                        last = nc.tensor.matmul(dst[:, j * P:(j + 1) * P], k[:, h, P:T], q[:, h, P:T],
                                                start=True, stop=True)
                else:
                    for j in range(2):
                        h = GROUP * g + 2 * (u % 3) + j
                        last = nc.tensor.matmul(dst[:, j * T:(j + 1) * T], k[:, h, 0:P], q[:, h, :],
                                                start=True, stop=True)
                last.then_inc(s_stp, 1)

            def times_v(b, g):
                pe.wait_ge(s_msk, UNITS * b.n + 3 * g + 3)
                if g == 0:
                    pe.wait_ge(s_va, b.n + 1)
                if g % 2 == 0 and (g or b.after(1)):
                    pe.wait_ge(s_ot, 2 * b.n + g // 2)
                s0 = UNITS * b.par + 3 * g
                dst = OT[:, (g % 2) * T:(g % 2 + 1) * T]
                for j in range(GROUP):
                    p = pr[:, (s0 + j // 2) % NP, :].rearrange("p (h q) -> p h q", h=2)[:, j % 2, :]
                    nc.tensor.matmul(dst[32 * j:32 * j + VC, :], va[b.par][:, 0, GROUP * g + j, :], p,
                                     start=True, stop=False, skip_group_check=True)
                for j in range(GROUP):
                    p = pr[:, (s0 + 2) % NP, j * P:(j + 1) * P]
                    last = nc.tensor.matmul(dst[32 * j:32 * j + VC, P:T], va[b.par][:, 1, GROUP * g + j, :], p,
                                            start=False, stop=True, skip_group_check=True)
                last.then_inc(s_pv, 1)

            def turn_max(b, half):
                split_done, copied, used_read = apart(pe, 4 * (2 * b.n + half) + 4, 2 * b.n + half,
                                                      3 * (b.n - 3) + 1)
                pe.wait_ge(s_ms, split_done)
                if half or b.after(1):
                    pe.wait_ge(s_mT, copied)
                if half == 0 and b.after(3):
                    pe.wait_ge(s_used, used_read)
                nc.tensor.transpose(mxT_ps, mx_split[:].rearrange("p a h t -> p (a h t)"),
                                    identb[:]).then_inc(s_mT_ps, 1)

            def project(b, u):
                if u == 0:
                    pe.wait_ge(s_xn1, TT * (b.n + 1))
                    if b.after(1):
                        pe.wait_ge(s_krot, 2 * b.n)
                    if b.after(2):
                        pe.wait_ge(s_va, b.n - 1)
                    for i in range(TT):
                        last = nc.tensor.transpose(PJ[:, i * P:(i + 1) * P], xn1[:, i, :], ident[:])
                    last.then_inc(s_xT_ps, 1)
                elif u == 1:
                    pe.wait_ge(s_xT, b.n + 1)
                    nc.tensor.matmul(PJ[:, 0:T], wqkv_sb[:, 0, :], xn1T[b.par][:], start=True, stop=True)
                    nc.tensor.matmul(PJ[:, T:2 * T], wswap[:, 0, :], xn1T[b.par][:], start=True, stop=True).then_inc(s_q_ps, 1)
                elif u == 2:
                    pe.wait_ge(s_qrot, 2 * (b.n + 1))
                    nc.tensor.matmul(PJ[:, 0:T], wqkv_sb[:, 1, :], xn1T[b.par][:], start=True, stop=True)
                    nc.tensor.matmul(PJ[:, T:2 * T], wswap[:, 1, :], xn1T[b.par][:], start=True, stop=True).then_inc(s_k_ps, 1)

            def project_v(b):
                    if b.off(1).real():
                        pe.wait_ge(s_krot, 2 * (b.n + 2))
                    if b.known and b.n == 0:
                        pe.wait_ge(s_brow, 16)
                    for i in range(TT):
                        nc.tensor.matmul(PJ[:, i * P:(i + 1) * P], xn1T[b.par][:, i * P:(i + 1) * P], wqkv_sb[:, 2, :],
                                         start=(i == 0), stop=False, skip_group_check=True)
                        last = add_bias(PJ[:, i * P:(i + 1) * P], BV_AT, E)
                    last.then_inc(s_v_ps, 1)

            def finish(b, u):
                if u in (3, 5):
                    qt = (u - 3) // 2
                    pe.wait_ge(s_ot, 2 * (b.n + 1))
                    if qt == 1:
                        pe.wait_ge(s_on, 2 * b.n + 1)
                    elif b.after(1):
                        pe.wait_ge(s_lg, b.n)
                    for g in range(NG):
                        last = nc.tensor.transpose(OC[:, g * P:(g + 1) * P], ot[:, g, qt * P:(qt + 1) * P], ident[:])
                    last.then_inc(s_oc, 1)
                elif u == 6:
                    pe.wait_ge(s_on, 2 * (b.n + 1))
                    for i in range(TT):
                        last = nc.tensor.transpose(OC[:, i * P:(i + 1) * P], on[:, i, :], ident[:])
                    last.then_inc(s_onT_ps, 1)
                elif u == 7:
                    pe.wait_ge(s_onT, b.n + 1)
                    for i in range(TT):
                        nc.tensor.matmul(OC[:, i * P:(i + 1) * P], onT[:, i * P:(i + 1) * P], wproj_sb[:],
                                         start=(i == 0), stop=False, skip_group_check=True)
                        last = add_bias(OC[:, i * P:(i + 1) * P], BP_AT, E)
                    last.then_inc(s_y_ps, 1)
                elif u == 10:
                    pe.wait_ge(s_row0, TT * (b.n + 1))
                    for i in range(TT):
                        last = nc.tensor.transpose(OC[:, i * P:(i + 1) * P], rows[b.par][:, 0, i, 0:E], ident[:])
                    last.then_inc(s_x2T_ps, 1)
                elif u == 11:
                    pe.wait_ge(s_x2T, b.n + 1)
                    for i in range(TT):
                        nc.tensor.matmul(OC[:, i * NE:(i + 1) * NE], xn2T[:, i * P:(i + 1) * P], wr_sb[:],
                                         start=(i == 0), stop=False, skip_group_check=True)
                        last = add_bias(OC[:, i * NE:(i + 1) * NE], BR_AT, NE)
                    last.then_inc(s_lg_ps, 1)

            def ranks(b):
                pe.wait_ge(s_rt, ROUTE * b.n + 12)
                pe.wait_ge(s_mT, min(2 * b.n + 6, 2 * NB) if b.known else 2 * b.n + 6)
                if b.after(1):
                    pe.wait_ge(s_used, 3 * b.n - 2)
                r = MISC[:, 0:(TT + 1) * NE]
                m = both[:].rearrange("p t e -> p (t e)")
                nc.tensor.matmul(r[:, 0:TT * NE], beforeb[:], m, start=True, stop=False, skip_group_check=True)
                for i in range(TT):
                    last = nc.tensor.matmul(r[:, (i + 1) * NE:(TT + 1) * NE], onesb[:], m[:, 0:(TT - i) * NE],
                                            start=False, stop=(i == TT - 1), skip_group_check=True)
                last.then_inc(s_rk_ps, 1)

            ROUTE = 13

            def step(t):
                b2, b1, bm1, bm2 = t.off(2), t.off(1), t.off(-1), t.off(-2)
                for u in range(UNITS):
                    if b1.real():
                        max_unit(b1, u)
                    if t.real():
                        exp_unit(t, u)
                    if b2.real():
                        project(b2, u)
                    if u == 4 and b1.real():
                        project_v(b1)
                    if u in (4, 7, 10) and t.real():
                        times_v(t, (u - 4) // 3)
                    if u == 1 and bm1.real():
                        times_v(bm1, NG - 1)
                    if u == 2 and t.real():
                        turn_max(t, 1)
                    if u == 8 and b1.real():
                        turn_max(b1, 0)
                    if bm1.real():
                        finish(bm1, u)
                    if u == 4 and bm2.real():
                        ranks(bm2)

            run_steps(pe, step)

            pe.wait_ge(s_tabs, 1)
            pe.wait_ge(s_we, 32)

            def turn_tile(j, i, g):
                pe.wait_ge(s_xt[i % NX], 16 * (g + 1))
                if j_in_loop(j, 2):
                    pe.wait_ge(s_xtT, j - 1)
                nc.tensor.transpose(XT_PS[i % 2][:, 0:P], xt[i % NX][:, 0:E], ident[:]).then_inc(s_tx, 1)

            def hidden(j, i):
                e = pe.value_load(tab[0:1, 0, bass.ds(j, 1)], min_val=0, max_val=NE - 1)
                pe.wait_ge(s_xtT, j + 1)
                if j_in_loop(j, 2):
                    pe.wait_ge(s_hid, j - 1)
                dst = HID_PS[i % 2][:]
                nc.tensor.matmul(dst, xtT[i % 2][:], w1_sb[:, bass.ds(e, 1), :].rearrange("p a n -> p (a n)"),
                                 start=True, stop=False)
                nc.tensor.matmul(dst, onesb[0:PARTS, :], bias_rows[:, bass.ds(e * HID + B1_AT, HID)],
                                 start=False, stop=True).then_inc(s_hp, 1)
                return e

            def turn_hidden(j, i):
                pe.wait_ge(s_hid, j + 1)
                if j_in_loop(j, 2):
                    pe.wait_ge(s_hidT, j - 1)
                for k in range(KT):
                    last = nc.tensor.transpose(HIDT_PS[i % 2][:, k * P:(k + 1) * P],
                                               hid[i % 2][:, k * P:(k + 1) * P], ident[:])
                last.then_inc(s_thp, 1)

            def second(j, i):
                e = pe.value_load(tab[0:1, 0, bass.ds(j, 1)], min_val=0, max_val=NE - 1)
                pe.wait_ge(s_hidT, j + 1)
                if j_in_loop(j, 2):
                    pe.wait_ge(s_yt, j - 1)
                dst = Y_PS[i % 2][:, 0:E]
                for k in range(KT):
                    nc.tensor.matmul(dst, hidT[i % 2][:, k * P:(k + 1) * P],
                                     w2_sb[:, bass.ds(e, 1), k, :].rearrange("p a n -> p (a n)"),
                                     start=(k == 0), stop=False)
                nc.tensor.matmul(dst, onesb[0:PARTS, :], bias_rows[:, bass.ds(e * E + B2_AT, E)],
                                 start=False, stop=True).then_inc(s_yp, 1)

            def j_in_loop(j, n):
                return j >= n if isinstance(j, int) else True

            def tile(j, i, g, last=TILES):
                if j_in(j, 2, last):
                    turn_tile(j + 2, i + 2, g + (i + 2) // NX)
                turn_hidden(j, i)
                if j_in(j, 1, last):
                    hidden(j + 1, i + 1)
                second(j, i)

            turn_tile(0, 0, 0)
            turn_tile(1, 1, 0)
            hidden(0, 0)
            for j in range(NX):
                tile(j, j, 0)
            with pe.Fori(1, TILES // NX - 1) as g:
                for i in range(NX):
                    tile(NX * g + i, i, g)
            for j in range(TILES - NX, TILES):
                tile(j, j % NX, j // NX)


def rope_table():
    pos = np.arange(T, dtype=np.float32)
    inv = (1.0 / np.float32(10000.0) ** (np.arange(0, D, 2, dtype=np.float32) / np.float32(D))).astype(np.float32)
    ang = pos[:, None] * inv[None, :]
    w = np.arange(P) // H
    c = np.cos(ang).astype(np.float32)[:, w // 2].T
    s = np.sin(ang).astype(np.float32)[:, w // 2].T * np.where(w % 2, 1, -1).astype(np.float32)[:, None]
    return np.ascontiguousarray(np.stack([c, s], axis=1).astype(np.float32))


def kernel(**inputs):
    import numpy as _np
    import concourse.bacc as _bacc
    from concourse import mybir as _mybir
    from concourse.bass_utils import run_bass_kernel_spmd as _run

    a = {k: _np.asarray(v) for k, v in inputs.items()}
    order = _np.arange(P).reshape(H, D).T.reshape(-1)
    swapped = order.reshape(D // 2, 2, H)[:, ::-1].reshape(-1)
    cols = _np.concatenate([order, P + order, 2 * P + _np.arange(P)])
    bqkv = a["L0_attn_bqkv"]
    bias = _np.concatenate([a["L0_ffn_b1"].reshape(-1), a["L0_ffn_b2"].reshape(-1), a["L0_attn_bproj"],
                            bqkv[2 * P:], a["L0_ffn_br"]])
    bias = _np.concatenate([bias, _np.zeros(NBIAS - bias.size, bias.dtype)])
    arrays = {
        "x": a["L0_attn_x"].reshape(NTOK, E),
        "wqkv": a["L0_attn_Wqkv"][:, cols],
        "qk_bias": _np.stack([bqkv[order], bqkv[P + order], bqkv[swapped], bqkv[P + swapped]], axis=1),
        "wproj": a["L0_attn_Wproj"],
        "w1": a["L0_ffn_W1"],
        "w2": a["L0_ffn_W2"],
        "wr": a["L0_ffn_Wr"],
        "biases": bias.reshape(P, BIAS_COLS),
        "rope": rope_table(),
    }
    arrays = {k: _np.ascontiguousarray(v) for k, v in arrays.items()}
    nc = _bacc.Bacc("TRN2", target_bir_lowering=False, num_devices=1)
    args = [nc.dram_tensor(k, v.shape, _mybir.dt.from_np(v.dtype), kind="ExternalInput").ap()
            for k, v in arrays.items()]
    y = nc.dram_tensor("y", (NTOK, E), fp32, kind="ExternalOutput").ap()
    layer(nc, *args, y)
    r = _run(nc, [arrays], core_ids=[0])
    return r.results[0]["y"].reshape(NB, T, E)
```

```python
import numpy as np
import concourse.bass as bass
from concourse import mybir
from contextlib import ExitStack

fp32 = mybir.dt.float32
bf16 = mybir.dt.bfloat16
i32 = mybir.dt.int32
ALU = mybir.AluOpType
ACT = mybir.ActivationFunctionType
X = mybir.AxisListType.X

NB, T, E = 16, 256, 128
H, D = 16, 8
NE, HID, TOPK = 8, 512, 2
P = 128
TT = T // P
NT = NB * TT
NTOK = NB * T
EPS = 1e-5
SCALE = D ** -0.5
HIDDEN_MASK = -3.0e38

PARTS = 3
TERMS = PARTS * PARTS
QK_ROWS = TERMS * D
HH = H // 2
GROUP = 4
NG = H // GROUP
UNITS = 3 * NG
VC = 32

STRIDE = NTOK + P
TILES = NTOK * TOPK // P + NE
SPARE = NE
ROW = E + 1
KT = HID // P
BIAS_COLS = 43
B1_AT, B2_AT = 0, NE * HID
BP_AT = B2_AT + NE * E
BV_AT = BP_AT + E
BR_AT = BV_AT + E
NBIAS = P * BIAS_COLS


class Batch:

    def __init__(self, pair, par):
        self.pair, self.par, self.n = pair, par, 2 * pair + par
        self.known = isinstance(pair, int)

    def off(self, d):
        return Batch(self.pair + (self.par + d) // 2, (self.par + d) % 2)

    def real(self):
        return 0 <= self.n < NB if self.known else True

    def after(self, n):
        return self.n >= n if self.known else True


FIRST_STEP, LOOP_FROM, LOOP_PAIRS, LAST_STEP = -4, 5, 3, NB + 3
LEAD = 3


def run_steps(eng, step):
    for t in range(FIRST_STEP, LOOP_FROM):
        step(Batch(t // 2, t % 2))
    with eng.Fori(LOOP_FROM // 2, LOOP_FROM // 2 + LOOP_PAIRS) as pair:
        step(Batch(pair, 1))
        step(Batch(pair + 1, 0))
    for t in range(LOOP_FROM + 2 * LOOP_PAIRS, LAST_STEP):
        step(Batch(t // 2, t % 2))


def layer(nc, x, wqkv, qk_bias, wproj, w1, w2, wr, biases, rope, out):
    ctx = ExitStack()
    with ctx:
        def sb(name, shape, dt=fp32):
            return ctx.enter_context(nc.sbuf_tensor(name, shape, dt))

        def sem(name):
            return ctx.enter_context(nc.semaphore(name))

        q_dram = nc.dram_tensor("q_dram", [2, PARTS, D, H, T], bf16)
        k_dram = nc.dram_tensor("k_dram", [2, D, PARTS, H, T], bf16)
        bias_dram = nc.dram_tensor("bias_dram", [PARTS, NBIAS], bf16)
        lists = nc.dram_tensor("lists", [NE * STRIDE + SPARE * P, ROW], fp32)
        results = nc.dram_tensor("results", [TOPK * NTOK + (NE + SPARE) * P, E], fp32)

        x_sb = sb("x_sb", [P, NT, E])
        wqkv_sb = sb("wqkv_sb", [P, 3, E])
        wswap = sb("wswap", [P, 2, E])
        wproj_sb = sb("wproj_sb", [P, E])
        wr_sb = sb("wr_sb", [P, NE])
        w1_sb = sb("w1_sb", [P, NE, HID])
        w2_sb = sb("w2_sb", [P, NE, KT, E])
        qkb = sb("qkb", [P, 4])
        rope_sb = sb("rope_sb", [P, 2, T])
        bias_in = sb("bias_in", [P, BIAS_COLS])
        bias_rest = sb("bias_rest", [P, 2, BIAS_COLS])
        bias_split = sb("bias_split", [P, PARTS, BIAS_COLS], bf16)
        bias_rows = sb("bias_rows", [PARTS, NBIAS], bf16)
        ident = sb("ident", [P, P])
        identb = sb("identb", [P, P], bf16)
        maskb = sb("maskb", [P, P], bf16)
        beforeb = sb("beforeb", [P, P], bf16)
        onesb = sb("onesb", [P, P], bf16)
        half_neg = sb("half_neg", [P, TT])
        rank_down = sb("rank_down", [P, TT, NE])
        stats1 = sb("stats1", [P, TT, 6])
        mv1 = sb("mv1", [P, TT, 2])
        ve1 = sb("ve1", [P, TT])
        rstd1 = sb("rstd1", [P, TT])
        xn1 = sb("xn1", [P, TT, E])
        xn1T = [sb(f"xn1T{i}", [P, T]) for i in range(2)]
        rope_a = sb("rope_a", [P, 2, T])
        rope_b = sb("rope_b", [P, 2, T])
        qk = sb("qk", [P, 2, T])
        qk_rest = sb("qk_rest", [P, 2, T])
        split = [sb(f"split{i}", [P, 2, PARTS, T], bf16) for i in range(2)]
        qa = [sb(f"qa{i}", [P, H, T], bf16) for i in range(2)]
        ka = [sb(f"ka{i}", [P, H, T], bf16) for i in range(2)]
        v_new = sb("v_new", [P, TT, E])
        va = [sb(f"va{i}", [P, TT, H, VC]) for i in range(2)]
        mx = [sb(f"mx{i}", [P, H, TT]) for i in range(2)]
        mx_rest = sb("mx_rest", [P, HH, TT])
        mx_split = sb("mx_split", [P, PARTS, HH, TT], bf16)
        mxT = [sb(f"mxT{i}", [PARTS * HH * TT, P], bf16) for i in range(2)]
        NP = 6
        pr = sb("pr", [P, NP, 512])
        ot = sb("ot", [P, NG, T])
        rec = sb("rec", [P, TT, H])
        on = sb("on", [P, TT, E])
        onT = sb("onT", [P, T])
        stats2 = sb("stats2", [P, TT, 6])
        mv2 = sb("mv2", [P, TT, 2])
        ve2 = sb("ve2", [P, TT])
        rstd2 = sb("rstd2", [P, TT])
        xn2T = sb("xn2T", [P, T])
        rows = [sb(f"rows{i}", [P, TOPK, TT, ROW]) for i in range(2)]
        lg = [sb(f"lg{i}", [P, TT, NE]) for i in range(2)]
        top = sb("top", [P, TOPK, NT])
        r_dif = sb("r_dif", [P, TT, NE])
        r_key = sb("r_key", [P, TT, NE])
        r_kmax = sb("r_kmax", [P, TT])
        r_rest = sb("r_rest", [P, TT, NE])
        chosen = sb("chosen", [P, TOPK, TT, NE])
        both = sb("both", [P, TT, NE], bf16)
        used = sb("used", [P, NE])
        slot_of = sb("slot_of", [P, TT, NE])
        slot_sel = sb("slot_sel", [P, TOPK, TT, NE])
        slot_f = sb("slot_f", [P, TOPK, TT])
        slot_i = [sb(f"slot_i{i}", [P, TOPK, TT], i32) for i in range(2)]
        gate = sb("gate", [P, TOPK, NT])
        gate_t = sb("gate_t", [P, 3, NT])
        pad = sb("pad", [P, NE + SPARE, ROW])
        list0 = sb("list0", [P, NE])
        count = sb("count", [1, NE])
        count_i = sb("count_i", [1, 2, NE], i32)
        tiles_f = sb("tiles_f", [1, NE])
        tiles_end = sb("tiles_end", [1, NE])
        zero_e = sb("zero_e", [1, NE])
        jump = sb("jump", [1, NE])
        tile_no = sb("tile_no", [1, TILES])
        ended = sb("ended", [1, TILES, NE])
        ended_j = sb("ended_j", [1, TILES, NE])
        tab_f = sb("tab_f", [1, 3, TILES])
        tab = sb("tab", [1, 2, TILES], i32)
        pad_at = sb("pad_at", [1, NE], i32)
        NX = 8
        xt = [sb(f"xt{i}", [P, ROW]) for i in range(NX)]
        xtT = [sb(f"xtT{i}", [P, P]) for i in range(2)]
        hid = [sb(f"hid{i}", [P, HID]) for i in range(2)]
        hidT = [sb(f"hidT{i}", [P, HID]) for i in range(2)]
        yt = [sb(f"yt{i}", [P, E]) for i in range(NX)]
        NF = 4
        fin = [sb(f"fin{i}", [P, TOPK, NF, E]) for i in range(4)]

        bank = [ctx.enter_context(nc.psum_tensor(f"bank{i}", [P, 512], fp32)) for i in range(8)]
        SQ, ST, OT, PJ, OC, MISC = bank[0:2], bank[2:4], bank[4], bank[5], bank[6], bank[7]
        mxT_ps = MISC[0:PARTS * HH * TT, 256:320].bitcast(bf16)
        XT_PS, HID_PS, HIDT_PS, Y_PS = bank[0:2], bank[2:4], bank[4:6], bank[6:8]

        s_x = [sem(f"x_chunk{i}") for i in range(3)]
        s_w = sem("weights_loaded")
        s_we = sem("expert_weights_loaded")
        s_bin = sem("bias_in_loaded")
        s_bout = sem("bias_parts_stored")
        s_brow = sem("bias_rows_loaded")
        s_const = sem("constants_made")
        s_bsplit = sem("bias_split_step")
        s_swap = sem("wswap_made")
        s_st1, s_mv1, s_ve1, s_rstd1, s_xn1 = (sem(n) for n in ("stats1_done", "mv1_done", "ve1_done", "rstd1_done", "xn1_done"))
        s_xT_ps, s_xT = sem("xn1T_in_psum"), sem("xn1T_done")
        s_q_ps, s_k_ps, s_v_ps = sem("q_in_psum"), sem("k_in_psum"), sem("v_in_psum")
        s_qrot, s_krot, s_va = sem("q_rotated"), sem("k_rotated"), sem("v_done")
        s_qk, s_hi, s_rest, s_mid, s_lo = (sem(n) for n in ("qk_done", "hi_done", "rest_done", "mid_done", "lo_done"))
        s_pst = [sem(f"parts_stored{i}") for i in range(2)]
        s_ld = [[sem(f"qk_loaded{h}{i}") for i in range(2)] for h in range(2)]
        s_sq, s_mx = sem("sq_in_psum"), sem("max_done")
        s_ms = sem("max_split_step")
        s_mT_ps, s_mT = sem("mxT_in_psum"), sem("mxT_done")
        s_vn = sem("v_copied")
        s_ml = [sem(f"max_rows_loaded{h}") for h in range(2)]
        s_stp, s_exp, s_msk = sem("st_in_psum"), sem("exp_done"), sem("mask_done")
        s_pv, s_ot = sem("pv_done"), sem("ot_done")
        s_oc, s_rec, s_on = sem("o_turned"), sem("reciprocals_done"), sem("on_done")
        s_onT_ps, s_onT, s_y_ps, s_x1 = sem("onT_in_psum"), sem("onT_done"), sem("proj_in_psum"), sem("x1_done")
        s_st2, s_mv2, s_ve2, s_rstd2 = (sem(n) for n in ("stats2_done", "mv2_done", "ve2_done", "rstd2_done"))
        s_row0, s_row1, s_rowno = sem("rows_first_done"), sem("rows_second_done"), sem("row_numbers_done")
        s_x2T_ps, s_x2T, s_lg_ps, s_lg = sem("xn2T_in_psum"), sem("xn2T_done"), sem("logits_in_psum"), sem("logits_done")
        s_rt = sem("route_step")
        s_both, s_rk_ps, s_slot = sem("both_done"), sem("ranks_in_psum"), sem("slots_done")
        s_sc = [sem(f"rows_scattered{i}") for i in range(2)]
        s_used, s_tab, s_tabs = sem("used_step"), sem("table_step"), sem("tables_done")
        s_pad, s_spare = sem("padding_stored"), sem("spare_stored")
        s_g, s_gexp, s_gate = sem("gate_step"), sem("gate_exp_done"), sem("gates_done")
        s_xt = [sem(f"tile_loaded{i}") for i in range(NX)]
        s_tx, s_xtT, s_hp, s_hid = sem("tile_turned"), sem("tileT_done"), sem("hidden_in_psum"), sem("hidden_done")
        s_thp, s_hidT, s_yp, s_yt = sem("hiddenT_in_psum"), sem("hiddenT_done"), sem("y_in_psum"), sem("y_done")
        s_ys = [sem(f"y_scattered{i}") for i in range(NX)]
        s_fl = [sem(f"results_loaded{i}") for i in range(4)]
        s_fs, s_fin, s_out = sem("first_added"), sem("final_done"), sem("out_stored")

        block = ctx.enter_context(nc.Block())

        N_CONST = 14
        N_W = 16 * 5
        x_tiles = x.rearrange("(n p) e -> p n e", p=P)
        out_tiles = out.rearrange("(n p) e -> p n e", p=P)
        LD_DMAS = 2
        ST_DMAS = 1 + PARTS
        NC_FIN = NT // NF

        def j_in(j, ahead, last):
            return j + ahead < last if isinstance(j, int) else True

        def apart(eng, *values):
            held = [v if isinstance(v, int) else eng.compute_val(v) for v in values]
            eng.wait_ge(s_const, N_CONST)
            return held

        @block.sync
        def _(sp):
            sp.dma_start(x_sb[:, 0:TT, :], x_tiles[:, 0:TT, :]).then_inc(s_x[0], 16)
            sp.dma_start(wqkv_sb[:], wqkv.rearrange("p (a e) -> p a e", a=3)).then_inc(s_w, 16)
            sp.dma_start(qkb[:], qk_bias).then_inc(s_w, 16)
            sp.dma_start(rope_sb[:], rope).then_inc(s_w, 16)
            sp.dma_start(x_sb[:, TT:4 * TT, :], x_tiles[:, TT:4 * TT, :]).then_inc(s_x[1], 16)
            sp.dma_start(wproj_sb[:], wproj).then_inc(s_w, 16)
            sp.dma_start(wr_sb[:], wr).then_inc(s_w, 16)
            sp.dma_start(x_sb[:, 4 * TT:NT, :], x_tiles[:, 4 * TT:NT, :]).then_inc(s_x[2], 16)
            sp.wait_ge(s_bsplit, 5)
            sp.dma_start(bias_dram.ap().rearrange("a (p c) -> p a c", p=P), bias_split[:]).then_inc(s_bout, 16)
            sp.wait_ge(s_bout, 16)
            sp.dma_start(bias_rows[:], bias_dram.ap()).then_inc(s_brow, 16)
            sp.dma_start(w1_sb[:], w1.rearrange("e p n -> p e n")).then_inc(s_we, 16)
            sp.dma_start(w2_sb[:], w2.rearrange("e (k p) n -> p e k n", p=P)).then_inc(s_we, 16)

            def load_half(b, half):
                sp.wait_ge(s_pst[b.par], 16 * ST_DMAS * (b.pair + 1))
                heads, at = slice(half * HH, (half + 1) * HH), b.par * PARTS * P * T + half * HH * T
                src = bass.AP(q_dram, at, [[H * T, PARTS * D], [0, PARTS], [1, HH * T]])
                sp.dma_start(qa[b.par][0:QK_ROWS, heads, :], src).then_inc(s_ld[half][b.par], 16)
                src = bass.AP(k_dram, at, [[0, PARTS], [H * T, PARTS * D], [1, HH * T]])
                sp.dma_start(ka[b.par][0:QK_ROWS, heads, :], src).then_inc(s_ld[half][b.par], 16)

            def max_rows(b, half):
                sp.wait_ge(s_mT, 2 * b.n + half + 1)
                dst = qa[b.par][QK_ROWS:QK_ROWS + PARTS, half * HH:(half + 1) * HH, :]
                sp.dma_start(dst.rearrange("a h (t q) -> a (h t) q", t=TT),
                             mxT[half][:]).then_inc(s_ml[half], 16)

            def step(t):
                b3, b2, b1 = t.off(3), t.off(2), t.off(1)
                for half in range(2):
                    if b2.real():
                        if b2.after(2):
                            sp.wait_ge(s_stp, UNITS * t.n + UNITS // 2 * (half + 1))
                        load_half(b2, half)
                    if b1.real():
                        max_rows(b1, half)
                if b3.real():
                    done, read = apart(sp, b3.n + 1, 16 * LD_DMAS * b3.pair)
                    sp.wait_ge(s_lo, done)
                    sp.wait_ge(s_mid, done)
                    if b3.after(2):
                        sp.wait_ge(s_ld[0][b3.par], read)
                        sp.wait_ge(s_ld[1][b3.par], read)
                    sp.dma_start(q_dram.ap()[b3.par].rearrange("a d h t -> (d h) a t"),
                                 split[b3.par][:, 0]).then_inc(s_pst[b3.par], 16)
                    for a in range(PARTS):
                        sp.dma_start(k_dram.ap()[b3.par, :, a], split[b3.par][:, 1, a]).then_inc(s_pst[b3.par], 16)

            run_steps(sp, step)

            sp.wait_ge(s_tabs, 1)
            for e in range(NE):
                at = sp.value_load(pad_at[0:1, e:e + 1], min_val=0, max_val=NE * STRIDE)
                sp.dma_start(lists.ap()[bass.ds(at, P), :], pad[:, e, :]).then_inc(s_pad, 16)
            for i in range(2):
                sp.wait_ge(s_sc[i], 16 * TOPK * TT * (NB // 2))
            sp.wait_ge(s_pad, 16 * NE)
            sp.wait_ge(s_spare, 16)

            for j in range(NX):
                at = sp.value_load(tab[0:1, 1, j:j + 1], min_val=0, max_val=NE * STRIDE + SPARE * P - P)
                sp.dma_start(xt[j][:], lists.ap()[bass.ds(at, P), :]).then_inc(s_xt[j], 16)
            with sp.Fori(1, TILES // NX) as g:
                for i in range(NX):
                    sent, = apart(sp, 16 * g)
                    sp.wait_ge(s_ys[i], sent)
                    at = sp.value_load(tab[0:1, 1, bass.ds(NX * g + i, 1)], min_val=0,
                                       max_val=NE * STRIDE + SPARE * P - P)
                    sp.dma_start(xt[i][:], lists.ap()[bass.ds(at, P), :]).then_inc(s_xt[i], 16)

            for i in range(NX):
                sp.wait_ge(s_ys[i], 16 * (TILES // NX))
            res = results.ap()[0:TOPK * NTOK, :].rearrange("(c n p) e -> p c n e", c=TOPK, p=P)

            def load_results(c):
                for k in range(TOPK):
                    sp.dma_start(fin[c % 4][:, k], res[:, k, c * NF:(c + 1) * NF, :]).then_inc(s_fl[c % 4], 16)

            for c in range(4):
                load_results(c)
            for c in range(NC_FIN):
                sp.wait_ge(s_fin, (c + 1) * NF)
                sp.dma_start(out_tiles[:, c * NF:(c + 1) * NF, :], x_sb[:, c * NF:(c + 1) * NF, :]).then_inc(s_out, 16)
                if c + 4 < NC_FIN:
                    load_results(c + 4)
            sp.wait_ge(s_out, 16 * NC_FIN)

        @block.gpsimd
        def _(pool):
            nc.gpsimd.memset(ident[:], 0.0).then_inc(s_const, 1)
            nc.gpsimd.memset(maskb[:], 0.0).then_inc(s_const, 1)
            nc.gpsimd.memset(beforeb[:], 1.0).then_inc(s_const, 1)
            nc.gpsimd.memset(half_neg[:], -0.5).then_inc(s_const, 1)
            pool.wait_ge(s_const, 4)
            nc.gpsimd.affine_select(out=ident[:], in_=ident[:], compare_op=ALU.not_equal, fill=1.0, base=0,
                                    pattern=[[-1, P]], channel_multiplier=1).then_inc(s_const, 1)
            nc.gpsimd.affine_select(out=maskb[:], in_=maskb[:], compare_op=ALU.is_ge, fill=HIDDEN_MASK, base=0,
                                    pattern=[[-1, P]], channel_multiplier=1).then_inc(s_const, 1)
            nc.gpsimd.affine_select(out=beforeb[:], in_=beforeb[:], compare_op=ALU.is_gt, fill=0.0, base=0,
                                    pattern=[[1, P]], channel_multiplier=-1).then_inc(s_const, 1)
            pool.iota(tile_no[:], pattern=[[1, TILES]], base=0, channel_multiplier=0,
                      allow_small_or_imprecise_dtypes=True).then_inc(s_const, 1)
            pool.iota(list0[:], pattern=[[STRIDE, NE]], base=0, channel_multiplier=0,
                      allow_small_or_imprecise_dtypes=True).then_inc(s_const, 1)
            pool.iota(rank_down[:], pattern=[[0, TT], [-1, NE]], base=NE, channel_multiplier=0,
                      allow_small_or_imprecise_dtypes=True).then_inc(s_const, 1)
            for par in range(2):
                pool.iota(rows[par][:, :, :, E].bitcast(i32), pattern=[[NTOK, TOPK], [P, TT]],
                          base=par * T - 2 * T, channel_multiplier=1).then_inc(s_const, 1)
            pool.iota(pad[:, :, E].bitcast(i32), pattern=[[P, NE + SPARE]], base=TOPK * NTOK,
                      channel_multiplier=1).then_inc(s_const, 1)
            nc.gpsimd.memset(pad[:, :, 0:E], 0.0).then_inc(s_const, 1)
            pool.wait_ge(s_const, N_CONST)
            pool.dma_start(lists.ap()[NE * STRIDE:NE * STRIDE + SPARE * P, :].rearrange("(k p) e -> p k e", p=P),
                           pad[:, NE:NE + SPARE, :]).then_inc(s_spare, 16)

            def scatter(b, c, tile):
                pool.indirect_dma_start(
                    lists.ap(), bass.IndirectOffsetOnAxis(ap=slot_i[b.par][:, c, tile:tile + 1], axis=0),
                    rows[b.par][:, c, tile, :], None).then_inc(s_sc[b.par], 16)

            def step(t):
                b4, b3, bm1, bm2, bm3 = t.off(4), t.off(3), t.off(-1), t.off(-2), t.off(-3)
                for u in range(UNITS):
                    if t.real():
                        done, = apart(pool, UNITS * t.n + u + 1)
                        pool.wait_ge(s_exp, done)
                        if u % 3 == 2:
                            v = pr[:, slot(t, u), :].rearrange("p (h q) -> p h q", h=GROUP)
                        else:
                            v = pr[:, slot(t, u), :].rearrange("p (h q) -> p h q", h=2)[:, :, 0:P]
                        nc.gpsimd.affine_select(out=v, in_=v, compare_op=ALU.is_ge, fill=0.0, base=0,
                                                pattern=[[0, v.shape[1]], [1, P]],
                                                channel_multiplier=-1).then_inc(s_msk, 1)
                    if u == 10 and b3.real():
                        pool.wait_ge(s_mid, b3.n + 1)
                        nc.gpsimd.tensor_tensor(split[b3.par][:, :, 2], qk_rest[:], split[b3.par][:, :, 1],
                                                ALU.subtract).then_inc(s_lo, 1)
                    if u == 7 and b4.real():
                        pool.wait_ge(s_ve1, b4.n + 1)
                        nc.gpsimd.tensor_tensor(rstd1[:], ve1[:], half_neg[:], ALU.pow).then_inc(s_rstd1, 1)
                    if u == 11 and bm1.real():
                        pool.wait_ge(s_ve2, bm1.n + 1)
                        nc.gpsimd.tensor_tensor(rstd2[:], ve2[:], half_neg[:], ALU.pow).then_inc(s_rstd2, 1)
                    if u == 2 and bm2.real():
                        sent, = apart(pool, 16 * TOPK * TT * bm2.pair)
                        if bm2.after(2):
                            pool.wait_ge(s_sc[bm2.par], sent)
                        v = rows[bm2.par][:, :, :, E].bitcast(i32)
                        nc.gpsimd.tensor_scalar(v, v, float(2 * T), None, ALU.add).then_inc(s_rowno, 1)
                    if u in (4, 5, 6, 7) and bm3.real():
                        k = u - 4
                        if k == 0:
                            done, done2 = apart(pool, bm3.n + 1, 2 * (bm3.n + 1))
                            pool.wait_ge(s_slot, done)
                            pool.wait_ge(s_row0, done2)
                            pool.wait_ge(s_row1, done)
                            pool.wait_ge(s_rowno, done)
                        scatter(bm3, k // 2, k % 2)

            def slot(t, u):
                return (UNITS * t.par + u) % NP

            run_steps(pool, step)

            def scatter_y(j, i, g):
                done, loaded = apart(pool, j + 1, 16 * (g + 1))
                pool.wait_ge(s_yt, done)
                pool.wait_ge(s_xt[i], loaded)
                pool.indirect_dma_start(
                    results.ap(), bass.IndirectOffsetOnAxis(ap=xt[i][:, E:E + 1].bitcast(i32), axis=0),
                    yt[i][:], None).then_inc(s_ys[i], 16)

            with pool.Fori(0, TILES // NX) as g:
                for i in range(NX):
                    scatter_y(NX * g + i, i, g)

        @block.scalar
        def _(act):
            act.dma_start(bias_in[:], biases).then_inc(s_bin, 16)

            def step(t):
                b3, b2, b1, bm1, bm2 = t.off(3), t.off(2), t.off(1), t.off(-1), t.off(-2)
                for u in range(UNITS):
                    if t.real():
                        act.wait_ge(s_stp, UNITS * t.n + u + 1)
                        if t.after(1) or u >= NP:
                            act.wait_ge(s_pv, NG * t.n + u // 3 - 1)
                        nc.scalar.activation(pr[:, (UNITS * t.par + u) % NP, :], ST[u % 2][:], ACT.Exp,
                                             scale=SCALE).then_inc(s_exp, 1)
                    if u == 0 and b3.real():
                        act.wait_ge(s_xT_ps, b3.n + 1)
                        nc.scalar.copy(xn1T[b3.par][:], PJ[:, 0:T]).then_inc(s_xT, 1)
                    if u == 6 and b3.real():
                        act.wait_ge(s_qk, b3.n + 1)
                        if b3.after(2):
                            act.wait_ge(s_pst[b3.par], 16 * ST_DMAS * b3.pair)
                        nc.scalar.copy(split[b3.par][:, :, 0], qk[:]).then_inc(s_hi, 1)
                    if u == 9 and b3.real():
                        act.wait_ge(s_rest, b3.n + 1)
                        nc.scalar.copy(split[b3.par][:, :, 1], qk_rest[:]).then_inc(s_mid, 1)
                    if u == 4 and b1.real():
                        act.wait_ge(s_vn, b1.n + 1)
                        if b1.after(2):
                            act.wait_ge(s_pv, NG * (b1.n - 1))
                        nc.scalar.copy(va[b1.par][:, :, :, 0:D],
                                       v_new[:].rearrange("p t (h d) -> p t h d", d=D)).then_inc(s_va, 1)
                    if u == 7 and b2.real():
                        act.wait_ge(s_v_ps, b2.n + 1)
                        if b2.after(1):
                            act.wait_ge(s_va, b2.n)
                        nc.scalar.copy(v_new[:].rearrange("p t e -> p (t e)"), PJ[:, 0:T]).then_inc(s_vn, 1)
                    if u == 6 and b1.real():
                        turn_max(b1, 0)
                    if u == 11 and b1.real():
                        turn_max(b1, 1)
                    if u == 2 and bm1.real():
                        out_pair(bm1, 1)
                    if u == 8 and t.real():
                        out_pair(t, 0)
                    if u == 7 and bm1.real():
                        act.wait_ge(s_onT_ps, bm1.n + 1)
                        nc.scalar.copy(onT[:], OC[:, 0:T]).then_inc(s_onT, 1)
                    if u == 2 and bm2.real():
                        act.wait_ge(s_x2T_ps, bm2.n + 1)
                        nc.scalar.copy(xn2T[:], MISC[:, 0:T]).then_inc(s_x2T, 1)
                    if u == 3 and bm2.real():
                        act.wait_ge(s_row0, 2 * (bm2.n + 1))
                        if bm2.after(2):
                            act.wait_ge(s_sc[bm2.par], 16 * TOPK * TT * bm2.pair)
                        nc.scalar.copy(rows[bm2.par][:, 1, :, 0:E], rows[bm2.par][:, 0, :, 0:E]).then_inc(s_row1, 1)

            def turn_max(b, half):
                act.wait_ge(s_mT_ps, 2 * b.n + half + 1)
                if b.after(1):
                    act.wait_ge(s_ml[half], 16 * b.n)
                nc.scalar.copy(mxT[half][:], mxT_ps).then_inc(s_mT, 1)

            def out_pair(b, k):
                act.wait_ge(s_pv, NG * b.n + 2 * k + 2)
                if b.after(1):
                    act.wait_ge(s_oc, 2 * b.n)
                nc.scalar.copy(ot[:, 2 * k:2 * k + 2, :].rearrange("p g q -> p (g q)"), OT[:]).then_inc(s_ot, 1)

            run_steps(act, step)

            act.wait_ge(s_g, 1)
            nc.scalar.activation(gate_t[:, 1, :], gate_t[:, 0, :], ACT.Exp).then_inc(s_gexp, 1)

            def copy_xT(j, i, first=False):
                act.wait_ge(s_tx, j + 1)
                nc.scalar.copy(xtT[i % 2][:], XT_PS[i % 2][:, 0:P]).then_inc(s_xtT, 1)

            def relu(j, i):
                act.wait_ge(s_hp, j + 1)
                nc.scalar.activation(hid[i % 2][:], HID_PS[i % 2][:], ACT.Relu).then_inc(s_hid, 1)

            def copy_y(j, i, g=None):
                act.wait_ge(s_yp, j + 1)
                if g is not None:
                    act.wait_ge(s_ys[i], 16 * g)
                nc.scalar.copy(yt[i][:], Y_PS[i % 2][:, 0:E]).then_inc(s_yt, 1)

            copy_xT(0, 0)
            copy_xT(1, 1)
            relu(0, 0)

            def tile(j, i, g=None, last=TILES):
                if j_in(j, 2, last):
                    copy_xT(j + 2, i)
                if j_in(j, 1, last):
                    relu(j + 1, i + 1)
                copy_y(j, i, g)

            for j in range(NX):
                tile(j, j)
            with act.Fori(1, TILES // NX - 1) as g:
                for i in range(NX):
                    tile(NX * g + i, i, g)
            for j in range(TILES - NX, TILES):
                tile(j, j % NX, j // NX)

        @block.vector
        def _(dve):
            nc.vector.memset(onesb[:], 1.0).then_inc(s_swap, 1)
            dve.wait_ge(s_const, N_CONST)
            nc.vector.tensor_copy(identb[:], ident[:]).then_inc(s_swap, 1)
            nc.vector.tensor_copy(used[:], list0[:]).then_inc(s_swap, 1)
            nc.vector.memset(zero_e[:], 0.0).then_inc(s_swap, 1)
            for i in range(2):
                nc.vector.memset(ka[i][64:P, :, :], 1.0).then_inc(s_swap, 1)
                nc.vector.memset(qa[i][64:P, :, :], 0.0).then_inc(s_swap, 1)
            for i in range(2):
                nc.vector.memset(va[i][:, :, :, D:VC], 0.0).then_inc(s_swap, 1)
            dve.wait_ge(s_swap, 10)
            for i in range(2):
                nc.vector.memset(va[i][:, :, :, D:D + 1], 1.0).then_inc(s_swap, 1)
            dve.wait_ge(s_w, N_W)
            for a in range(2):
                for z in range(2):
                    nc.vector.tensor_copy(wswap[:, a, :].rearrange("p (i z h) -> p i z h", z=2, h=H)[:, :, z, :],
                                          wqkv_sb[:, a, :].rearrange("p (i z h) -> p i z h", z=2, h=H)[:, :, 1 - z, :]
                                          ).then_inc(s_swap, 1)
            dve.wait_ge(s_bin, 16)
            nc.vector.tensor_copy(bias_split[:, 0], bias_in[:]).then_inc(s_bsplit, 1)
            dve.wait_ge(s_bsplit, 1)
            nc.vector.tensor_tensor(bias_rest[:, 0], bias_in[:], bias_split[:, 0], ALU.subtract).then_inc(s_bsplit, 1)
            dve.wait_ge(s_bsplit, 2)
            nc.vector.tensor_copy(bias_split[:, 1], bias_rest[:, 0]).then_inc(s_bsplit, 1)
            dve.wait_ge(s_bsplit, 3)
            nc.vector.tensor_tensor(bias_rest[:, 1], bias_rest[:, 0], bias_split[:, 1], ALU.subtract).then_inc(s_bsplit, 1)
            dve.wait_ge(s_bsplit, 4)
            nc.vector.tensor_copy(bias_split[:, 2], bias_rest[:, 1]).then_inc(s_bsplit, 1)

            def norm_stats(b, xin, stats, mv, ve, s_stat, s_mv, s_ve):
                for i in range(TT):
                    nc.vector.bn_stats(stats[:, i, :], xin(i)).then_inc(s_stat, 1)
                for i in range(TT):
                    done, = apart(dve, TT * b.n + i + 1)
                    dve.wait_ge(s_stat, done)
                    nc.vector.bn_aggr(mv[:, i, :], stats[:, i, :]).then_inc(s_mv, 1)
                dve.wait_ge(s_mv, TT * (b.n + 1))
                nc.vector.tensor_scalar(ve[:], mv[:, :, 1], EPS, None, ALU.add).then_inc(s_ve, 1)

            def rotate(b, which, s_ps, s_done):
                dve.wait_ge(s_ps, b.n + 1)
                nc.vector.scalar_tensor_tensor(rope_a[:, which], PJ[:, 0:T], qkb[:, which:which + 1],
                                               rope_sb[:, 0], ALU.add, ALU.mult).then_inc(s_done, 1)
                nc.vector.scalar_tensor_tensor(rope_b[:, which], PJ[:, T:2 * T], qkb[:, 2 + which:3 + which],
                                               rope_sb[:, 1], ALU.add, ALU.mult).then_inc(s_done, 1)

            def split_max(b, half, k):
                m = mx[b.par][:, half * HH:(half + 1) * HH, :]
                at = 4 * (2 * b.n + half)
                if k == 0:
                    dve.wait_ge(s_mx, UNITS * b.n + UNITS // 2 * (half + 1))
                    if half or b.after(1):
                        dve.wait_ge(s_mT_ps, 2 * b.n + half)
                    nc.vector.tensor_scalar(mx_split[:, 0], m, -1.0, None, ALU.mult).then_inc(s_ms, 1)
                elif k == 1:
                    dve.wait_ge(s_ms, at + 1)
                    nc.vector.scalar_tensor_tensor(mx_rest[:], m, -1.0, mx_split[:, 0], ALU.mult,
                                                   ALU.subtract).then_inc(s_ms, 1)
                elif k == 2:
                    dve.wait_ge(s_ms, at + 2)
                    nc.vector.tensor_copy(mx_split[:, 1], mx_rest[:]).then_inc(s_ms, 1)
                else:
                    dve.wait_ge(s_ms, at + 3)
                    nc.vector.tensor_tensor(mx_split[:, 2], mx_rest[:], mx_split[:, 1],
                                            ALU.subtract).then_inc(s_ms, 1)

            ROUTE = 13

            def route(b, k):
                at = ROUTE * b.n
                if k > 0:
                    dve.wait_ge(s_rt, at + k)
                lgb = lg[b.par]
                tiles = bass.ds(TT * b.n, TT) if not b.known else slice(TT * b.n, TT * b.n + TT)

                def wide(v):
                    return v.unsqueeze(2).to_broadcast([P, TT, NE])

                if k == 0:
                    dve.wait_ge(s_lg, b.n + 1)
                    ins = nc.vector.tensor_reduce(top[:, 0, tiles], lgb[:], X, ALU.max)
                elif k == 1:
                    ins = nc.vector.tensor_tensor(r_dif[:], lgb[:], wide(top[:, 0, tiles]), ALU.is_ge)
                elif k == 2:
                    ins = nc.vector.tensor_tensor(r_key[:], r_dif[:], rank_down[:], ALU.mult)
                elif k == 3:
                    ins = nc.vector.tensor_reduce(r_kmax[:], r_key[:], X, ALU.max)
                elif k == 4:
                    ins = nc.vector.tensor_tensor(chosen[:, 0], r_key[:], wide(r_kmax[:]), ALU.is_equal)
                elif k == 5:
                    ins = nc.vector.scalar_tensor_tensor(r_rest[:], chosen[:, 0], HIDDEN_MASK, lgb[:],
                                                         ALU.mult, ALU.add)
                elif k == 6:
                    ins = nc.vector.tensor_reduce(top[:, 1, tiles], r_rest[:], X, ALU.max)
                elif k == 7:
                    ins = nc.vector.tensor_tensor(r_dif[:], r_rest[:], wide(top[:, 1, tiles]), ALU.is_ge)
                elif k == 8:
                    ins = nc.vector.tensor_tensor(r_key[:], r_dif[:], rank_down[:], ALU.mult)
                elif k == 9:
                    ins = nc.vector.tensor_reduce(r_kmax[:], r_key[:], X, ALU.max)
                elif k == 10:
                    ins = nc.vector.tensor_tensor(chosen[:, 1], r_key[:], wide(r_kmax[:]), ALU.is_equal)
                elif k == 11:
                    ins = nc.vector.tensor_tensor(both[:], chosen[:, 0], chosen[:, 1], ALU.add)
                elif k == 12:
                    dve.wait_ge(s_rk_ps, b.n + 1)
                    ins = nc.vector.tensor_tensor(slot_of[:], MISC[:, 0:TT * NE].rearrange("p (t e) -> p t e", e=NE),
                                                  used[:].unsqueeze(1).to_broadcast([P, TT, NE]), ALU.add)
                ins.then_inc(s_rt, 1)

            def route_end(b, k):
                at = 3 * b.n
                if k == 0:
                    dve.wait_ge(s_rt, ROUTE * (b.n + 1))
                    nc.vector.tensor_tensor(used[:], used[:], MISC[:, TT * NE:(TT + 1) * NE],
                                            ALU.add).then_inc(s_used, 1)
                    nc.vector.tensor_tensor(slot_sel[:], chosen[:], slot_of[:].unsqueeze(1).to_broadcast([P, TOPK, TT, NE]),
                                            ALU.mult).then_inc(s_used, 1)
                elif k == 1:
                    dve.wait_ge(s_used, at + 2)
                    nc.vector.tensor_reduce(slot_f[:], slot_sel[:], X, ALU.add).then_inc(s_used, 1)
                else:
                    dve.wait_ge(s_used, at + 3)
                    nc.vector.tensor_copy(slot_i[b.par][:], slot_f[:]).then_inc(s_slot, 1)

            def tiles_of(b, i):
                return TT * b.n + i

            def xrow(b, i):
                if b.known:
                    return x_sb[:, TT * b.n + i, :]
                return x_sb[:, bass.ds(TT * b.n + i, 1), :].rearrange("p a e -> p (a e)")

            def row_max(b, v):
                dve.wait_ge(s_sq, UNITS * b.n + v + 1)
                g = v // 3
                if v % 3 == 2:
                    src = SQ[v % 2][:].rearrange("p (h k) -> p h k", h=GROUP)
                    dst = mx[b.par][:, GROUP * g:GROUP * g + GROUP, 0]
                else:
                    h0 = GROUP * g + 2 * (v % 3)
                    src = SQ[v % 2][:].rearrange("p (h k) -> p h k", h=2)
                    dst = mx[b.par][:, h0:h0 + 2, 1]
                nc.vector.tensor_reduce(dst, src, X, ALU.max).then_inc(s_mx, 1)

            def step(t):
                b4, b3, b2, b1 = t.off(4), t.off(3), t.off(2), t.off(1)
                bm1, bm2, bm3 = t.off(-1), t.off(-2), t.off(-3)
                for u in range(UNITS):
                    bm, v = (b1, u + LEAD) if u + LEAD < UNITS else (b2, u + LEAD - UNITS)
                    if bm.real():
                        row_max(bm, v)
                    if u == 0 and bm2.real():
                        dve.wait_ge(s_rstd2, bm2.n + 1)
                        if bm2.after(2):
                            dve.wait_ge(s_sc[bm2.par], 16 * TOPK * TT * bm2.pair)
                        for i in range(TT):
                            nc.vector.tensor_scalar(rows[bm2.par][:, 0, i, 0:E], xrow(bm2, i), mv2[:, i, 0:1],
                                                    rstd2[:, i:i + 1], ALU.subtract, ALU.mult).then_inc(s_row0, 1)
                    if bm3.real():
                        if u == 1:
                            route(bm3, 12)
                            route_end(bm3, 0)
                        if u == 2:
                            route_end(bm3, 1)
                        if u == 3:
                            if bm3.after(2):
                                dve.wait_ge(s_sc[bm3.par], 16 * TOPK * TT * bm3.pair)
                            route_end(bm3, 2)
                    if u in (3, 4) and b1.real():
                        split_max(b1, 0, 2 * (u - 3))
                        split_max(b1, 0, 2 * (u - 3) + 1)
                    if u in (9, 10) and b1.real():
                        split_max(b1, 1, 2 * (u - 9))
                        split_max(b1, 1, 2 * (u - 9) + 1)
                    if u == 2 and b3.real():
                        rotate(b3, 0, s_q_ps, s_qrot)
                    if u == 4 and b3.real():
                        rotate(b3, 1, s_k_ps, s_krot)
                    if u in (3, 5) and bm1.real():
                        qt = (u - 3) // 2
                        dve.wait_ge(s_oc, 2 * bm1.n + qt + 1)
                        o4 = OC[:].rearrange("p (h c) -> p h c", c=VC)
                        nc.vector.reciprocal(rec[:, qt, :], o4[:, :, D]).then_inc(s_rec, 1)
                        dve.wait_ge(s_rec, 2 * bm1.n + qt + 1)
                        nc.vector.tensor_tensor(on[:, qt, :].rearrange("p (h d) -> p h d", d=D), o4[:, :, 0:D],
                                                rec[:, qt, :].unsqueeze(2).to_broadcast([P, H, D]),
                                                ALU.mult).then_inc(s_on, 1)
                    if u == 5 and b3.real():
                        dve.wait_ge(s_krot, 2 * (b3.n + 1))
                        if b3.after(1):
                            dve.wait_ge(s_rest, b3.n)
                            dve.wait_ge(s_hi, b3.n)
                        nc.vector.tensor_tensor(qk[:], rope_a[:], rope_b[:], ALU.add).then_inc(s_qk, 1)
                    if u == 5 and bm2.real():
                        dve.wait_ge(s_lg_ps, bm2.n + 1)
                        nc.vector.tensor_copy(lg[bm2.par][:],
                                              MISC[:, 0:TT * NE].rearrange("p (t e) -> p t e", e=NE)).then_inc(s_lg, 1)
                    if u >= 6 and bm2.real():
                        for k in (2 * (u - 6), 2 * (u - 6) + 1):
                            if k == 11 and bm2.after(1):
                                dve.wait_ge(s_rk_ps, bm2.n)
                            route(bm2, k)
                    if u == 6 and b4.real():
                        if b4.known and b4.n in (0, 1, 4):
                            dve.wait_ge(s_x[{0: 0, 1: 1, 4: 2}[b4.n]], 16)
                        norm_stats(b4, lambda i: xrow(b4, i), stats1, mv1, ve1, s_st1, s_mv1, s_ve1)
                    if u == 8 and b3.real():
                        dve.wait_ge(s_hi, b3.n + 1)
                        if b3.after(1):
                            dve.wait_ge(s_lo, b3.n)
                            dve.wait_ge(s_mid, b3.n)
                        nc.vector.tensor_tensor(qk_rest[:], qk[:], split[b3.par][:, :, 0],
                                                ALU.subtract).then_inc(s_rest, 1)
                    if u == 10 and bm1.real():
                        dve.wait_ge(s_y_ps, bm1.n + 1)
                        xr = (x_sb[:, TT * bm1.n:TT * (bm1.n + 1), :] if bm1.known
                              else x_sb[:, bass.ds(TT * bm1.n, TT), :])
                        nc.vector.tensor_tensor(xr, OC[:, 0:T].rearrange("p (t e) -> p t e", t=TT), xr,
                                                ALU.add).then_inc(s_x1, 1)
                    if u == 10 and b4.real():
                        dve.wait_ge(s_rstd1, b4.n + 1)
                        if b4.after(1):
                            dve.wait_ge(s_xT_ps, b4.n)
                        for i in range(TT):
                            nc.vector.tensor_scalar(xn1[:, i, :], xrow(b4, i), mv1[:, i, 0:1], rstd1[:, i:i + 1],
                                                    ALU.subtract, ALU.mult).then_inc(s_xn1, 1)
                    if u == 10 and bm1.real():
                        done, = apart(dve, bm1.n + 1)
                        dve.wait_ge(s_x1, done)
                        norm_stats(bm1, lambda i: xrow(bm1, i), stats2, mv2, ve2, s_st2, s_mv2, s_ve2)

            run_steps(dve, step)

            chain = [0]

            def then(ins):
                chain[0] += 1
                ins.then_inc(s_tab, 1)
                dve.wait_ge(s_tab, chain[0])

            dve.wait_ge(s_used, 3 * NB)
            then(nc.vector.tensor_copy(pad_at[:], used[0:1, :]))
            then(nc.vector.tensor_tensor(count[:], used[0:1, :], list0[0:1, :], ALU.subtract))
            then(nc.vector.tensor_scalar(count_i[:, 0], count[:], float(P - 1), None, ALU.add))
            then(nc.vector.tensor_scalar(count_i[:, 1], count_i[:, 0], P.bit_length() - 1, None,
                                         ALU.arith_shift_right))
            then(nc.vector.tensor_copy(tiles_f[:], count_i[:, 1]))
            then(nc.vector.tensor_tensor_scan(tiles_end[:], tiles_f[:], zero_e[:], 0.0, ALU.add, ALU.add))
            then(nc.vector.tensor_scalar(jump[:], tiles_f[:], float(-P), float(STRIDE), ALU.mult, ALU.add))
            then(nc.vector.tensor_tensor(ended[:], tile_no[:].unsqueeze(2).to_broadcast([1, TILES, NE]),
                                         tiles_end[:].unsqueeze(1).to_broadcast([1, TILES, NE]), ALU.is_ge))
            then(nc.vector.tensor_reduce(tab_f[:, 0], ended[:], X, ALU.add))
            then(nc.vector.tensor_tensor(ended_j[:], ended[:], jump[:].unsqueeze(1).to_broadcast([1, TILES, NE]), ALU.mult))
            then(nc.vector.tensor_reduce(tab_f[:, 1], ended_j[:], X, ALU.add))
            then(nc.vector.scalar_tensor_tensor(tab_f[:, 2], tile_no[:], float(P), tab_f[:, 1], ALU.mult, ALU.add))
            then(nc.vector.tensor_scalar(tab[:, 0], tab_f[:, 0], float(NE - 1), None, ALU.min))
            nc.vector.tensor_copy(tab[:, 1], tab_f[:, 2]).then_inc(s_tabs, 1)
            nc.vector.tensor_tensor(gate_t[:, 0], top[:, 1], top[:, 0], ALU.subtract).then_inc(s_g, 1)
            dve.wait_ge(s_gexp, 1)
            nc.vector.tensor_scalar(gate_t[:, 2], gate_t[:, 1], 1.0, None, ALU.add).then_inc(s_g, 1)
            dve.wait_ge(s_g, 2)
            nc.vector.reciprocal(gate[:, 0], gate_t[:, 2]).then_inc(s_g, 1)
            dve.wait_ge(s_g, 3)
            nc.vector.tensor_tensor(gate[:, 1], gate_t[:, 1], gate[:, 0], ALU.mult).then_inc(s_gate, 1)

            def copy_hT(j, i):
                dve.wait_ge(s_thp, j + 1)
                nc.vector.tensor_copy(hidT[i % 2][:], HIDT_PS[i % 2][:]).then_inc(s_hidT, 1)

            with dve.Fori(0, TILES // 2) as g:
                for i in range(2):
                    copy_hT(2 * g + i, i)

            dve.wait_ge(s_gate, 1)
            for c in range(NC_FIN):
                dve.wait_ge(s_fl[c % 4], 16 * TOPK * (c // 4 + 1))
                for i in range(NF):
                    n = c * NF + i
                    nc.vector.scalar_tensor_tensor(fin[c % 4][:, 0, i], fin[c % 4][:, 0, i], gate[:, 0, n:n + 1],
                                                   x_sb[:, n, :], ALU.mult, ALU.add).then_inc(s_fs, 1)
                for i in range(NF):
                    n = c * NF + i
                    dve.wait_ge(s_fs, n + 1)
                    nc.vector.scalar_tensor_tensor(x_sb[:, n, :], fin[c % 4][:, 1, i], gate[:, 1, n:n + 1],
                                                   fin[c % 4][:, 0, i], ALU.mult, ALU.add).then_inc(s_fin, 1)

        @block.tensor
        def _(pe):
            pe.wait_ge(s_const, N_CONST)
            pe.wait_ge(s_w, N_W)
            pe.wait_ge(s_swap, 16)

            def add_bias(dst, at, n, stop=True):
                return nc.tensor.matmul(dst, onesb[0:PARTS, 0:dst.shape[0]], bias_rows[:, at:at + n],
                                        start=False, stop=stop, skip_group_check=True)

            def max_unit(b, u):
                n = UNITS * b.n + u
                g, dst = u // 3, SQ[u % 2]
                if b.after(1) or u >= 2:
                    pe.wait_ge(s_mx, n - 1)
                if u % 6 == 0:
                    pe.wait_ge(s_ld[u // 6][b.par], 16 * LD_DMAS * (b.pair + 1))
                q, k = qa[b.par], ka[b.par]
                if u % 3 == 2:
                    for j in range(GROUP):
                        h = GROUP * g + j
                        nc.tensor.matmul(dst[:, j * P:(j + 1) * P], q[0:QK_ROWS, h, 0:P], k[0:QK_ROWS, h, 0:P],
                                         start=(j == 0), stop=False, skip_group_check=True)
                    nc.tensor.matmul(dst[:].rearrange("p (h k) -> p h k", h=GROUP), identb[:],
                                     maskb[:].unsqueeze(1).to_broadcast([P, GROUP, P]), start=False, stop=True,
                                     skip_group_check=True).then_inc(s_sq, 1)
                else:
                    for j in range(2):
                        h = GROUP * g + 2 * (u % 3) + j
                        nc.tensor.matmul(dst[:, j * T:(j + 1) * T], q[0:QK_ROWS, h, P:T], k[0:QK_ROWS, h, :],
                                         start=(j == 0), stop=False, skip_group_check=True)
                    nc.tensor.matmul(dst[:].rearrange("p (h k) -> p h k", h=2)[:, :, P:T], identb[:],
                                     maskb[:].unsqueeze(1).to_broadcast([P, 2, P]), start=False, stop=True,
                                     skip_group_check=True).then_inc(s_sq, 1)

            def exp_unit(b, u):
                n = UNITS * b.n + u
                g, dst = u // 3, ST[u % 2]
                if b.after(1) or u >= 2:
                    pe.wait_ge(s_exp, n - 1)
                if u % 6 == 0:
                    pe.wait_ge(s_ml[u // 6], 16 * (b.n + 1))
                q, k = qa[b.par], ka[b.par]
                if u % 3 == 2:
                    for j in range(GROUP):
                        h = GROUP * g + j
                        last = nc.tensor.matmul(dst[:, j * P:(j + 1) * P], k[:, h, P:T], q[:, h, P:T],
                                                start=True, stop=True)
                else:
                    for j in range(2):
                        h = GROUP * g + 2 * (u % 3) + j
                        last = nc.tensor.matmul(dst[:, j * T:(j + 1) * T], k[:, h, 0:P], q[:, h, :],
                                                start=True, stop=True)
                last.then_inc(s_stp, 1)

            def times_v(b, g):
                pe.wait_ge(s_msk, UNITS * b.n + 3 * g + 3)
                if g == 0:
                    pe.wait_ge(s_va, b.n + 1)
                if g % 2 == 0 and (g or b.after(1)):
                    pe.wait_ge(s_ot, 2 * b.n + g // 2)
                s0 = UNITS * b.par + 3 * g
                dst = OT[:, (g % 2) * T:(g % 2 + 1) * T]
                for j in range(GROUP):
                    p = pr[:, (s0 + j // 2) % NP, :].rearrange("p (h q) -> p h q", h=2)[:, j % 2, :]
                    nc.tensor.matmul(dst[32 * j:32 * j + VC, :], va[b.par][:, 0, GROUP * g + j, :], p,
                                     start=True, stop=False, skip_group_check=True)
                for j in range(GROUP):
                    p = pr[:, (s0 + 2) % NP, j * P:(j + 1) * P]
                    last = nc.tensor.matmul(dst[32 * j:32 * j + VC, P:T], va[b.par][:, 1, GROUP * g + j, :], p,
                                            start=False, stop=True, skip_group_check=True)
                last.then_inc(s_pv, 1)

            def turn_max(b, half):
                split_done, copied, routed = apart(pe, 4 * (2 * b.n + half) + 4, 2 * b.n + half, b.n - 2)
                pe.wait_ge(s_ms, split_done)
                if half or b.after(1):
                    pe.wait_ge(s_mT, copied)
                if half == 0 and b.after(3):
                    pe.wait_ge(s_lg, routed)
                nc.tensor.transpose(mxT_ps, mx_split[:].rearrange("p a h t -> p (a h t)"),
                                    identb[:]).then_inc(s_mT_ps, 1)

            def project(b, u):
                if u == 0:
                    pe.wait_ge(s_xn1, TT * (b.n + 1))
                    if b.after(1):
                        pe.wait_ge(s_krot, 2 * b.n)
                    if b.after(2):
                        pe.wait_ge(s_vn, b.n - 1)
                    for i in range(TT):
                        last = nc.tensor.transpose(PJ[:, i * P:(i + 1) * P], xn1[:, i, :], ident[:])
                    last.then_inc(s_xT_ps, 1)
                elif u == 2:
                    pe.wait_ge(s_xT, b.n + 1)
                    nc.tensor.matmul(PJ[:, 0:T], wqkv_sb[:, 0, :], xn1T[b.par][:], start=True, stop=True)
                    nc.tensor.matmul(PJ[:, T:2 * T], wswap[:, 0, :], xn1T[b.par][:], start=True, stop=True).then_inc(s_q_ps, 1)
                elif u == 4:
                    pe.wait_ge(s_qrot, 2 * (b.n + 1))
                    nc.tensor.matmul(PJ[:, 0:T], wqkv_sb[:, 1, :], xn1T[b.par][:], start=True, stop=True)
                    nc.tensor.matmul(PJ[:, T:2 * T], wswap[:, 1, :], xn1T[b.par][:], start=True, stop=True).then_inc(s_k_ps, 1)

            def project_v(b):
                if b.off(1).real():
                    pe.wait_ge(s_krot, 2 * (b.n + 2))
                if b.after(1):
                    pe.wait_ge(s_vn, b.n)
                if b.known and b.n == 0:
                    pe.wait_ge(s_brow, 16)
                for i in range(TT):
                    nc.tensor.matmul(PJ[:, i * P:(i + 1) * P], xn1T[b.par][:, i * P:(i + 1) * P], wqkv_sb[:, 2, :],
                                     start=(i == 0), stop=False, skip_group_check=True)
                    last = add_bias(PJ[:, i * P:(i + 1) * P], BV_AT, E)
                last.then_inc(s_v_ps, 1)

            def finish(b, u):
                if u in (3, 5):
                    qt = (u - 3) // 2
                    pe.wait_ge(s_ot, 2 * (b.n + 1))
                    if qt == 1:
                        pe.wait_ge(s_on, 2 * b.n + 1)
                    elif b.after(1):
                        pe.wait_ge(s_x1, b.n)
                    for g in range(NG):
                        last = nc.tensor.transpose(OC[:, g * P:(g + 1) * P], ot[:, g, qt * P:(qt + 1) * P], ident[:])
                    last.then_inc(s_oc, 1)
                elif u == 7:
                    pe.wait_ge(s_on, 2 * (b.n + 1))
                    for i in range(TT):
                        last = nc.tensor.transpose(OC[:, i * P:(i + 1) * P], on[:, i, :], ident[:])
                    last.then_inc(s_onT_ps, 1)
                elif u == 9:
                    pe.wait_ge(s_onT, b.n + 1)
                    for i in range(TT):
                        nc.tensor.matmul(OC[:, i * P:(i + 1) * P], onT[:, i * P:(i + 1) * P], wproj_sb[:],
                                         start=(i == 0), stop=False, skip_group_check=True)
                        last = add_bias(OC[:, i * P:(i + 1) * P], BP_AT, E)
                    last.then_inc(s_y_ps, 1)

            def logits(b, u):
                if u == 2:
                    pe.wait_ge(s_row0, TT * (b.n + 1))
                    if b.after(1):
                        pe.wait_ge(s_used, 3 * b.n - 2)
                    if b.known:
                        pe.wait_ge(s_mT, min(2 * b.n + 6, 2 * NB))
                    for i in range(TT):
                        last = nc.tensor.transpose(MISC[:, i * P:(i + 1) * P], rows[b.par][:, 0, i, 0:E], ident[:])
                    last.then_inc(s_x2T_ps, 1)
                elif u == 4:
                    pe.wait_ge(s_x2T, b.n + 1)
                    for i in range(TT):
                        nc.tensor.matmul(MISC[:, i * NE:(i + 1) * NE], xn2T[:, i * P:(i + 1) * P], wr_sb[:],
                                         start=(i == 0), stop=False, skip_group_check=True)
                        last = add_bias(MISC[:, i * NE:(i + 1) * NE], BR_AT, NE)
                    last.then_inc(s_lg_ps, 1)

            def ranks(b):
                pe.wait_ge(s_rt, ROUTE * b.n + 12)
                pe.wait_ge(s_lg, min(b.n + 1, NB) if b.known else b.n + 1)
                pe.wait_ge(s_mT, min(2 * b.n + 8, 2 * NB) if b.known else 2 * b.n + 8)
                r = MISC[:, 0:(TT + 1) * NE]
                m = both[:].rearrange("p t e -> p (t e)")
                nc.tensor.matmul(r[:, 0:TT * NE], beforeb[:], m, start=True, stop=False, skip_group_check=True)
                for i in range(TT):
                    last = nc.tensor.matmul(r[:, (i + 1) * NE:(TT + 1) * NE], onesb[:], m[:, 0:(TT - i) * NE],
                                            start=False, stop=(i == TT - 1), skip_group_check=True)
                last.then_inc(s_rk_ps, 1)

            ROUTE = 13

            def step(t):
                b3, b2, b1 = t.off(3), t.off(2), t.off(1)
                bm1, bm2, bm3 = t.off(-1), t.off(-2), t.off(-3)
                for u in range(UNITS):
                    bm, v = (b1, u + LEAD) if u + LEAD < UNITS else (b2, u + LEAD - UNITS)
                    if bm.real():
                        max_unit(bm, v)
                    if t.real():
                        exp_unit(t, u)
                    if u == 0 and bm3.real():
                        ranks(bm3)
                    if u in (0, 2, 4) and b3.real():
                        project(b3, u)
                    if u == 1 and bm1.real():
                        times_v(bm1, NG - 1)
                    if u in (2, 4) and bm2.real():
                        logits(bm2, u)
                    if u == 6 and b2.real():
                        project_v(b2)
                    if u in (4, 7, 10) and t.real():
                        times_v(t, (u - 4) // 3)
                    if u == 6 and b1.real():
                        turn_max(b1, 0)
                    if u == 11 and b1.real():
                        turn_max(b1, 1)
                    if bm1.real():
                        finish(bm1, u)

            run_steps(pe, step)

            pe.wait_ge(s_tabs, 1)
            pe.wait_ge(s_we, 32)

            def turn_tile(j, i, g):
                pe.wait_ge(s_xt[i % NX], 16 * (g + 1))
                if j_in_loop(j, 2):
                    pe.wait_ge(s_xtT, j - 1)
                nc.tensor.transpose(XT_PS[i % 2][:, 0:P], xt[i % NX][:, 0:E], ident[:]).then_inc(s_tx, 1)

            def hidden(j, i):
                e = pe.value_load(tab[0:1, 0, bass.ds(j, 1)], min_val=0, max_val=NE - 1)
                pe.wait_ge(s_xtT, j + 1)
                if j_in_loop(j, 2):
                    pe.wait_ge(s_hid, j - 1)
                dst = HID_PS[i % 2][:]
                nc.tensor.matmul(dst, xtT[i % 2][:], w1_sb[:, bass.ds(e, 1), :].rearrange("p a n -> p (a n)"),
                                 start=True, stop=False)
                nc.tensor.matmul(dst, onesb[0:PARTS, :], bias_rows[:, bass.ds(e * HID + B1_AT, HID)],
                                 start=False, stop=True).then_inc(s_hp, 1)
                return e

            def turn_hidden(j, i):
                pe.wait_ge(s_hid, j + 1)
                if j_in_loop(j, 2):
                    pe.wait_ge(s_hidT, j - 1)
                for k in range(KT):
                    last = nc.tensor.transpose(HIDT_PS[i % 2][:, k * P:(k + 1) * P],
                                               hid[i % 2][:, k * P:(k + 1) * P], ident[:])
                last.then_inc(s_thp, 1)

            def second(j, i):
                e = pe.value_load(tab[0:1, 0, bass.ds(j, 1)], min_val=0, max_val=NE - 1)
                pe.wait_ge(s_hidT, j + 1)
                if j_in_loop(j, 2):
                    pe.wait_ge(s_yt, j - 1)
                dst = Y_PS[i % 2][:, 0:E]
                for k in range(KT):
                    nc.tensor.matmul(dst, hidT[i % 2][:, k * P:(k + 1) * P],
                                     w2_sb[:, bass.ds(e, 1), k, :].rearrange("p a n -> p (a n)"),
                                     start=(k == 0), stop=False)
                nc.tensor.matmul(dst, onesb[0:PARTS, :], bias_rows[:, bass.ds(e * E + B2_AT, E)],
                                 start=False, stop=True).then_inc(s_yp, 1)

            def j_in_loop(j, n):
                return j >= n if isinstance(j, int) else True

            def tile(j, i, g, last=TILES):
                if j_in(j, 2, last):
                    turn_tile(j + 2, i + 2, g + (i + 2) // NX)
                turn_hidden(j, i)
                if j_in(j, 1, last):
                    hidden(j + 1, i + 1)
                second(j, i)

            turn_tile(0, 0, 0)
            turn_tile(1, 1, 0)
            hidden(0, 0)
            for j in range(NX):
                tile(j, j, 0)
            with pe.Fori(1, TILES // NX - 1) as g:
                for i in range(NX):
                    tile(NX * g + i, i, g)
            for j in range(TILES - NX, TILES):
                tile(j, j % NX, j // NX)


def rope_table():
    pos = np.arange(T, dtype=np.float32)
    inv = (1.0 / np.float32(10000.0) ** (np.arange(0, D, 2, dtype=np.float32) / np.float32(D))).astype(np.float32)
    ang = pos[:, None] * inv[None, :]
    w = np.arange(P) // H
    c = np.cos(ang).astype(np.float32)[:, w // 2].T
    s = np.sin(ang).astype(np.float32)[:, w // 2].T * np.where(w % 2, 1, -1).astype(np.float32)[:, None]
    return np.ascontiguousarray(np.stack([c, s], axis=1).astype(np.float32))


def kernel(**inputs):
    import numpy as _np
    import concourse.bacc as _bacc
    from concourse import mybir as _mybir
    from concourse.bass_utils import run_bass_kernel_spmd as _run

    a = {k: _np.asarray(v) for k, v in inputs.items()}
    order = _np.arange(P).reshape(H, D).T.reshape(-1)
    swapped = order.reshape(D // 2, 2, H)[:, ::-1].reshape(-1)
    cols = _np.concatenate([order, P + order, 2 * P + _np.arange(P)])
    bqkv = a["L0_attn_bqkv"]
    bias = _np.concatenate([a["L0_ffn_b1"].reshape(-1), a["L0_ffn_b2"].reshape(-1), a["L0_attn_bproj"],
                            bqkv[2 * P:], a["L0_ffn_br"]])
    bias = _np.concatenate([bias, _np.zeros(NBIAS - bias.size, bias.dtype)])
    arrays = {
        "x": a["L0_attn_x"].reshape(NTOK, E),
        "wqkv": a["L0_attn_Wqkv"][:, cols],
        "qk_bias": _np.stack([bqkv[order], bqkv[P + order], bqkv[swapped], bqkv[P + swapped]], axis=1),
        "wproj": a["L0_attn_Wproj"],
        "w1": a["L0_ffn_W1"],
        "w2": a["L0_ffn_W2"],
        "wr": a["L0_ffn_Wr"],
        "biases": bias.reshape(P, BIAS_COLS),
        "rope": rope_table(),
    }
    arrays = {k: _np.ascontiguousarray(v) for k, v in arrays.items()}
    nc = _bacc.Bacc("TRN2", target_bir_lowering=False, num_devices=1)
    args = [nc.dram_tensor(k, v.shape, _mybir.dt.from_np(v.dtype), kind="ExternalInput").ap()
            for k, v in arrays.items()]
    y = nc.dram_tensor("y", (NTOK, E), fp32, kind="ExternalOutput").ap()
    layer(nc, *args, y)
    r = _run(nc, [arrays], core_ids=[0])
    return r.results[0]["y"].reshape(NB, T, E)
```

```python
import numpy as np
import concourse.bass as bass
from concourse import mybir
from contextlib import ExitStack

fp32 = mybir.dt.float32
bf16 = mybir.dt.bfloat16
i32 = mybir.dt.int32
ALU = mybir.AluOpType
ACT = mybir.ActivationFunctionType
X = mybir.AxisListType.X

NB, T, E = 16, 256, 128
H, D = 16, 8
NE, HID, TOPK = 8, 512, 2
P = 128
TT = T // P
NT = NB * TT
NTOK = NB * T
EPS = 1e-5
SCALE = D ** -0.5
HIDDEN_MASK = -3.0e38

PARTS = 3
TERMS = PARTS * PARTS
QK_ROWS = TERMS * D
HH = H // 2
GROUP = 4
NG = H // GROUP
UNITS = 3 * NG
VC = 32

STRIDE = NTOK + P
TILES = NTOK * TOPK // P + NE
EARLY = 24
EARLY_FROM = NB - 4
assert EARLY_FROM * T * TOPK - NE * (P - 1) >= EARLY * P
SPARE = NE
ROW = E + 1
KT = HID // P
B2_AT = 0
BP_AT = B2_AT + NE * E
BV_AT = BP_AT + E
BR_AT = BV_AT + E
BIAS_COLS = -(-(BR_AT + NE) // P)
NBIAS = P * BIAS_COLS


class Batch:

    def __init__(self, pair, par):
        self.pair, self.par, self.n = pair, par, 2 * pair + par
        self.known = isinstance(pair, int)

    def off(self, d):
        return Batch(self.pair + (self.par + d) // 2, (self.par + d) % 2)

    def real(self):
        return 0 <= self.n < NB if self.known else True

    def after(self, n):
        return self.n >= n if self.known else True


FIRST_STEP, LOOP_FROM, LOOP_PAIRS, LAST_STEP = -4, 5, 3, NB + 3
EARLY_AT = [(NB, u) for u in (3, 5, 7, 9, 10)] + [(NB + 1, u) for u in (1, 4, 6, 8, 10)] \
    + [(NB + 2, u) for u in (0, 1)] + 12 * [(NB + 2, UNITS - 1)]
TABLE_AT = (NB - 1, 0)
WEIGHTS_AT = [(NB - 1, u) for u in (4, 6, 8)]
SCATTER_AT = (7, 8, 9, 11)
LATE_TABLE_AT = (NB + 2, 8)
REST_OF_TABLE_AFTER = EARLY_AT.index((NB + 2, UNITS - 1)) + 3
LEAD = 2


TWO_ONES = float(np.array([0x3F803F80], np.uint32).view(np.float32)[0])


def run_steps(eng, step):
    for t in range(FIRST_STEP, LOOP_FROM):
        step(Batch(t // 2, t % 2))
    with eng.Fori(LOOP_FROM // 2, LOOP_FROM // 2 + LOOP_PAIRS) as pair:
        step(Batch(pair, 1))
        step(Batch(pair + 1, 0))
    for t in range(LOOP_FROM + 2 * LOOP_PAIRS, LAST_STEP):
        step(Batch(t // 2, t % 2))


def layer(nc, x, wqkv, qk_bias, wproj, w1, b1_cols, w2, wr, biases, rope, out):
    ctx = ExitStack()
    with ctx:
        def sb(name, shape, dt=fp32):
            return ctx.enter_context(nc.sbuf_tensor(name, shape, dt))

        def sem(name):
            return ctx.enter_context(nc.semaphore(name))

        q_dram = nc.dram_tensor("q_dram", [2, PARTS, D, H, T], bf16)
        k_dram = nc.dram_tensor("k_dram", [2, D, PARTS, H, T], bf16)
        bias_dram = nc.dram_tensor("bias_dram", [PARTS, NBIAS], bf16)
        lists = nc.dram_tensor("lists", [NE * STRIDE + SPARE * P, ROW], fp32)
        results = nc.dram_tensor("results", [TOPK * NTOK + (NE + SPARE) * P, E], fp32)

        x_sb = sb("x_sb", [P, NT, E])
        wqkv_sb = sb("wqkv_sb", [P, 3, E])
        wproj_sb = sb("wproj_sb", [P, E])
        wr_sb = sb("wr_sb", [P, NE])
        w1_sb = sb("w1_sb", [P, NE, HID + KT])
        w2_sb = sb("w2_sb", [P, NE, KT, E])
        qkb = sb("qkb", [P, 2])
        rope_sb = sb("rope_sb", [P, 2, 2, T])
        bias_in = sb("bias_in", [P, BIAS_COLS])
        bias_rest = sb("bias_rest", [P, 2, BIAS_COLS])
        bias_split = sb("bias_split", [P, PARTS, BIAS_COLS], bf16)
        bias_rows = sb("bias_rows", [PARTS, NBIAS], bf16)
        ident = sb("ident", [P, P])
        identb = sb("identb", [P, P], bf16)
        maskb = sb("maskb", [P, P], bf16)
        beforeb = sb("beforeb", [P, P], bf16)
        onesb = sb("onesb", [P, P], bf16)
        half_neg = sb("half_neg", [P, TT])
        rank_down = sb("rank_down", [P, TT, NE])
        stats1 = sb("stats1", [P, TT, 6])
        mv1 = sb("mv1", [P, TT, 2])
        ve1 = sb("ve1", [P, TT])
        rstd1 = sb("rstd1", [P, TT])
        neg_mean1 = sb("neg_mean1", [P, TT])
        xc1 = sb("xc1", [P, TT, E])
        xn1 = sb("xn1", [P, TT, E])
        xn1T = [sb(f"xn1T{i}", [P, T]) for i in range(2)]
        rope_a = sb("rope_a", [P, 2, T])
        rope_b = sb("rope_b", [P, 2, T])
        qk = sb("qk", [P, 2, T])
        qk_rest = sb("qk_rest", [P, 2, T])
        split = [sb(f"split{i}", [P, PARTS, 2, T], bf16) for i in range(2)]
        qa = [sb(f"qa{i}", [P, H, T], bf16) for i in range(2)]
        ka = [sb(f"ka{i}", [P, H, T], bf16) for i in range(2)]
        v_new = sb("v_new", [P, TT, E])
        va = [sb(f"va{i}", [P, TT, H, VC]) for i in range(2)]
        mx = [sb(f"mx{i}", [P, H, TT]) for i in range(2)]
        mx_rest = sb("mx_rest", [P, HH, TT])
        mx_split = sb("mx_split", [P, PARTS, HH, TT], bf16)
        mxT = [sb(f"mxT{i}", [PARTS * HH * TT, P], bf16) for i in range(2)]
        NP = 6
        pr = sb("pr", [P, NP, 512])
        ot = sb("ot", [P, NG, T])
        rec = sb("rec", [P, TT, H])
        on = sb("on", [P, TT, E])
        onT = sb("onT", [P, T])
        stats2 = sb("stats2", [P, TT, 6])
        mv2 = sb("mv2", [P, TT, 2])
        ve2 = sb("ve2", [P, TT])
        rstd2 = sb("rstd2", [P, TT])
        neg_mean2 = sb("neg_mean2", [P, TT])
        xc2 = sb("xc2", [P, TT, E])
        xn2T = sb("xn2T", [P, T])
        rows = [sb(f"rows{i}", [P, TOPK, TT, ROW]) for i in range(2)]
        lg = [sb(f"lg{i}", [P, TT, NE]) for i in range(2)]
        top = sb("top", [P, TOPK, NT])
        r_dif = sb("r_dif", [P, TT, NE])
        r_key = sb("r_key", [P, TT, NE])
        r_kmax = sb("r_kmax", [P, TT])
        r_rest = sb("r_rest", [P, TT, NE])
        chosen = sb("chosen", [P, TOPK, TT, NE])
        both = sb("both", [P, TT, NE], bf16)
        used = sb("used", [P, NE])
        slot_of = sb("slot_of", [P, TT, NE])
        slot_sel = sb("slot_sel", [P, TOPK, TT, NE])
        slot_f = sb("slot_f", [P, TOPK, TT])
        slot_i = [sb(f"slot_i{i}", [P, TOPK, TT], i32) for i in range(2)]
        gate = sb("gate", [P, TOPK, NT])
        gate_t = sb("gate_t", [P, 3, NT])
        pad = sb("pad", [P, NE + SPARE, ROW])
        list0 = sb("list0", [P, NE])
        full_done = sb("full_done", [1, NE + 1])
        before_done = sb("before_done", [1, NE])
        skip = sb("skip", [1, NE])
        tile_row = sb("tile_row", [1, 2, TILES])
        row0 = sb("row0", [1, 1])
        count_i = sb("count_i", [1, 2, NE], i32)
        tiles_f = sb("tiles_f", [1, NE])
        tiles_end = sb("tiles_end", [1, NE])
        zero_e = sb("zero_e", [1, NE])
        jump = sb("jump", [1, NE])
        tile_no = sb("tile_no", [1, TILES])
        ended = sb("ended", [1, TILES, NE])
        ended_j = sb("ended_j", [1, TILES, NE])
        tab_f = sb("tab_f", [1, 2, TILES])
        tab = sb("tab", [1, 2, TILES], i32)
        pad_at = sb("pad_at", [1, NE], i32)
        NX = 8
        xt = [sb(f"xt{i}", [P, ROW]) for i in range(NX)]
        xtT = [sb(f"xtT{i}", [P, P]) for i in range(2)]
        NW = 4
        w1_t = [sb(f"w1_t{i}", [P, HID + KT]) for i in range(NW)]
        w2_t = [sb(f"w2_t{i}", [P, KT, E]) for i in range(NW)]
        b2_t = [sb(f"b2_t{i}", [PARTS, E], bf16) for i in range(NW)]
        hidT = [sb(f"hidT{i}", [P, HID]) for i in range(2)]
        yt = [sb(f"yt{i}", [P, E]) for i in range(NX)]
        NF = 4
        fin = [sb(f"fin{i}", [P, TOPK, NF, E]) for i in range(4)]

        bank = [ctx.enter_context(nc.psum_tensor(f"bank{i}", [P, 512], fp32)) for i in range(8)]
        SQ, ST, OT, PJ, OC, MISC = bank[0:2], bank[2:4], bank[4], bank[5], bank[6], bank[7]
        X2T_PS, mxT_ps = PJ[:, 0:T], MISC[0:PARTS * HH * TT, 0:P // 2].bitcast(bf16)
        LG_PS, RK_PS = MISC[:, 0:TT * NE], MISC[:, 0:(TT + 1) * NE]
        XT_PS, HIDT_PS = bank[0:2], bank[2:4]

        def y_ps(j, i):
            return OT[:, 0:E] if isinstance(j, int) and j < EARLY else bank[6 + i % 2][:, 0:E]


        s_x = [sem(f"x_chunk{i}") for i in range(3)]
        s_w = sem("weights_loaded")
        s_we = sem("expert_weights_loaded")
        s_bin = sem("bias_in_loaded")
        s_bout = sem("bias_parts_stored")
        s_brow = sem("bias_rows_loaded")
        s_const = sem("constants_made")
        s_bsplit = sem("bias_split_step")
        s_dconst = sem("copied_constants_made")
        s_vpad = sem("v_padding_made")
        s_kpad = [sem(f"qk_padding_made{i}") for i in range(2)]
        s_st1, s_mv1, s_ve1, s_rstd1, s_xn1 = (sem(n) for n in ("stats1_done", "mv1_done", "ve1_done", "rstd1_done", "xn1_done"))
        s_xT_ps, s_xT = sem("xn1T_in_psum"), sem("xn1T_done")
        s_qk_ps, s_v_ps = sem("qk_in_psum"), sem("v_in_psum")
        s_rot, s_va = sem("qk_rotated"), sem("v_done")
        s_qk, s_hi, s_rest, s_mid, s_lo = (sem(n) for n in ("qk_done", "hi_done", "rest_done", "mid_done", "lo_done"))
        s_pst = [sem(f"parts_stored{i}") for i in range(2)]
        s_ld = [[sem(f"qk_loaded{h}{i}") for i in range(2)] for h in range(2)]
        s_sq, s_mx = sem("sq_in_psum"), sem("max_done")
        s_ms = sem("max_split_step")
        s_mT_ps, s_mT = sem("mxT_in_psum"), sem("mxT_done")
        s_vn = sem("v_copied")
        s_ml = [sem(f"max_rows_loaded{h}") for h in range(2)]
        s_stp, s_exp, s_msk = sem("st_in_psum"), sem("exp_done"), sem("mask_done")
        s_pv, s_ot = sem("pv_done"), sem("ot_done")
        s_oc, s_rec, s_on = sem("o_turned"), sem("reciprocals_done"), sem("on_done")
        s_onT_ps, s_onT, s_y_ps, s_x1 = sem("onT_in_psum"), sem("onT_done"), sem("proj_in_psum"), sem("x1_done")
        s_st2, s_mv2, s_ve2, s_rstd2 = (sem(n) for n in ("stats2_done", "mv2_done", "ve2_done", "rstd2_done"))
        s_neg1, s_neg2, s_xc1, s_xc2 = (sem(n) for n in ("neg_mean1_done", "neg_mean2_done", "centred1_done", "centred2_done"))
        s_row0, s_row1, s_rowno = sem("rows_first_done"), sem("rows_second_done"), sem("row_numbers_done")
        s_x2T_ps, s_x2T, s_lg_ps, s_lg = sem("xn2T_in_psum"), sem("xn2T_done"), sem("logits_in_psum"), sem("logits_done")
        s_rt = sem("route_step")
        s_both, s_rk_ps, s_slot = sem("both_done"), sem("ranks_in_psum"), sem("slots_done")
        s_sc = [sem(f"rows_scattered{i}") for i in range(2)]
        s_used, s_tab, s_tabs = sem("used_step"), sem("table_step"), sem("tables_done")
        s_pad0 = sem("padding_made")
        s_ends = sem("list_ends_copied")
        s_pad, s_spare = sem("padding_stored"), sem("spare_stored")
        s_g, s_gexp, s_gate = sem("gate_step"), sem("gate_exp_done"), sem("gates_done")
        s_xt = [sem(f"tile_loaded{i}") for i in range(NX)]
        s_tx, s_xtT, s_hp, s_hid = sem("tile_turned"), sem("tileT_done"), sem("hidden_in_psum"), sem("hidden_done")
        s_w1t, s_w2t, s_yp, s_yt = sem("tile_w1_copied"), sem("tile_w2_copied"), sem("y_in_psum"), sem("y_done")
        s_ys = [sem(f"y_scattered{i}") for i in range(NX)]
        s_fl = [sem(f"results_loaded{i}") for i in range(4)]
        s_f0 = sem("first_choice_scaled")
        s_fs, s_fin, s_out = sem("first_added"), sem("final_done"), sem("out_stored")

        block = ctx.enter_context(nc.Block())

        N_CONST = 13
        W_PIECES = 4
        N_DCONST = 4
        N_W = 16 * 5
        x_tiles = x.rearrange("(n p) e -> p n e", p=P)
        out_tiles = out.rearrange("(n p) e -> p n e", p=P)
        LD_DMAS = 2
        ST_DMAS = 1 + 2 * PARTS
        NC_FIN = NT // NF

        def j_in(j, ahead, last):
            return j + ahead < last if isinstance(j, int) else True

        def j_before(j, n):
            return j >= n if isinstance(j, int) else True

        def apart(eng, *values):
            held = [v if isinstance(v, int) else eng.compute_val(v) for v in values]
            eng.wait_ge(s_const, N_CONST)
            return held

        def xrow(b, i):
            if b.known:
                return x_sb[:, TT * b.n + i, :]
            return x_sb[:, bass.ds(TT * b.n + i, 1), :].rearrange("p a e -> p (a e)")

        def early_tiles_at(t, u):
            return [j for j in range(EARLY) if t.known and EARLY_AT[j] == (t.n, u)]

        @block.sync
        def _(sp):
            sp.dma_start(x_sb[:, 0:TT, :], x_tiles[:, 0:TT, :]).then_inc(s_x[0], 16)
            sp.dma_start(wqkv_sb[:], wqkv.rearrange("p (a e) -> p a e", a=3)).then_inc(s_w, 16)
            sp.dma_start(qkb[:], qk_bias).then_inc(s_w, 16)
            sp.dma_start(rope_sb[:], rope).then_inc(s_w, 16)
            sp.dma_start(x_sb[:, TT:4 * TT, :], x_tiles[:, TT:4 * TT, :]).then_inc(s_x[1], 16)
            sp.dma_start(wproj_sb[:], wproj).then_inc(s_w, 16)
            sp.dma_start(wr_sb[:], wr).then_inc(s_w, 16)
            sp.wait_ge(s_bsplit, 5)
            sp.dma_start(bias_dram.ap().rearrange("a (p c) -> p a c", p=P), bias_split[:]).then_inc(s_bout, 16)
            sp.wait_ge(s_bout, 16)
            sp.dma_start(bias_rows[:], bias_dram.ap()).then_inc(s_brow, 16)
            sp.dma_start(x_sb[:, 4 * TT:NT, :], x_tiles[:, 4 * TT:NT, :]).then_inc(s_x[2], 16)

            sp.dma_start(w1_sb[:, :, HID:HID + KT], b1_cols).then_inc(s_we, 16)

            def load_half(b, half):
                sp.wait_ge(s_pst[b.par], 16 * ST_DMAS * (b.pair + 1))
                if b.known and b.n < 2:
                    sp.wait_ge(s_kpad[b.par], 2)
                heads, at = slice(half * HH, (half + 1) * HH), b.par * PARTS * P * T + half * HH * T
                src = bass.AP(q_dram, at, [[H * T, PARTS * D], [0, PARTS], [1, HH * T]])
                sp.dma_start(qa[b.par][0:QK_ROWS, heads, :], src).then_inc(s_ld[half][b.par], 16)
                src = bass.AP(k_dram, at, [[0, PARTS], [H * T, PARTS * D], [1, HH * T]])
                sp.dma_start(ka[b.par][0:QK_ROWS, heads, :], src).then_inc(s_ld[half][b.par], 16)

            def max_rows(b, half):
                sp.wait_ge(s_mT, 2 * b.n + half + 1)
                dst = qa[b.par][QK_ROWS:QK_ROWS + PARTS, half * HH:(half + 1) * HH, :]
                sp.dma_start(dst.rearrange("a h (t q) -> a (h t) q", t=TT),
                             mxT[half][:]).then_inc(s_ml[half], 16)

            def store_k(b, a):
                for e in range(2):
                    sp.dma_start(k_dram.ap()[b.par, e * D // 2:(e + 1) * D // 2, a],
                                 split[b.par][P // 2:P, a, e]).then_inc(s_pst[b.par], 16)

            def step(t):
                b3, b2, b1 = t.off(3), t.off(2), t.off(1)
                if t.real():
                    max_rows(t, 1)
                if b2.real():
                    store_k(b2, 1)
                    store_k(b2, 2)
                for half in range(2):
                    if b2.real():
                        if b2.after(2):
                            sp.wait_ge(s_stp, UNITS * t.n + UNITS // 2 * (half + 1))
                        load_half(b2, half)
                    if half == 0 and b1.real():
                        max_rows(b1, 0)
                    if t.known and 0 <= t.n < W_PIECES:
                        e = slice(t.n * NE // W_PIECES, (t.n + 1) * NE // W_PIECES)
                        if half == 0:
                            sp.dma_start(w1_sb[:, e, 0:HID], w1.rearrange("e p n -> p e n")[:, e]).then_inc(s_we, 16)
                        else:
                            sp.dma_start(w2_sb[:, e], w2.rearrange("e (k p) n -> p e k n", p=P)[:, e]).then_inc(s_we, 16)
                if b3.real():
                    done, read = apart(sp, b3.n + 1, 16 * LD_DMAS * b3.pair)
                    sp.wait_ge(s_lo, done)
                    sp.wait_ge(s_mid, done)
                    if b3.after(2):
                        sp.wait_ge(s_ld[0][b3.par], read)
                        sp.wait_ge(s_ld[1][b3.par], read)
                    sp.dma_start(q_dram.ap()[b3.par].rearrange("a (e i) h t -> (i h) (a e) t", e=2),
                                 split[b3.par][0:P // 2].rearrange("p a e t -> p (a e) t")).then_inc(s_pst[b3.par], 16)
                    store_k(b3, 0)

            run_steps(sp, step)

            def load_tile(j, i):
                at = sp.value_load(tab[0:1, 1, bass.ds(j, 1)], min_val=0, max_val=NE * STRIDE + SPARE * P - P)
                sp.dma_start(xt[i][:], lists.ap()[bass.ds(at, P), :]).then_inc(s_xt[i], 16)

            def store_padding(e):
                sp.wait_ge(s_pad0, 1)
                sp.wait_ge(s_ends, 1)
                at = sp.value_load(pad_at[0:1, e:e + 1], min_val=0, max_val=NE * STRIDE)
                sp.dma_start(lists.ap()[bass.ds(at, P), :], pad[:, e, :]).then_inc(s_pad, 16)

            sp.wait_ge(s_tabs, 2)
            for i in range(2):
                sp.wait_ge(s_sc[i], 16 * TOPK * TT * ((EARLY_FROM + 1 - i) // 2))
            for j in range(EARLY):
                if j >= NX:
                    sp.wait_ge(s_ys[j % NX], 16 * (j // NX))
                load_tile(j, j % NX)
                e = j - (EARLY - NE)
                if e >= 0:
                    store_padding(e)
            for i in range(2):
                sp.wait_ge(s_sc[i], 16 * TOPK * TT * (NB // 2))
            sp.wait_ge(s_pad, 16 * NE)
            sp.wait_ge(s_spare, 16)
            sp.wait_ge(s_tabs, 6)
            with sp.Fori(EARLY // NX, TILES // NX) as g:
                for i in range(NX):
                    sent, = apart(sp, 16 * g)
                    sp.wait_ge(s_ys[i], sent)
                    load_tile(NX * g + i, i)

            for i in range(NX):
                sp.wait_ge(s_ys[i], 16 * (TILES // NX))
            res = results.ap()[0:TOPK * NTOK, :].rearrange("(c n p) e -> p c n e", c=TOPK, p=P)

            def load_results(c):
                for k in range(TOPK):
                    sp.dma_start(fin[c % 4][:, k], res[:, k, c * NF:(c + 1) * NF, :]).then_inc(s_fl[c % 4], 16)

            for c in range(4):
                load_results(c)
            for c in range(NC_FIN):
                sp.wait_ge(s_fin, c + 1)
                sp.dma_start(out_tiles[:, c * NF:(c + 1) * NF, :], x_sb[:, c * NF:(c + 1) * NF, :]).then_inc(s_out, 16)
                if c + 4 < NC_FIN:
                    load_results(c + 4)
            sp.wait_ge(s_out, 16 * NC_FIN)

        @block.gpsimd
        def _(pool):
            nc.gpsimd.memset(ident[:], 0.0).then_inc(s_const, 1)
            nc.gpsimd.memset(maskb[:], 0.0).then_inc(s_const, 1)
            nc.gpsimd.memset(beforeb[:], 1.0).then_inc(s_const, 1)
            nc.gpsimd.memset(half_neg[:], -0.5).then_inc(s_const, 1)
            pool.wait_ge(s_const, 4)
            nc.gpsimd.affine_select(out=ident[:], in_=ident[:], compare_op=ALU.not_equal, fill=1.0, base=0,
                                    pattern=[[-1, P]], channel_multiplier=1).then_inc(s_const, 1)
            nc.gpsimd.affine_select(out=maskb[:], in_=maskb[:], compare_op=ALU.is_ge, fill=HIDDEN_MASK, base=0,
                                    pattern=[[-1, P]], channel_multiplier=1).then_inc(s_const, 1)
            nc.gpsimd.affine_select(out=beforeb[:], in_=beforeb[:], compare_op=ALU.is_gt, fill=0.0, base=0,
                                    pattern=[[1, P]], channel_multiplier=-1).then_inc(s_const, 1)
            pool.iota(tile_no[:], pattern=[[1, TILES]], base=0, channel_multiplier=0,
                      allow_small_or_imprecise_dtypes=True).then_inc(s_const, 1)
            pool.iota(list0[:], pattern=[[STRIDE, NE]], base=0, channel_multiplier=0,
                      allow_small_or_imprecise_dtypes=True).then_inc(s_const, 1)
            pool.iota(rank_down[:], pattern=[[0, TT], [-1, NE]], base=NE, channel_multiplier=0,
                      allow_small_or_imprecise_dtypes=True).then_inc(s_const, 1)
            for par in range(2):
                pool.iota(rows[par][:, :, :, E].bitcast(i32), pattern=[[NTOK, TOPK], [P, TT]],
                          base=par * T - 2 * T, channel_multiplier=1).then_inc(s_const, 1)
            pool.iota(pad[:, :, E].bitcast(i32), pattern=[[P, NE + SPARE]], base=TOPK * NTOK,
                      channel_multiplier=1).then_inc(s_const, 1)
            pool.wait_ge(s_const, N_CONST)

            def scatter(b, c, tile):
                pool.indirect_dma_start(
                    lists.ap(), bass.IndirectOffsetOnAxis(ap=slot_i[b.par][:, c, tile:tile + 1], axis=0),
                    rows[b.par][:, c, tile, :], None).then_inc(s_sc[b.par], 16)

            def step(t):
                b4, b3, bm1, bm2, bm3 = t.off(4), t.off(3), t.off(-1), t.off(-2), t.off(-3)
                for u in range(UNITS):
                    if t.real():
                        done, = apart(pool, UNITS * t.n + u + 1)
                        pool.wait_ge(s_exp, done)
                        if u % 3 == 2:
                            v = pr[:, slot(t, u), :].rearrange("p (h q) -> p h q", h=GROUP)
                        else:
                            v = pr[:, slot(t, u), :].rearrange("p (h q) -> p h q", h=2)[:, :, 0:P]
                        nc.gpsimd.affine_select(out=v, in_=v, compare_op=ALU.is_ge, fill=0.0, base=0,
                                                pattern=[[0, v.shape[1]], [1, P]],
                                                channel_multiplier=-1).then_inc(s_msk, 1)
                    if u == 0 and bm2.real():
                        if bm2.after(1):
                            pool.wait_ge(s_row0, TT * bm2.n)
                        pool.wait_ge(s_ve2, bm2.n + 1)
                        nc.gpsimd.tensor_tensor(rstd2[:], ve2[:], half_neg[:], ALU.pow).then_inc(s_rstd2, 1)
                        nc.gpsimd.tensor_scalar(neg_mean2[:], mv2[:, :, 0], -1.0, None, ALU.mult).then_inc(s_neg2, 1)
                    if u == 2 and b4.real():
                        if b4.after(1):
                            pool.wait_ge(s_xn1, TT * b4.n)
                        pool.wait_ge(s_ve1, b4.n + 1)
                        nc.gpsimd.tensor_tensor(rstd1[:], ve1[:], half_neg[:], ALU.pow).then_inc(s_rstd1, 1)
                        nc.gpsimd.tensor_scalar(neg_mean1[:], mv1[:, :, 0], -1.0, None, ALU.mult).then_inc(s_neg1, 1)
                    if u == 3 and t.known and t.n == FIRST_STEP + 3:
                        nc.gpsimd.memset(pad[:, :, 0:E], 0.0).then_inc(s_pad0, 1)
                        pool.wait_ge(s_pad0, 1)
                        pool.dma_start(lists.ap()[NE * STRIDE:NE * STRIDE + SPARE * P, :].rearrange("(k p) e -> p k e", p=P),
                                       pad[:, NE:NE + SPARE, :]).then_inc(s_spare, 16)
                    if u == 3 and t.known and t.n - FIRST_STEP in (1, 2):
                        i = t.n - FIRST_STEP - 1
                        pool.wait_ge(s_neg1, b4.n + 1)
                        nc.gpsimd.memset(ka[i][64:P, :, :].bitcast(fp32), TWO_ONES).then_inc(s_kpad[i], 1)
                        nc.gpsimd.memset(qa[i][64:P, :, :].bitcast(fp32), 0.0).then_inc(s_kpad[i], 1)
                        pool.wait_ge(s_kpad[i], 2)
                    if u == 4 and bm2.real():
                        sent, = apart(pool, 16 * TOPK * TT * bm2.pair)
                        if bm2.after(2):
                            pool.wait_ge(s_sc[bm2.par], sent)
                        v = rows[bm2.par][:, :, :, E].bitcast(i32)
                        nc.gpsimd.tensor_scalar(v, v, float(2 * T), None, ALU.add).then_inc(s_rowno, 1)
                    if u == 11 and b3.real():
                        pool.wait_ge(s_mid, b3.n + 1)
                        nc.gpsimd.tensor_tensor(split[b3.par][:, 2], qk_rest[:], split[b3.par][:, 1],
                                                ALU.subtract).then_inc(s_lo, 1)
                    for k in range(TOPK * TT):
                        if SCATTER_AT[k] != u or not bm3.real():
                            continue
                        if k == 0:
                            done, done2 = apart(pool, bm3.n + 1, 2 * (bm3.n + 1))
                            pool.wait_ge(s_slot, done)
                            pool.wait_ge(s_row0, done2)
                            pool.wait_ge(s_row1, done)
                            pool.wait_ge(s_rowno, done)
                        scatter(bm3, k // 2, k % 2)
                    for j in early_tiles_at(t, u):
                        scatter_y(j, j % NX, j // NX)

            def slot(t, u):
                return (UNITS * t.par + u) % NP

            def scatter_y(j, i, g):
                done, loaded = apart(pool, j + 1, 16 * (g + 1))
                pool.wait_ge(s_yt, done)
                pool.wait_ge(s_xt[i], loaded)
                pool.indirect_dma_start(
                    results.ap(), bass.IndirectOffsetOnAxis(ap=xt[i][:, E:E + 1].bitcast(i32), axis=0),
                    yt[i][:], None).then_inc(s_ys[i], 16)

            run_steps(pool, step)

            with pool.Fori(EARLY // NX, TILES // NX) as g:
                for i in range(NX):
                    scatter_y(NX * g + i, i, g)

        @block.scalar
        def _(act):
            act.dma_start(bias_in[:], biases).then_inc(s_bin, 16)
            act.wait_ge(s_bin, 16)
            nc.scalar.copy(bias_split[:, 0], bias_in[:]).then_inc(s_bsplit, 1)

            def step(t):
                b4, b3, b2, b1, bm1, bm2 = (t.off(d) for d in (4, 3, 2, 1, -1, -2))
                for u in range(UNITS):
                    if t.real():
                        act.wait_ge(s_stp, UNITS * t.n + u + 1)
                        if t.after(1) or u >= NP:
                            act.wait_ge(s_pv, NG * t.n + u // 3 - 1)
                        nc.scalar.activation(pr[:, (UNITS * t.par + u) % NP, :], ST[u % 2][:], ACT.Exp,
                                             scale=SCALE).then_inc(s_exp, 1)
                    if u == 0 and b3.real():
                        act.wait_ge(s_xT_ps, b3.n + 1)
                        nc.scalar.copy(xn1T[b3.par][:], PJ[:, 0:T]).then_inc(s_xT, 1)
                    if u == 5 and b3.real():
                        act.wait_ge(s_qk, b3.n + 1)
                        if b3.after(2):
                            act.wait_ge(s_pst[b3.par], 16 * ST_DMAS * b3.pair)
                        nc.scalar.copy(split[b3.par][:, 0], qk[:]).then_inc(s_hi, 1)
                    if u == 8 and b3.real():
                        act.wait_ge(s_rest, b3.n + 1)
                        nc.scalar.copy(split[b3.par][:, 1], qk_rest[:]).then_inc(s_mid, 1)
                    if u == 4 and b1.real():
                        act.wait_ge(s_vn, b1.n + 1)
                        if b1.after(2):
                            act.wait_ge(s_pv, NG * (b1.n - 1))
                        nc.scalar.copy(va[b1.par][:, :, :, 0:D],
                                       v_new[:].rearrange("p t (h d) -> p t h d", d=D)).then_inc(s_va, 1)
                    if u == 7 and b2.real():
                        act.wait_ge(s_v_ps, b2.n + 1)
                        if b2.after(1):
                            act.wait_ge(s_va, b2.n)
                        nc.scalar.copy(v_new[:].rearrange("p t e -> p (t e)"), PJ[:, 0:T]).then_inc(s_vn, 1)
                    if u == 8 and b1.real():
                        turn_max(b1, 0)
                    if u == 2 and t.real():
                        turn_max(t, 1)
                    if u == 3 and bm2.real():
                        centre(bm2, s_neg2, neg_mean2, xc2, s_xc2)
                    if u == 4 and bm2.real():
                        if bm2.after(2):
                            act.wait_ge(s_sc[bm2.par], 16 * TOPK * TT * bm2.pair)
                        scale_by(bm2, rstd2, s_xc2, xc2, rows[bm2.par][:, 0, :, 0:E], s_row0)
                    if u == 6 and b4.real():
                        centre(b4, s_neg1, neg_mean1, xc1, s_xc1)
                    if u == 7 and b4.real():
                        if b4.after(1):
                            act.wait_ge(s_xT_ps, b4.n)
                        scale_by(b4, rstd1, s_xc1, xc1, xn1, s_xn1)
                    if u == 10 and bm2.real():
                        act.wait_ge(s_lg_ps, bm2.n + 1)
                        nc.scalar.copy(lg[bm2.par][:], LG_PS.rearrange("p (t e) -> p t e", e=NE)).then_inc(s_lg, 1)
                    if u == 2 and bm1.real():
                        out_pair(bm1, 1)
                    if u == 8 and t.real():
                        out_pair(t, 0)
                    if u == 7 and bm1.real():
                        act.wait_ge(s_onT_ps, bm1.n + 1)
                        nc.scalar.copy(onT[:], OC[:, 0:T]).then_inc(s_onT, 1)
                    if u == 8 and bm2.real():
                        act.wait_ge(s_x2T_ps, bm2.n + 1)
                        nc.scalar.copy(xn2T[:], X2T_PS).then_inc(s_x2T, 1)
                    if u == 9 and bm2.real():
                        act.wait_ge(s_row0, 2 * (bm2.n + 1))
                        if bm2.after(2):
                            act.wait_ge(s_sc[bm2.par], 16 * TOPK * TT * bm2.pair)
                        nc.scalar.copy(rows[bm2.par][:, 1, :, 0:E], rows[bm2.par][:, 0, :, 0:E]).then_inc(s_row1, 1)
                    for j in early_tiles_at(t, u):
                        if j == 0:
                            start_tiles(0)
                        tile(j, j % NX, j // NX, EARLY)

            def centre(b, s_neg, neg_mean, xc, s_xc):
                done, = apart(act, b.n + 1)
                act.wait_ge(s_neg, done)
                for i in range(TT):
                    nc.scalar.activation(xc[:, i, :], xrow(b, i), ACT.Identity, bias=neg_mean[:, i:i + 1]
                                         ).then_inc(s_xc, 1)

            def scale_by(b, rstd, s_xc, xc, dst, s_done):
                act.wait_ge(s_xc, TT * (b.n + 1))
                for i in range(TT):
                    nc.scalar.activation(dst[:, i, :], xc[:, i, :], ACT.Copy, scale=rstd[:, i:i + 1]).then_inc(s_done, 1)

            def turn_max(b, half):
                act.wait_ge(s_mT_ps, 2 * b.n + half + 1)
                if b.after(1):
                    act.wait_ge(s_ml[half], 16 * b.n)
                nc.scalar.copy(mxT[half][:], mxT_ps).then_inc(s_mT, 1)

            def out_pair(b, k):
                act.wait_ge(s_pv, NG * b.n + 2 * k + 2)
                if b.after(1):
                    act.wait_ge(s_oc, 2 * b.n)
                nc.scalar.copy(ot[:, 2 * k:2 * k + 2, :].rearrange("p g q -> p (g q)"), OT[:]).then_inc(s_ot, 1)

            def copy_xT(j, i):
                act.wait_ge(s_tx, j + 1)
                nc.scalar.copy(xtT[i % 2][:], XT_PS[i % 2][:, 0:P]).then_inc(s_xtT, 1)

            def relu(j, i):
                act.wait_ge(s_hp, j + 1)
                if j_before(j, 2):
                    act.wait_ge(s_yp, j - 1)
                for k in range(KT):
                    last = nc.scalar.activation(hidT[i % 2][:, k * P:(k + 1) * P], HIDT_PS[i % 2][:, k * P:(k + 1) * P],
                                                ACT.Relu, bias=w1_t[i % NW][:, HID + k:HID + k + 1])
                last.then_inc(s_hid, 1)

            def copy_y(j, i, g):
                act.wait_ge(s_yp, j + 1)
                if j_before(j, NX):
                    act.wait_ge(s_ys[i], 16 * g)
                nc.scalar.copy(yt[i][:], y_ps(j, i)).then_inc(s_yt, 1)

            def start_tiles(j):
                copy_xT(j, 0)
                copy_xT(j + 1, 1)
                relu(j, 0)

            def tile(j, i, g, last):
                if j_in(j, 2, last):
                    copy_xT(j + 2, i)
                if j_in(j, 1, last):
                    relu(j + 1, i + 1)
                copy_y(j, i, g)

            run_steps(act, step)

            start_tiles(EARLY)
            with act.Fori(EARLY // NX, TILES // NX - 1) as g:
                for i in range(NX):
                    tile(NX * g + i, i, g, TILES)
            for j in range(TILES - NX, TILES):
                tile(j, j % NX, j // NX, TILES)

            act.wait_ge(s_g, 1)
            nc.scalar.activation(gate_t[:, 1, :], gate_t[:, 0, :], ACT.Exp).then_inc(s_gexp, 1)

            act.wait_ge(s_gate, 1)
            for c in range(NC_FIN):
                act.wait_ge(s_fl[c % 4], 16 * TOPK * (c // 4 + 1))
                for i in range(NF):
                    n = c * NF + i
                    nc.scalar.activation(fin[c % 4][:, 0, i], fin[c % 4][:, 0, i], ACT.Copy,
                                         scale=gate[:, 0, n:n + 1]).then_inc(s_f0, 1)

        @block.vector
        def _(dve):
            def own_constants():
                nc.vector.memset(onesb[:], 1.0).then_inc(s_dconst, 1)
                dve.wait_ge(s_const, N_CONST)
                nc.vector.tensor_copy(identb[:], ident[:]).then_inc(s_dconst, 1)
                nc.vector.tensor_copy(used[:], list0[:]).then_inc(s_dconst, 1)
                nc.vector.memset(zero_e[:], 0.0).then_inc(s_dconst, 1)
                dve.wait_ge(s_bin, 16)
                dve.wait_ge(s_bsplit, 1)
                nc.vector.tensor_tensor(bias_rest[:, 0], bias_in[:], bias_split[:, 0], ALU.subtract).then_inc(s_bsplit, 1)
                dve.wait_ge(s_bsplit, 2)
                nc.vector.tensor_copy(bias_split[:, 1], bias_rest[:, 0]).then_inc(s_bsplit, 1)
                dve.wait_ge(s_bsplit, 3)
                nc.vector.tensor_tensor(bias_rest[:, 1], bias_rest[:, 0], bias_split[:, 1], ALU.subtract).then_inc(s_bsplit, 1)
                dve.wait_ge(s_bsplit, 4)
                nc.vector.tensor_copy(bias_split[:, 2], bias_rest[:, 1]).then_inc(s_bsplit, 1)

            def own_v_padding():
                for i in range(2):
                    nc.vector.memset(va[i][:, :, :, D:VC], 0.0).then_inc(s_vpad, 1)
                dve.wait_ge(s_vpad, 2)
                for i in range(2):
                    nc.vector.memset(va[i][:, :, :, D:D + 1], 1.0).then_inc(s_vpad, 1)
                dve.wait_ge(s_dconst, N_DCONST)

            def norm_step(b, k, stats, mv, ve, s_stat, s_mv, s_ve, s_neg):
                if k < TT:
                    nc.vector.bn_stats(stats[:, k, :], xrow(b, k)).then_inc(s_stat, 1)
                elif k < 2 * TT:
                    if k == TT:
                        done, read = apart(dve, TT * (b.n + 1), b.n)
                        dve.wait_ge(s_stat, done)
                        if b.after(1):
                            dve.wait_ge(s_neg, read)
                    nc.vector.bn_aggr(mv[:, k - TT, :], stats[:, k - TT, :]).then_inc(s_mv, 1)
                else:
                    dve.wait_ge(s_mv, TT * (b.n + 1))
                    nc.vector.tensor_scalar(ve[:], mv[:, :, 1], EPS, None, ALU.add).then_inc(s_ve, 1)

            def rotate(b, odd):
                dve.wait_ge(s_qk_ps, b.n + 1)
                if b.known and b.n == 0:
                    dve.wait_ge(s_w, N_W)
                width = PJ[:, odd * T:(odd + 1) * T].unsqueeze(1).to_broadcast([P, 2, T])
                nc.vector.scalar_tensor_tensor((rope_b if odd else rope_a)[:], width, qkb[:, odd:odd + 1],
                                               rope_sb[:, odd], ALU.add, ALU.mult).then_inc(s_rot, 1)

            def split_max(b, half, k):
                m = mx[b.par][:, half * HH:(half + 1) * HH, :]
                at = 4 * (2 * b.n + half)
                if k == 0:
                    dve.wait_ge(s_mx, UNITS * b.n + UNITS // 2 * (half + 1))
                    if half or b.after(1):
                        dve.wait_ge(s_mT_ps, 2 * b.n + half)
                    nc.vector.tensor_scalar(mx_split[:, 0], m, -1.0, None, ALU.mult).then_inc(s_ms, 1)
                elif k == 1:
                    dve.wait_ge(s_ms, at + 1)
                    nc.vector.scalar_tensor_tensor(mx_rest[:], m, -1.0, mx_split[:, 0], ALU.mult,
                                                   ALU.subtract).then_inc(s_ms, 1)
                elif k == 2:
                    dve.wait_ge(s_ms, at + 2)
                    nc.vector.tensor_copy(mx_split[:, 1], mx_rest[:]).then_inc(s_ms, 1)
                else:
                    dve.wait_ge(s_ms, at + 3)
                    nc.vector.tensor_tensor(mx_split[:, 2], mx_rest[:], mx_split[:, 1],
                                            ALU.subtract).then_inc(s_ms, 1)

            ROUTE = 13

            def route(b, k):
                at = ROUTE * b.n
                if k > 0:
                    dve.wait_ge(s_rt, at + k)
                lgb = lg[b.par]
                tiles = bass.ds(TT * b.n, TT) if not b.known else slice(TT * b.n, TT * b.n + TT)

                def wide(v):
                    return v.unsqueeze(2).to_broadcast([P, TT, NE])

                if k == 0:
                    dve.wait_ge(s_lg, b.n + 1)
                    ins = nc.vector.tensor_reduce(top[:, 0, tiles], lgb[:], X, ALU.max)
                elif k == 1:
                    ins = nc.vector.tensor_tensor(r_dif[:], lgb[:], wide(top[:, 0, tiles]), ALU.is_ge)
                elif k == 2:
                    ins = nc.vector.tensor_tensor(r_key[:], r_dif[:], rank_down[:], ALU.mult)
                elif k == 3:
                    ins = nc.vector.tensor_reduce(r_kmax[:], r_key[:], X, ALU.max)
                elif k == 4:
                    ins = nc.vector.tensor_tensor(chosen[:, 0], r_key[:], wide(r_kmax[:]), ALU.is_equal)
                elif k == 5:
                    ins = nc.vector.scalar_tensor_tensor(r_rest[:], chosen[:, 0], HIDDEN_MASK, lgb[:],
                                                         ALU.mult, ALU.add)
                elif k == 6:
                    ins = nc.vector.tensor_reduce(top[:, 1, tiles], r_rest[:], X, ALU.max)
                elif k == 7:
                    ins = nc.vector.tensor_tensor(r_dif[:], r_rest[:], wide(top[:, 1, tiles]), ALU.is_ge)
                elif k == 8:
                    ins = nc.vector.tensor_tensor(r_key[:], r_dif[:], rank_down[:], ALU.mult)
                elif k == 9:
                    ins = nc.vector.tensor_reduce(r_kmax[:], r_key[:], X, ALU.max)
                elif k == 10:
                    ins = nc.vector.tensor_tensor(chosen[:, 1], r_key[:], wide(r_kmax[:]), ALU.is_equal)
                elif k == 11:
                    ins = nc.vector.tensor_tensor(both[:], chosen[:, 0], chosen[:, 1], ALU.add)
                elif k == 12:
                    dve.wait_ge(s_rk_ps, b.n + 1)
                    ins = nc.vector.tensor_tensor(slot_of[:], RK_PS[:, 0:TT * NE].rearrange("p (t e) -> p t e", e=NE),
                                                  used[:].unsqueeze(1).to_broadcast([P, TT, NE]), ALU.add)
                ins.then_inc(s_rt, 1)

            def route_end(b, k):
                at = 3 * b.n
                if k == 0:
                    dve.wait_ge(s_rt, ROUTE * (b.n + 1))
                    nc.vector.tensor_tensor(used[:], used[:], RK_PS[:, TT * NE:(TT + 1) * NE],
                                            ALU.add).then_inc(s_used, 1)
                elif k == 1:
                    nc.vector.tensor_tensor(slot_sel[:], chosen[:], slot_of[:].unsqueeze(1).to_broadcast([P, TOPK, TT, NE]),
                                            ALU.mult).then_inc(s_used, 1)
                elif k == 2:
                    dve.wait_ge(s_used, at + 2)
                    nc.vector.tensor_reduce(slot_f[:], slot_sel[:], X, ALU.add).then_inc(s_used, 1)
                else:
                    dve.wait_ge(s_used, at + 3)
                    if b.after(2):
                        dve.wait_ge(s_sc[b.par], 16 * TOPK * TT * b.pair)
                    nc.vector.tensor_copy(slot_i[b.par][:], slot_f[:]).then_inc(s_slot, 1)

            def row_max(b, v):
                dve.wait_ge(s_sq, UNITS * b.n + v + 1)
                g = v // 3
                if v % 3 == 2:
                    src = SQ[v % 2][:].rearrange("p (h k) -> p h k", h=GROUP)
                    dst = mx[b.par][:, GROUP * g:GROUP * g + GROUP, 0]
                else:
                    h0 = GROUP * g + 2 * (v % 3)
                    src = SQ[v % 2][:].rearrange("p (h k) -> p h k", h=2)
                    dst = mx[b.par][:, h0:h0 + 2, 1]
                nc.vector.tensor_reduce(dst, src, X, ALU.max).then_inc(s_mx, 1)

            def step(t):
                b4, b3, b2, b1 = t.off(4), t.off(3), t.off(2), t.off(1)
                bm1, bm2, bm3 = t.off(-1), t.off(-2), t.off(-3)
                for u in range(UNITS):
                    bm, v = (b1, u + LEAD) if u + LEAD < UNITS else (b2, u + LEAD - UNITS)
                    if bm.real():
                        row_max(bm, v)
                    if u == 0:
                        if bm3.real():
                            route(bm3, 3)
                        if b4.real():
                            if b4.known and b4.n in (0, 1, 4):
                                dve.wait_ge(s_x[{0: 0, 1: 1, 4: 2}[b4.n]], 16)
                            norm1(b4, 0)
                        if bm3.real():
                            route(bm3, 4)
                        if b4.real():
                            norm1(b4, 1)
                        if bm3.real():
                            route(bm3, 5)
                    if u == 1:
                        if b4.real():
                            norm1(b4, 2)
                        if bm3.real():
                            route(bm3, 6)
                        if b4.real():
                            norm1(b4, 3)
                        if bm3.real():
                            route(bm3, 7)
                        if b4.real():
                            norm1(b4, 4)
                        if bm3.real():
                            route(bm3, 8)
                    if u == 2:
                        if b3.real():
                            rotate(b3, 0)
                        if bm3.real():
                            route(bm3, 9)
                        if b3.real():
                            rotate(b3, 1)
                        if bm3.real():
                            route(bm3, 10)
                    if u == 3:
                        if bm1.real():
                            reciprocals(bm1, 0)
                        if bm3.real():
                            if bm3.after(1):
                                dve.wait_ge(s_rk_ps, bm3.n)
                            route(bm3, 11)
                        if b1.real():
                            split_max(b1, 0, 0)
                        if bm1.real():
                            divide(bm1, 0)
                        if b1.real():
                            split_max(b1, 0, 1)
                    if u == 4:
                        if b3.real():
                            dve.wait_ge(s_rot, 2 * (b3.n + 1))
                            if b3.after(1):
                                dve.wait_ge(s_rest, b3.n)
                                dve.wait_ge(s_hi, b3.n)
                            nc.vector.tensor_tensor(qk[:], rope_a[:], rope_b[:], ALU.add).then_inc(s_qk, 1)
                        if b1.real():
                            split_max(b1, 0, 2)
                        if b1.real():
                            split_max(b1, 0, 3)
                    if u == 5:
                        if bm1.real():
                            reciprocals(bm1, 1)
                        if bm3.real():
                            route(bm3, 12)
                        if bm3.real():
                            route_end(bm3, 0)
                        if bm1.real():
                            divide(bm1, 1)
                        if bm3.real():
                            route_end(bm3, 1)
                    if u == 6:
                        if b3.real():
                            dve.wait_ge(s_hi, b3.n + 1)
                            if b3.after(1):
                                dve.wait_ge(s_lo, b3.n)
                                dve.wait_ge(s_mid, b3.n)
                            nc.vector.tensor_tensor(qk_rest[:], qk[:], split[b3.par][:, 0],
                                                    ALU.subtract).then_inc(s_rest, 1)
                        if bm3.real():
                            route_end(bm3, 2)
                    if u == 7 and bm3.real():
                        route_end(bm3, 3)
                    if u == 9:
                        if t.known and t.n == FIRST_STEP:
                            own_constants()
                        if b1.real():
                            split_max(b1, 1, 0)
                            split_max(b1, 1, 1)
                    if u == 10:
                        if bm1.real():
                            dve.wait_ge(s_y_ps, bm1.n + 1)
                            xr = (x_sb[:, TT * bm1.n:TT * (bm1.n + 1), :] if bm1.known
                                  else x_sb[:, bass.ds(TT * bm1.n, TT), :])
                            nc.vector.tensor_tensor(xr, OC[:, 0:T].rearrange("p (t e) -> p t e", t=TT), xr,
                                                    ALU.add).then_inc(s_x1, 1)
                        if bm1.real():
                            done, = apart(dve, bm1.n + 1)
                            dve.wait_ge(s_x1, done)
                            norm2(bm1, 0)
                        if b1.real():
                            split_max(b1, 1, 2)
                        if bm1.real():
                            norm2(bm1, 1)
                    if u == 11:
                        if t.known and t.n == FIRST_STEP + 1:
                            own_v_padding()
                        if b1.real():
                            split_max(b1, 1, 3)
                        if bm1.real():
                            norm2(bm1, 2)
                        if bm2.real():
                            route(bm2, 0)
                        if bm1.real():
                            norm2(bm1, 3)
                        if bm2.real():
                            route(bm2, 1)
                        if bm1.real():
                            norm2(bm1, 4)
                        if bm2.real():
                            route(bm2, 2)

                    if t.known and (t.n, u) == TABLE_AT:
                        early_table()
                    if t.known and (t.n, u) in WEIGHTS_AT:
                        j = WEIGHTS_AT.index((t.n, u))
                        if j == 0:
                            dve.wait_ge(s_we, 16 * (1 + 2 * W_PIECES))
                            dve.wait_ge(s_brow, 16)
                            dve.wait_ge(s_tabs, 2)
                        copy_weights(j, j)
                    if t.known and (t.n, u) == LATE_TABLE_AT:
                        late_table()
                    for j in early_tiles_at(t, u):
                        if j + len(WEIGHTS_AT) < EARLY:
                            copy_weights(j + len(WEIGHTS_AT), j + len(WEIGHTS_AT))
                        if j == REST_OF_TABLE_AFTER:
                            fill_table(EARLY + NX, TILES, EARLY, jump[:])

            def norm1(b, k):
                norm_step(b, k, stats1, mv1, ve1, s_st1, s_mv1, s_ve1, s_neg1)

            def norm2(b, k):
                norm_step(b, k, stats2, mv2, ve2, s_st2, s_mv2, s_ve2, s_neg2)

            def reciprocals(b, qt):
                dve.wait_ge(s_oc, 2 * b.n + qt + 1)
                nc.vector.reciprocal(rec[:, qt, :], OC[:].rearrange("p (h c) -> p h c", c=VC)[:, :, D]).then_inc(s_rec, 1)

            def divide(b, qt):
                dve.wait_ge(s_rec, 2 * b.n + qt + 1)
                nc.vector.tensor_tensor(on[:, qt, :].rearrange("p (h d) -> p h d", d=D),
                                        OC[:].rearrange("p (h c) -> p h c", c=VC)[:, :, 0:D],
                                        rec[:, qt, :].unsqueeze(2).to_broadcast([P, H, D]),
                                        ALU.mult).then_inc(s_on, 1)

            chain = [0]

            def then(ins):
                aside(ins)
                dve.wait_ge(s_tab, chain[0])

            def aside(ins):
                chain[0] += 1
                ins.then_inc(s_tab, 1)

            def fill_table(lo, hi, first, jump):
                n, at = hi - lo, slice(lo - first, hi - first)
                then(nc.vector.tensor_tensor(ended[:, lo:hi], tile_no[:, at].unsqueeze(2).to_broadcast([1, n, NE]),
                                             tiles_end[:].unsqueeze(1).to_broadcast([1, n, NE]), ALU.is_ge))
                aside(nc.vector.tensor_reduce(tab_f[:, 0, lo:hi], ended[:, lo:hi], X, ALU.add))
                then(nc.vector.tensor_tensor(ended_j[:, lo:hi], ended[:, lo:hi],
                                             jump.unsqueeze(1).to_broadcast([1, n, NE]), ALU.mult))
                then(nc.vector.tensor_reduce(tab_f[:, 1, lo:hi], ended_j[:, lo:hi], X, ALU.add))
                nc.vector.tensor_scalar(tab[:, 0, lo:hi], tab_f[:, 0, lo:hi], float(NE - 1), None,
                                        ALU.min).then_inc(s_tabs, 1)
                nc.vector.tensor_tensor(tab[:, 1, lo:hi], tile_row[:, int(first > 0), at], tab_f[:, 1, lo:hi],
                                        ALU.add).then_inc(s_tabs, 1)

            def list_tiles(more):
                then(nc.vector.scalar_tensor_tensor(count_i[:, 0], used[0:1, :], float(more), list0[0:1, :], ALU.add,
                                                    ALU.subtract))
                then(nc.vector.tensor_scalar(count_i[:, 1], count_i[:, 0], P.bit_length() - 1, None,
                                             ALU.arith_shift_right))
                then(nc.vector.tensor_copy(tiles_f[:], count_i[:, 1]))

            def early_table():
                dve.wait_ge(s_used, 3 * EARLY_FROM)
                aside(nc.vector.memset(full_done[:, NE:NE + 1], 0.0))
                aside(nc.vector.tensor_scalar(tile_row[:, 0], tile_no[:], float(P), None, ALU.mult))
                list_tiles(0)
                aside(nc.vector.tensor_scalar(jump[:], tiles_f[:], float(-P), float(STRIDE), ALU.mult, ALU.add))
                then(nc.vector.tensor_tensor_scan(tiles_end[:], tiles_f[:], zero_e[:], 0.0, ALU.add, ALU.add))
                fill_table(0, EARLY, 0, jump[:])
                then(nc.vector.tensor_tensor(before_done[:], tiles_f[:], tiles_end[:], ALU.subtract))
                then(nc.vector.tensor_scalar(before_done[:], before_done[:], float(EARLY), 0.0, ALU.add, ALU.max))
                then(nc.vector.tensor_tensor(full_done[:, 0:NE], before_done[:], tiles_f[:], ALU.min))
                aside(nc.vector.tensor_scalar(row0[:], full_done[:, 0:1], float(P), None, ALU.mult))
                then(nc.vector.tensor_tensor(skip[:], full_done[:, 1:NE + 1], full_done[:, 0:NE], ALU.subtract))
                aside(nc.vector.tensor_scalar(tile_row[:, 1], tile_row[:, 0], row0[:, 0:1], None, ALU.add))
                then(nc.vector.tensor_scalar(skip[:], skip[:], float(P), float(STRIDE), ALU.mult, ALU.add))

            def late_table():
                dve.wait_ge(s_used, 3 * NB)
                nc.vector.tensor_copy(pad_at[:], used[0:1, :]).then_inc(s_ends, 1)
                list_tiles(P - 1)
                then(nc.vector.tensor_tensor(tiles_f[:], tiles_f[:], full_done[:, 0:NE], ALU.subtract))
                aside(nc.vector.scalar_tensor_tensor(jump[:], tiles_f[:], float(-P), skip[:], ALU.mult, ALU.add))
                then(nc.vector.tensor_tensor_scan(tiles_end[:], tiles_f[:], zero_e[:], 0.0, ALU.add, ALU.add))
                fill_table(EARLY, EARLY + NX, EARLY, jump[:])

            def copy_weights(j, i):
                e = dve.value_load(tab[0:1, 0, bass.ds(j, 1)], min_val=0, max_val=NE - 1)
                if j_before(j, NW):
                    dve.wait_ge(s_hid, j - NW + 1)
                nc.vector.tensor_copy(w1_t[i % NW][:], w1_sb[:, bass.ds(e, 1), :].rearrange("p a n -> p (a n)")
                                      ).then_inc(s_w1t, 1)
                if j_before(j, NW):
                    dve.wait_ge(s_yp, j - NW + 1)
                nc.vector.tensor_copy(w2_t[i % NW][:].rearrange("p k n -> p (k n)"),
                                      w2_sb[:, bass.ds(e, 1), :, :].rearrange("p a k n -> p (a k n)")).then_inc(s_w2t, 1)
                nc.vector.tensor_copy(b2_t[i % NW][:], bias_rows[:, bass.ds(e * E + B2_AT, E)]).then_inc(s_w2t, 1)

            run_steps(dve, step)


            dve.wait_ge(s_tabs, 6)
            with dve.Fori(EARLY // NX, TILES // NX) as g:
                for i in range(NX):
                    copy_weights(NX * g + i, i)

            nc.vector.tensor_tensor(gate_t[:, 0], top[:, 1], top[:, 0], ALU.subtract).then_inc(s_g, 1)
            dve.wait_ge(s_gexp, 1)
            nc.vector.tensor_scalar(gate_t[:, 2], gate_t[:, 1], 1.0, None, ALU.add).then_inc(s_g, 1)
            dve.wait_ge(s_g, 2)
            nc.vector.reciprocal(gate[:, 0], gate_t[:, 2]).then_inc(s_g, 1)
            dve.wait_ge(s_g, 3)
            nc.vector.tensor_tensor(gate[:, 1], gate_t[:, 1], gate[:, 0], ALU.mult).then_inc(s_gate, 1)

            dve.wait_ge(s_gate, 1)
            for c in range(NC_FIN):
                dve.wait_ge(s_fl[c % 4], 16 * TOPK * (c // 4 + 1))
                for i in range(NF):
                    n = c * NF + i
                    nc.vector.scalar_tensor_tensor(fin[c % 4][:, 1, i], fin[c % 4][:, 1, i], gate[:, 1, n:n + 1],
                                                   x_sb[:, n, :], ALU.mult, ALU.add).then_inc(s_fs, 1)
                dve.wait_ge(s_fs, NF * (c + 1))
                dve.wait_ge(s_f0, NF * (c + 1))
                nc.vector.tensor_tensor(x_sb[:, c * NF:(c + 1) * NF, :], fin[c % 4][:, 0], fin[c % 4][:, 1],
                                        ALU.add).then_inc(s_fin, 1)

        @block.tensor
        def _(pe):
            pe.wait_ge(s_const, N_CONST)

            def add_bias(dst, at, n, stop=True):
                return nc.tensor.matmul(dst, onesb[0:PARTS, 0:dst.shape[0]], bias_rows[:, at:at + n],
                                        start=False, stop=stop, skip_group_check=True)

            def max_unit(b, u):
                n = UNITS * b.n + u
                g, dst = u // 3, SQ[u % 2]
                if b.after(1) or u >= 2:
                    pe.wait_ge(s_mx, n - 1)
                if u % 6 == 0:
                    pe.wait_ge(s_ld[u // 6][b.par], 16 * LD_DMAS * (b.pair + 1))
                q, k = qa[b.par], ka[b.par]
                if u % 3 == 2:
                    for j in range(GROUP):
                        h = GROUP * g + j
                        nc.tensor.matmul(dst[:, j * P:(j + 1) * P], q[0:QK_ROWS, h, 0:P], k[0:QK_ROWS, h, 0:P],
                                         start=(j == 0), stop=False, skip_group_check=True)
                    nc.tensor.matmul(dst[:].rearrange("p (h k) -> p h k", h=GROUP), identb[:],
                                     maskb[:].unsqueeze(1).to_broadcast([P, GROUP, P]), start=False, stop=True,
                                     skip_group_check=True).then_inc(s_sq, 1)
                else:
                    for j in range(2):
                        h = GROUP * g + 2 * (u % 3) + j
                        nc.tensor.matmul(dst[:, j * T:(j + 1) * T], q[0:QK_ROWS, h, P:T], k[0:QK_ROWS, h, :],
                                         start=(j == 0), stop=False, skip_group_check=True)
                    nc.tensor.matmul(dst[:].rearrange("p (h k) -> p h k", h=2)[:, :, P:T], identb[:],
                                     maskb[:].unsqueeze(1).to_broadcast([P, 2, P]), start=False, stop=True,
                                     skip_group_check=True).then_inc(s_sq, 1)

            def exp_unit(b, u):
                n = UNITS * b.n + u
                g, dst = u // 3, ST[u % 2]
                if b.after(1) or u >= 2:
                    pe.wait_ge(s_exp, n - 1)
                if u % 6 == 0:
                    pe.wait_ge(s_ml[u // 6], 16 * (b.n + 1))
                q, k = qa[b.par], ka[b.par]
                if u % 3 == 2:
                    for j in range(GROUP):
                        h = GROUP * g + j
                        last = nc.tensor.matmul(dst[:, j * P:(j + 1) * P], k[:, h, P:T], q[:, h, P:T],
                                                start=True, stop=True)
                else:
                    for j in range(2):
                        h = GROUP * g + 2 * (u % 3) + j
                        last = nc.tensor.matmul(dst[:, j * T:(j + 1) * T], k[:, h, 0:P], q[:, h, :],
                                                start=True, stop=True)
                last.then_inc(s_stp, 1)

            def times_v(b, g):
                pe.wait_ge(s_msk, UNITS * b.n + 3 * g + 3)
                if g == 0:
                    pe.wait_ge(s_va, b.n + 1)
                    if b.known and b.n == 0:
                        pe.wait_ge(s_vpad, 4)
                if g % 2 == 0 and (g or b.after(1)):
                    pe.wait_ge(s_ot, 2 * b.n + g // 2)
                s0 = UNITS * b.par + 3 * g
                dst = OT[:, (g % 2) * T:(g % 2 + 1) * T]
                for j in range(GROUP):
                    p = pr[:, (s0 + j // 2) % NP, :].rearrange("p (h q) -> p h q", h=2)[:, j % 2, :]
                    nc.tensor.matmul(dst[32 * j:32 * j + VC, :], va[b.par][:, 0, GROUP * g + j, :], p,
                                     start=True, stop=False, skip_group_check=True)
                for j in range(GROUP):
                    p = pr[:, (s0 + 2) % NP, j * P:(j + 1) * P]
                    last = nc.tensor.matmul(dst[32 * j:32 * j + VC, P:T], va[b.par][:, 1, GROUP * g + j, :], p,
                                            start=False, stop=True, skip_group_check=True)
                last.then_inc(s_pv, 1)

            def turn_max(b, half):
                split_done, copied, ranked, routed = apart(pe, 4 * (2 * b.n + half) + 4, 2 * b.n + half,
                                                           3 * (b.n - 4) + 1, b.n - 2)
                pe.wait_ge(s_ms, split_done)
                if half or b.after(1):
                    pe.wait_ge(s_mT, copied)
                if half == 0 and b.after(4):
                    pe.wait_ge(s_used, ranked)
                if half == 1 and b.after(3):
                    pe.wait_ge(s_lg, routed)
                nc.tensor.transpose(mxT_ps, mx_split[:].rearrange("p a h t -> p (a h t)"),
                                    identb[:]).then_inc(s_mT_ps, 1)

            def project(b, u):
                if u == 0:
                    pe.wait_ge(s_xn1, TT * (b.n + 1))
                    if b.after(1):
                        pe.wait_ge(s_rot, 2 * b.n)
                    if b.after(2):
                        pe.wait_ge(s_vn, b.n - 1)
                    if b.after(6):
                        pe.wait_ge(s_x2T, b.n - 5)
                    for i in range(TT):
                        last = nc.tensor.transpose(PJ[:, i * P:(i + 1) * P], xn1[:, i, :], ident[:])
                    last.then_inc(s_xT_ps, 1)
                elif u == 2:
                    pe.wait_ge(s_xT, b.n + 1)
                    if b.known and b.n == 0:
                        pe.wait_ge(s_w, N_W)
                        pe.wait_ge(s_dconst, N_DCONST)
                    nc.tensor.matmul(PJ[:, 0:T], wqkv_sb[:, 0, :], xn1T[b.par][:], start=True, stop=True)
                    nc.tensor.matmul(PJ[:, T:2 * T], wqkv_sb[:, 1, :], xn1T[b.par][:], start=True, stop=True).then_inc(s_qk_ps, 1)

            def project_v(b):
                if b.off(1).real():
                    pe.wait_ge(s_rot, 2 * (b.n + 2))
                if b.after(1):
                    pe.wait_ge(s_vn, b.n)
                if b.known and b.n == 0:
                    pe.wait_ge(s_brow, 16)
                for i in range(TT):
                    nc.tensor.matmul(PJ[:, i * P:(i + 1) * P], xn1T[b.par][:, i * P:(i + 1) * P], wqkv_sb[:, 2, :],
                                     start=(i == 0), stop=False, skip_group_check=True)
                    last = add_bias(PJ[:, i * P:(i + 1) * P], BV_AT, E)
                last.then_inc(s_v_ps, 1)

            def finish(b, u):
                if u in (3, 5):
                    qt = (u - 3) // 2
                    pe.wait_ge(s_ot, 2 * (b.n + 1))
                    if qt == 1:
                        pe.wait_ge(s_on, 2 * b.n + 1)
                    elif b.after(1):
                        pe.wait_ge(s_x1, b.n)
                    for g in range(NG):
                        last = nc.tensor.transpose(OC[:, g * P:(g + 1) * P], ot[:, g, qt * P:(qt + 1) * P], ident[:])
                    last.then_inc(s_oc, 1)
                elif u == 7:
                    pe.wait_ge(s_on, 2 * (b.n + 1))
                    for i in range(TT):
                        last = nc.tensor.transpose(OC[:, i * P:(i + 1) * P], on[:, i, :], ident[:])
                    last.then_inc(s_onT_ps, 1)
                elif u == 9:
                    pe.wait_ge(s_onT, b.n + 1)
                    for i in range(TT):
                        nc.tensor.matmul(OC[:, i * P:(i + 1) * P], onT[:, i * P:(i + 1) * P], wproj_sb[:],
                                         start=(i == 0), stop=False, skip_group_check=True)
                        last = add_bias(OC[:, i * P:(i + 1) * P], BP_AT, E)
                    last.then_inc(s_y_ps, 1)

            def logits(b, u):
                if u == 8:
                    pe.wait_ge(s_row0, TT * (b.n + 1))
                    pe.wait_ge(s_vn, min(b.n + 5, NB) if b.known else b.n + 5)
                    for i in range(TT):
                        last = nc.tensor.transpose(X2T_PS[:, i * P:(i + 1) * P], rows[b.par][:, 0, i, 0:E], ident[:])
                    last.then_inc(s_x2T_ps, 1)
                else:
                    pe.wait_ge(s_x2T, b.n + 1)
                    if b.after(1):
                        pe.wait_ge(s_used, 3 * b.n - 2)
                    pe.wait_ge(s_mT, min(2 * b.n + 7, 2 * NB) if b.known else 2 * b.n + 7)
                    for i in range(TT):
                        nc.tensor.matmul(LG_PS[:, i * NE:(i + 1) * NE], xn2T[:, i * P:(i + 1) * P], wr_sb[:],
                                         start=(i == 0), stop=False, skip_group_check=True)
                        last = add_bias(LG_PS[:, i * NE:(i + 1) * NE], BR_AT, NE)
                    last.then_inc(s_lg_ps, 1)

            def ranks(b):
                pe.wait_ge(s_rt, ROUTE * b.n + 12)
                pe.wait_ge(s_mT, min(2 * b.n + 8, 2 * NB) if b.known else 2 * b.n + 8)
                m = both[:].rearrange("p t e -> p (t e)")
                nc.tensor.matmul(RK_PS[:, 0:TT * NE], beforeb[:], m, start=True, stop=False, skip_group_check=True)
                for i in range(TT):
                    last = nc.tensor.matmul(RK_PS[:, (i + 1) * NE:(TT + 1) * NE], onesb[:], m[:, 0:(TT - i) * NE],
                                            start=False, stop=(i == TT - 1), skip_group_check=True)
                last.then_inc(s_rk_ps, 1)

            ROUTE = 13

            def step(t):
                b3, b2, b1 = t.off(3), t.off(2), t.off(1)
                bm1, bm2, bm3 = t.off(-1), t.off(-2), t.off(-3)
                for u in range(UNITS):
                    bm, v = (b1, u + LEAD) if u + LEAD < UNITS else (b2, u + LEAD - UNITS)
                    if bm.real():
                        max_unit(bm, v)
                    if t.real():
                        exp_unit(t, u)
                    if u in (0, 2) and b3.real():
                        project(b3, u)
                    if u == 1 and bm1.real():
                        times_v(bm1, NG - 1)
                    if u in (8, 10) and bm2.real():
                        logits(bm2, u)
                    if u == 6 and b2.real():
                        project_v(b2)
                    if u in (4, 7, 10) and t.real():
                        times_v(t, (u - 4) // 3)
                    if u == 7 and b1.real():
                        turn_max(b1, 0)
                    if u == 1 and t.real():
                        turn_max(t, 1)
                    if u == 4 and bm3.real():
                        ranks(bm3)
                    if bm1.real():
                        finish(bm1, u)
                    tiles = early_tiles_at(t, u)
                    if 0 in tiles:
                        pe.wait_ge(s_mx, UNITS * NB)
                        pe.wait_ge(s_exp, UNITS * NB)
                        pe.wait_ge(s_ot, 2 * NB)
                        start_tiles(0)
                    for j in tiles:
                        tile(j, j % NX, j // NX, EARLY)

            def turn_tile(j, i, g):
                pe.wait_ge(s_xt[i % NX], 16 * (g + 1))
                if j_before(j, 2):
                    pe.wait_ge(s_xtT, j - 1)
                nc.tensor.transpose(XT_PS[i % 2][:, 0:P], xt[i % NX][:, 0:E], ident[:]).then_inc(s_tx, 1)

            def hidden(j, i):
                pe.wait_ge(s_xtT, j + 1)
                pe.wait_ge(s_w1t, j + 1)
                if j_before(j, 2):
                    pe.wait_ge(s_hid, j - 1)
                for k in range(KT):
                    last = nc.tensor.matmul(HIDT_PS[i % 2][:, k * P:(k + 1) * P], w1_t[i % NW][:, k * P:(k + 1) * P],
                                            xtT[i % 2][:], start=True, stop=True)
                last.then_inc(s_hp, 1)

            def second(j, i):
                pe.wait_ge(s_hid, j + 1)
                pe.wait_ge(s_w2t, 2 * (j + 1))
                if isinstance(j, int) and 0 < j < EARLY:
                    pe.wait_ge(s_yt, j)
                elif j_before(j, 2):
                    pe.wait_ge(s_yt, j - 1)
                dst = y_ps(j, i)
                for k in range(KT):
                    nc.tensor.matmul(dst, hidT[i % 2][:, k * P:(k + 1) * P], w2_t[i % NW][:, k, :],
                                     start=(k == 0), stop=False)
                nc.tensor.matmul(dst, onesb[0:PARTS, :], b2_t[i % NW][:], start=False, stop=True).then_inc(s_yp, 1)

            def start_tiles(j):
                g = j // NX
                turn_tile(j, 0, g)
                turn_tile(j + 1, 1, g)
                hidden(j, 0)

            def tile(j, i, g, last):
                if j_in(j, 2, last):
                    turn_tile(j + 2, i + 2, g + (i + 2) // NX)
                if j_in(j, 1, last):
                    hidden(j + 1, i + 1)
                second(j, i)

            run_steps(pe, step)

            pe.wait_ge(s_used, 3 * NB)
            pe.wait_ge(s_x1, NB)
            start_tiles(EARLY)
            with pe.Fori(EARLY // NX, TILES // NX - 1) as g:
                for i in range(NX):
                    tile(NX * g + i, i, g, TILES)
            for j in range(TILES - NX, TILES):
                tile(j, j % NX, j // NX, TILES)


def rope_table():
    pos = np.arange(T, dtype=np.float32)
    inv = (1.0 / np.float32(10000.0) ** (np.arange(0, D, 2, dtype=np.float32) / np.float32(D))).astype(np.float32)
    ang = pos[:, None] * inv[None, :]
    pair = np.arange(P) // H % (D // 2)
    c, s = (f(ang).astype(np.float32)[:, pair].T for f in (np.cos, np.sin))
    return np.stack([c, s, -s, c], axis=1).reshape(P, 2, 2, T)


def kernel(**inputs):
    import numpy as _np
    import concourse.bacc as _bacc
    from concourse import mybir as _mybir
    from concourse.bass_utils import run_bass_kernel_spmd as _run

    a = {k: _np.asarray(v) for k, v in inputs.items()}
    even = _np.arange(2 * P).reshape(2, H, D // 2, 2)[:, :, :, 0].transpose(0, 2, 1).reshape(-1)
    cols = _np.concatenate([even, even + 1, 2 * P + _np.arange(P)])
    bqkv = a["L0_attn_bqkv"]
    bias = _np.concatenate([a["L0_ffn_b2"].reshape(-1), a["L0_attn_bproj"],
                            bqkv[2 * P:], a["L0_ffn_br"]])
    bias = _np.concatenate([bias, _np.zeros(NBIAS - bias.size, bias.dtype)])
    arrays = {
        "x": a["L0_attn_x"].reshape(NTOK, E),
        "wqkv": a["L0_attn_Wqkv"][:, cols],
        "qk_bias": _np.stack([bqkv[even], bqkv[even + 1]], axis=1),
        "wproj": a["L0_attn_Wproj"],
        "w1": a["L0_ffn_W1"],
        "b1_cols": a["L0_ffn_b1"].reshape(NE, KT, P).transpose(2, 0, 1),
        "w2": a["L0_ffn_W2"],
        "wr": a["L0_ffn_Wr"],
        "biases": bias.reshape(P, BIAS_COLS),
        "rope": rope_table(),
    }
    arrays = {k: _np.ascontiguousarray(v) for k, v in arrays.items()}
    nc = _bacc.Bacc("TRN2", target_bir_lowering=False, num_devices=1)
    args = [nc.dram_tensor(k, v.shape, _mybir.dt.from_np(v.dtype), kind="ExternalInput").ap()
            for k, v in arrays.items()]
    y = nc.dram_tensor("y", (NTOK, E), fp32, kind="ExternalOutput").ap()
    layer(nc, *args, y)
    r = _run(nc, [arrays], core_ids=[0])
    return r.results[0]["y"].reshape(NB, T, E)
```
